# Optimizing a Trainium2 kernel written in Bass

```python
import numpy as np
import jax
import jax.numpy as jnp

def _softmax(x, axis=-1):
    return jax.nn.softmax(x, axis=axis)

def _gelu(x):
    return jax.nn.gelu(x, approximate=True)

def _silu(x):
    return jax.nn.silu(x)

def _sigmoid(x):
    return jax.nn.sigmoid(x)

def _layernorm(x, axis=-1, eps=1e-05):
    m = jnp.mean(x, axis=axis, keepdims=True)
    v = jnp.var(x, axis=axis, keepdims=True)
    return (x - m) / jnp.sqrt(v + eps)

def _scatter_add(tgt, idx, src, axis=0):
    return tgt.at[idx].add(src)

def _segment_sum(src, seg, n):
    return jax.ops.segment_sum(src, seg, n)
kernel_name = 'mk_sandwich_d2_jaxref_r8_ff624a'

def setup_inputs(seed: int=0):
    np.random.seed(seed)
    _w = jnp.asarray

    def _L0_attn_setup():
        import jax, jax.numpy as jnp
        import numpy as np
        D_MODEL = 256
        D_INNER = 256
        N_HEADS = 32
        D_STATE = 64
        HEADDIM = D_INNER // N_HEADS
        D_CONV = 4
        CHUNK = 128
        D_FF = 1024
        EPS = 1e-05
        CONV_DIM = D_INNER + 2 * N_HEADS * D_STATE
        D_IN_PROJ = 2 * D_INNER + 2 * N_HEADS * D_STATE + N_HEADS

        def rmsnorm(x, w, eps=EPS):
            x32 = x.astype(jnp.float32)
            x32 = x32 * jax.lax.rsqrt(jnp.mean(x32 * x32, axis=-1, keepdims=True) + eps)
            return (w * x32).astype(x.dtype)

        def causal_conv1d(x, w, b):
            K = w.shape[1]
            y = jax.lax.conv_general_dilated(x, jnp.transpose(w)[:, None, :], window_strides=(1,), padding=[(K - 1, 0)], dimension_numbers=('NWC', 'WIO', 'NWC'), feature_group_count=x.shape[-1])
            return y + b

        def ssd_scan(x, dt, Bm, Cm, chunk=CHUNK):
            b, l, h, p = x.shape
            n = Bm.shape[-1]
            c = l // chunk
            xr = x.reshape(b, c, chunk, h, p)
            a_log = (-jax.nn.softplus(dt)).reshape(b, c, chunk, h)
            Br = Bm.reshape(b, c, chunk, h, n)
            Cr = Cm.reshape(b, c, chunk, h, n)
            cum = jnp.cumsum(a_log, axis=2)
            seg = jnp.exp(cum[:, :, :, None, :] - cum[:, :, None, :, :])
            cb = jnp.einsum('bcihn,bcjhn->bcijh', Cr, Br)
            mask = jnp.tril(jnp.ones((chunk, chunk), bool))
            scores = jnp.where(mask[None, None, :, :, None], seg * cb, 0.0)
            y_intra = jnp.einsum('bcijh,bcjhp->bcihp', scores, xr)
            decay_to_end = jnp.exp(cum[:, :, -1:, :] - cum)
            S = jnp.einsum('bcqh,bcqhn,bcqhp->bchnp', decay_to_end, Br, xr)
            A_chunk = jnp.exp(cum[:, :, -1, :])

            def step(hprev, inp):
                Ac, Sc = inp
                return (Ac[..., None, None] * hprev + Sc, hprev)
            h0 = jnp.zeros((b, h, n, p), x.dtype)
            _, Hprev = jax.lax.scan(step, h0, (jnp.moveaxis(A_chunk, 1, 0), jnp.moveaxis(S, 1, 0)))
            Hprev = jnp.moveaxis(Hprev, 0, 1)
            y_inter = jnp.einsum('bcqh,bcqhn,bchnp->bcqhp', jnp.exp(cum), Cr, Hprev)
            return (y_intra + y_inter).reshape(b, l, h, p)

        def mixer(u, in_proj_w, z_bias, conv_w, conv_b, D, out_proj_w):
            b, l, _ = u.shape
            zxbcdt = u @ in_proj_w.T
            z = zxbcdt[..., :D_INNER]
            xBC = zxbcdt[..., D_INNER:D_INNER + CONV_DIM]
            dt = zxbcdt[..., D_INNER + CONV_DIM:]
            xBC = causal_conv1d(xBC, conv_w, conv_b)
            x = xBC[..., :D_INNER].reshape(b, l, N_HEADS, HEADDIM)
            Bm = xBC[..., D_INNER:D_INNER + N_HEADS * D_STATE].reshape(b, l, N_HEADS, D_STATE)
            Cm = xBC[..., D_INNER + N_HEADS * D_STATE:].reshape(b, l, N_HEADS, D_STATE)
            y = ssd_scan(x, dt, Bm, Cm)
            y = y + D[None, None, :, None] * x
            y = y.reshape(b, l, D_INNER)
            return y * jax.nn.silu(z + z_bias) @ out_proj_w.T
        key = jax.random.key(seed)
        ks = jax.random.split(key, 8)
        s = 0.02
        return {'hidden_states': jax.random.normal(ks[0], (2, 256, D_MODEL), jnp.float32), 'in_proj_w': jax.random.normal(ks[1], (D_IN_PROJ, D_MODEL), jnp.float32) * s, 'z_bias': jnp.zeros((D_INNER,), jnp.float32), 'conv_w': jax.random.normal(ks[2], (CONV_DIM, D_CONV), jnp.float32) * s, 'conv_b': jnp.zeros((CONV_DIM,), jnp.float32), 'D': jnp.ones((N_HEADS,), jnp.float32), 'out_proj_w': jax.random.normal(ks[3], (D_MODEL, D_INNER), jnp.float32) * s, 'norm1_w': jnp.ones((D_MODEL,), jnp.float32), 'norm2_w': jnp.ones((D_MODEL,), jnp.float32), 'gate_w': jax.random.normal(ks[4], (D_FF, D_MODEL), jnp.float32) * s, 'up_w': jax.random.normal(ks[5], (D_FF, D_MODEL), jnp.float32) * s, 'down_w': jax.random.normal(ks[6], (D_MODEL, D_FF), jnp.float32) * s}
    _L0_attn_in = _L0_attn_setup()

    def _L0_ffn_setup():
        import jax, jax.numpy as jnp
        import numpy as np
        B_, S_, H_, O_ = (4, 256, 256, 256)
        E_, R_ = (8, 16)
        LORA_ALPHA = 16.0
        key = jax.random.key(seed)
        ks = jax.random.split(key, 5)
        x = jax.random.normal(ks[0], (B_, S_, H_), dtype=jnp.float32)
        W = jax.random.normal(ks[1], (O_, H_), dtype=jnp.float32) * 0.02
        gate_w = jax.random.normal(ks[2], (E_, H_), dtype=jnp.float32) * 0.02
        A = jax.random.normal(ks[3], (E_, R_, H_), dtype=jnp.float32) * 0.02
        B = jax.random.normal(ks[4], (E_, O_, R_), dtype=jnp.float32) * 0.02
        return {'x': x, 'W': W, 'gate_w': gate_w, 'A': A, 'B': B}
    _L0_ffn_in = _L0_ffn_setup()

    def _L1_attn_setup():
        import jax, jax.numpy as jnp
        import numpy as np
        D_MODEL = 256
        H = 16
        D_K = D_MODEL // H
        key = jax.random.key(seed)
        ks = jax.random.split(key, 9)
        b, n, d = (2, 256, D_MODEL)
        s = 1.0 / np.sqrt(d)
        return {'x': jax.random.normal(ks[0], (b, n, d), jnp.float32), 'Wq': jax.random.normal(ks[1], (d, d), jnp.float32) * s, 'bq': jax.random.normal(ks[2], (d,), jnp.float32) * 0.01, 'Wk': jax.random.normal(ks[3], (d, d), jnp.float32) * s, 'bk': jax.random.normal(ks[4], (d,), jnp.float32) * 0.01, 'Wv': jax.random.normal(ks[5], (d, d), jnp.float32) * s, 'bv': jax.random.normal(ks[6], (d,), jnp.float32) * 0.01, 'Wo': jax.random.normal(ks[7], (d, d), jnp.float32) * s, 'bo': jax.random.normal(ks[8], (d,), jnp.float32) * 0.01}
    _L1_attn_in = _L1_attn_setup()

    def _L1_ffn_setup():
        import jax, jax.numpy as jnp
        import numpy as np
        B, T, D = (1, 256, 256)
        E, K, F = (64, 4, 64)
        S, SF = (2, 64 * 4)
        CAP = 32

        def _moe_forward(x, router_w, router_bias, gate_w, up_w, down_w, sh_gate_w, sh_up_w, sh_down_w):
            b, t, d = x.shape
            flat = x.reshape(b * t, d)
            N = flat.shape[0]
            logits = flat @ router_w.T
            scores = jax.nn.softmax(logits, axis=-1)
            _, topk_idx = jax.lax.top_k(logits + router_bias, K)
            topk_w = jnp.take_along_axis(scores, topk_idx, axis=-1)
            topk_w = topk_w / topk_w.sum(axis=-1, keepdims=True)
            P = N * K
            e_flat = topk_idx.reshape(-1)
            t_flat = jnp.repeat(jnp.arange(N), K)
            w_flat = topk_w.reshape(-1)
            order = jnp.argsort(e_flat)
            e_s, t_s, w_s = (e_flat[order], t_flat[order], w_flat[order])
            counts = jnp.bincount(e_s, length=E)
            starts = jnp.concatenate([jnp.zeros((1,), counts.dtype), jnp.cumsum(counts)[:-1]])
            pos = jnp.arange(P) - starts[e_s]
            slot = jnp.where(pos < CAP, pos, CAP)
            tok_table = jnp.zeros((E, CAP + 1), jnp.int32).at[e_s, slot].set(t_s)[:, :CAP]
            w_table = jnp.zeros((E, CAP + 1), w_s.dtype).at[e_s, slot].set(w_s)[:, :CAP]
            xg = flat[tok_table]
            g = jnp.einsum('ecd,efd->ecf', xg, gate_w)
            u = jnp.einsum('ecd,efd->ecf', xg, up_w)
            y = jnp.einsum('ecf,edf->ecd', jax.nn.silu(g) * u, down_w)
            out = jnp.zeros_like(flat).at[tok_table.reshape(-1)].add((y * w_table[..., None]).reshape(-1, d))
            sg = jnp.einsum('nd,sfd->nsf', flat, sh_gate_w)
            su = jnp.einsum('nd,sfd->nsf', flat, sh_up_w)
            out = out + jnp.einsum('nsf,sdf->nd', jax.nn.silu(sg) * su, sh_down_w)
            return out.reshape(b, t, d)
        key = jax.random.key(seed)
        ks = jax.random.split(key, 9)
        s = 0.02
        return {'x': jax.random.normal(ks[0], (B, T, D), jnp.float32), 'router_w': jax.random.normal(ks[1], (E, D), jnp.float32) * s, 'router_bias': jnp.zeros((E,), jnp.float32), 'gate_w': jax.random.normal(ks[2], (E, F, D), jnp.float32) * s, 'up_w': jax.random.normal(ks[3], (E, F, D), jnp.float32) * s, 'down_w': jax.random.normal(ks[4], (E, D, F), jnp.float32) * s, 'sh_gate_w': jax.random.normal(ks[5], (S, SF, D), jnp.float32) * s, 'sh_up_w': jax.random.normal(ks[6], (S, SF, D), jnp.float32) * s, 'sh_down_w': jax.random.normal(ks[7], (S, D, SF), jnp.float32) * s}
    _L1_ffn_in = _L1_ffn_setup()
    _d = {'L0_attn_hidden_states': _L0_attn_in['hidden_states'], 'L0_attn_in_proj_w': _L0_attn_in['in_proj_w'], 'L0_attn_z_bias': _L0_attn_in['z_bias'], 'L0_attn_conv_w': _L0_attn_in['conv_w'], 'L0_attn_conv_b': _L0_attn_in['conv_b'], 'L0_attn_D': _L0_attn_in['D'], 'L0_attn_out_proj_w': _L0_attn_in['out_proj_w'], 'L0_attn_norm1_w': _L0_attn_in['norm1_w'], 'L0_attn_norm2_w': _L0_attn_in['norm2_w'], 'L0_attn_gate_w': _L0_attn_in['gate_w'], 'L0_attn_up_w': _L0_attn_in['up_w'], 'L0_attn_down_w': _L0_attn_in['down_w'], 'L0_ffn_W': _L0_ffn_in['W'], 'L0_ffn_gate_w': _L0_ffn_in['gate_w'], 'L0_ffn_A': _L0_ffn_in['A'], 'L0_ffn_B': _L0_ffn_in['B'], 'L1_attn_Wq': _L1_attn_in['Wq'], 'L1_attn_bq': _L1_attn_in['bq'], 'L1_attn_Wk': _L1_attn_in['Wk'], 'L1_attn_bk': _L1_attn_in['bk'], 'L1_attn_Wv': _L1_attn_in['Wv'], 'L1_attn_bv': _L1_attn_in['bv'], 'L1_attn_Wo': _L1_attn_in['Wo'], 'L1_attn_bo': _L1_attn_in['bo'], 'L1_ffn_router_w': _L1_ffn_in['router_w'], 'L1_ffn_router_bias': _L1_ffn_in['router_bias'], 'L1_ffn_gate_w': _L1_ffn_in['gate_w'], 'L1_ffn_up_w': _L1_ffn_in['up_w'], 'L1_ffn_down_w': _L1_ffn_in['down_w'], 'L1_ffn_sh_gate_w': _L1_ffn_in['sh_gate_w'], 'L1_ffn_sh_up_w': _L1_ffn_in['sh_up_w'], 'L1_ffn_sh_down_w': _L1_ffn_in['sh_down_w']}
    _x0 = _d['L0_attn_hidden_states']
    _d['L0_attn_hidden_states'] = jax.random.normal(jax.random.fold_in(jax.random.key(seed), 1), (8, 256, 256), dtype=_x0.dtype)
    del _x0
    return _d

def reference(L0_attn_hidden_states, L0_attn_in_proj_w, L0_attn_z_bias, L0_attn_conv_w, L0_attn_conv_b, L0_attn_D, L0_attn_out_proj_w, L0_attn_norm1_w, L0_attn_norm2_w, L0_attn_gate_w, L0_attn_up_w, L0_attn_down_w, L0_ffn_W, L0_ffn_gate_w, L0_ffn_A, L0_ffn_B, L1_attn_Wq, L1_attn_bq, L1_attn_Wk, L1_attn_bk, L1_attn_Wv, L1_attn_bv, L1_attn_Wo, L1_attn_bo, L1_ffn_router_w, L1_ffn_router_bias, L1_ffn_gate_w, L1_ffn_up_w, L1_ffn_down_w, L1_ffn_sh_gate_w, L1_ffn_sh_up_w, L1_ffn_sh_down_w):

    def _L0_attn_ref(hidden_states, in_proj_w, z_bias, conv_w, conv_b, D, out_proj_w, norm1_w, norm2_w, gate_w, up_w, down_w):
        import jax, jax.numpy as jnp
        import numpy as np
        D_MODEL = 256
        D_INNER = 256
        N_HEADS = 32
        D_STATE = 64
        HEADDIM = D_INNER // N_HEADS
        D_CONV = 4
        CHUNK = 128
        D_FF = 1024
        EPS = 1e-05
        CONV_DIM = D_INNER + 2 * N_HEADS * D_STATE
        D_IN_PROJ = 2 * D_INNER + 2 * N_HEADS * D_STATE + N_HEADS

        def rmsnorm(x, w, eps=EPS):
            x32 = x.astype(jnp.float32)
            x32 = x32 * jax.lax.rsqrt(jnp.mean(x32 * x32, axis=-1, keepdims=True) + eps)
            return (w * x32).astype(x.dtype)

        def causal_conv1d(x, w, b):
            K = w.shape[1]
            y = jax.lax.conv_general_dilated(x, jnp.transpose(w)[:, None, :], window_strides=(1,), padding=[(K - 1, 0)], dimension_numbers=('NWC', 'WIO', 'NWC'), feature_group_count=x.shape[-1])
            return y + b

        def ssd_scan(x, dt, Bm, Cm, chunk=CHUNK):
            b, l, h, p = x.shape
            n = Bm.shape[-1]
            c = l // chunk
            xr = x.reshape(b, c, chunk, h, p)
            a_log = (-jax.nn.softplus(dt)).reshape(b, c, chunk, h)
            Br = Bm.reshape(b, c, chunk, h, n)
            Cr = Cm.reshape(b, c, chunk, h, n)
            cum = jnp.cumsum(a_log, axis=2)
            seg = jnp.exp(cum[:, :, :, None, :] - cum[:, :, None, :, :])
            cb = jnp.einsum('bcihn,bcjhn->bcijh', Cr, Br)
            mask = jnp.tril(jnp.ones((chunk, chunk), bool))
            scores = jnp.where(mask[None, None, :, :, None], seg * cb, 0.0)
            y_intra = jnp.einsum('bcijh,bcjhp->bcihp', scores, xr)
            decay_to_end = jnp.exp(cum[:, :, -1:, :] - cum)
            S = jnp.einsum('bcqh,bcqhn,bcqhp->bchnp', decay_to_end, Br, xr)
            A_chunk = jnp.exp(cum[:, :, -1, :])

            def step(hprev, inp):
                Ac, Sc = inp
                return (Ac[..., None, None] * hprev + Sc, hprev)
            h0 = jnp.zeros((b, h, n, p), x.dtype)
            _, Hprev = jax.lax.scan(step, h0, (jnp.moveaxis(A_chunk, 1, 0), jnp.moveaxis(S, 1, 0)))
            Hprev = jnp.moveaxis(Hprev, 0, 1)
            y_inter = jnp.einsum('bcqh,bcqhn,bchnp->bcqhp', jnp.exp(cum), Cr, Hprev)
            return (y_intra + y_inter).reshape(b, l, h, p)

        def mixer(u, in_proj_w, z_bias, conv_w, conv_b, D, out_proj_w):
            b, l, _ = u.shape
            zxbcdt = u @ in_proj_w.T
            z = zxbcdt[..., :D_INNER]
            xBC = zxbcdt[..., D_INNER:D_INNER + CONV_DIM]
            dt = zxbcdt[..., D_INNER + CONV_DIM:]
            xBC = causal_conv1d(xBC, conv_w, conv_b)
            x = xBC[..., :D_INNER].reshape(b, l, N_HEADS, HEADDIM)
            Bm = xBC[..., D_INNER:D_INNER + N_HEADS * D_STATE].reshape(b, l, N_HEADS, D_STATE)
            Cm = xBC[..., D_INNER + N_HEADS * D_STATE:].reshape(b, l, N_HEADS, D_STATE)
            y = ssd_scan(x, dt, Bm, Cm)
            y = y + D[None, None, :, None] * x
            y = y.reshape(b, l, D_INNER)
            return y * jax.nn.silu(z + z_bias) @ out_proj_w.T
        residual = hidden_states
        h = rmsnorm(hidden_states, norm1_w)
        h = mixer(h, in_proj_w, z_bias, conv_w, conv_b, D, out_proj_w) + residual
        residual = h
        h = rmsnorm(h, norm2_w)
        h = jax.nn.silu(h @ gate_w.T) * (h @ up_w.T) @ down_w.T
        return residual + h

    def _L0_ffn_ref(x, W, gate_w, A, B):
        import jax, jax.numpy as jnp
        import numpy as np
        B_, S_, H_, O_ = (4, 256, 256, 256)
        E_, R_ = (8, 16)
        LORA_ALPHA = 16.0
        bsz, seq, hid = x.shape
        E = gate_w.shape[0]
        x_flat = x.reshape(-1, hid)
        out = x_flat @ W.T
        logits = x_flat @ gate_w.T
        probs = jax.nn.softmax(logits, axis=-1)
        topk_w, topk_idx = jax.lax.top_k(probs, 2)
        topk_w = topk_w / jnp.sum(topk_w, axis=-1, keepdims=True)
        onehot = jax.nn.one_hot(topk_idx, E, dtype=x.dtype)
        wmat = jnp.einsum('tk,tke->te', topk_w, onehot) * LORA_ALPHA
        h = jnp.einsum('th,erh->etr', x_flat, A)
        hw = h * wmat.T[:, :, None]
        lora = jnp.einsum('etr,eor->to', hw, B)
        return (out + lora).reshape(bsz, seq, -1)

    def _L1_attn_ref(x, Wq, bq, Wk, bk, Wv, bv, Wo, bo):
        import jax, jax.numpy as jnp
        import numpy as np
        D_MODEL = 256
        H = 16
        D_K = D_MODEL // H
        b, n, d = x.shape
        h, dk = (H, D_K)

        def split_heads(t):
            return t.reshape(b, n, h, dk).transpose(0, 2, 1, 3)
        q = split_heads(x @ Wq + bq)
        k = split_heads(x @ Wk + bk)
        v = split_heads(x @ Wv + bv)
        scores = jnp.einsum('bhqd,bhkd->bhqk', q, k) / jnp.sqrt(jnp.float32(dk))
        causal = jnp.tril(jnp.ones((n, n), dtype=bool))
        scores = jnp.where(causal[None, None], scores, -jnp.inf)
        attn = jax.nn.softmax(scores, axis=-1)
        out = jnp.einsum('bhqk,bhkd->bhqd', attn, v)
        out = out.transpose(0, 2, 1, 3).reshape(b, n, d)
        return out @ Wo + bo

    def _L1_ffn_ref(x, router_w, router_bias, gate_w, up_w, down_w, sh_gate_w, sh_up_w, sh_down_w):
        import jax, jax.numpy as jnp
        import numpy as np
        B, T, D = (1, 256, 256)
        E, K, F = (64, 4, 64)
        S, SF = (2, 64 * 4)
        CAP = 32

        def _moe_forward(x, router_w, router_bias, gate_w, up_w, down_w, sh_gate_w, sh_up_w, sh_down_w):
            b, t, d = x.shape
            flat = x.reshape(b * t, d)
            N = flat.shape[0]
            logits = flat @ router_w.T
            scores = jax.nn.softmax(logits, axis=-1)
            _, topk_idx = jax.lax.top_k(logits + router_bias, K)
            topk_w = jnp.take_along_axis(scores, topk_idx, axis=-1)
            topk_w = topk_w / topk_w.sum(axis=-1, keepdims=True)
            P = N * K
            e_flat = topk_idx.reshape(-1)
            t_flat = jnp.repeat(jnp.arange(N), K)
            w_flat = topk_w.reshape(-1)
            order = jnp.argsort(e_flat)
            e_s, t_s, w_s = (e_flat[order], t_flat[order], w_flat[order])
            counts = jnp.bincount(e_s, length=E)
            starts = jnp.concatenate([jnp.zeros((1,), counts.dtype), jnp.cumsum(counts)[:-1]])
            pos = jnp.arange(P) - starts[e_s]
            slot = jnp.where(pos < CAP, pos, CAP)
            tok_table = jnp.zeros((E, CAP + 1), jnp.int32).at[e_s, slot].set(t_s)[:, :CAP]
            w_table = jnp.zeros((E, CAP + 1), w_s.dtype).at[e_s, slot].set(w_s)[:, :CAP]
            xg = flat[tok_table]
            g = jnp.einsum('ecd,efd->ecf', xg, gate_w)
            u = jnp.einsum('ecd,efd->ecf', xg, up_w)
            y = jnp.einsum('ecf,edf->ecd', jax.nn.silu(g) * u, down_w)
            out = jnp.zeros_like(flat).at[tok_table.reshape(-1)].add((y * w_table[..., None]).reshape(-1, d))
            sg = jnp.einsum('nd,sfd->nsf', flat, sh_gate_w)
            su = jnp.einsum('nd,sfd->nsf', flat, sh_up_w)
            out = out + jnp.einsum('nsf,sdf->nd', jax.nn.silu(sg) * su, sh_down_w)
            return out.reshape(b, t, d)
        return _moe_forward(x, router_w, router_bias, gate_w, up_w, down_w, sh_gate_w, sh_up_w, sh_down_w)
    x = L0_attn_hidden_states
    x = x + _layernorm(_L0_attn_ref(_layernorm(x, axis=-1), L0_attn_in_proj_w, L0_attn_z_bias, L0_attn_conv_w, L0_attn_conv_b, L0_attn_D, L0_attn_out_proj_w, L0_attn_norm1_w, L0_attn_norm2_w, L0_attn_gate_w, L0_attn_up_w, L0_attn_down_w), axis=-1)
    x = x + _layernorm(_L0_ffn_ref(_layernorm(x, axis=-1), L0_ffn_W, L0_ffn_gate_w, L0_ffn_A, L0_ffn_B), axis=-1)
    x = x + _layernorm(_L1_attn_ref(_layernorm(x, axis=-1), L1_attn_Wq, L1_attn_bq, L1_attn_Wk, L1_attn_bk, L1_attn_Wv, L1_attn_bv, L1_attn_Wo, L1_attn_bo), axis=-1)
    x = x + _layernorm(_L1_ffn_ref(_layernorm(x, axis=-1), L1_ffn_router_w, L1_ffn_router_bias, L1_ffn_gate_w, L1_ffn_up_w, L1_ffn_down_w, L1_ffn_sh_gate_w, L1_ffn_sh_up_w, L1_ffn_sh_down_w), axis=-1)
    return x

_drawn_inputs = setup_inputs


def setup_inputs(seed=0):
    import zlib

    import numpy as np

    out = dict(_drawn_inputs(seed))
    spreads = {'L0_attn_z_bias': (0.0, 0.8),
     'L0_attn_conv_b': (0.0, 0.345),
     'L0_attn_D': (1.0, 0.6),
     'L0_attn_norm1_w': (1.0, 0.6),
     'L0_attn_norm2_w': (1.0, 0.573),
     'L1_ffn_router_bias': (0.0, 0.312)}
    factors = {'L0_attn_in_proj_w': 3.326,
     'L0_attn_conv_w': 7.759,
     'L0_attn_out_proj_w': 3.187,
     'L1_attn_bq': 8.0,
     'L1_attn_bk': 8.0}
    for name, (base, spread) in spreads.items():
        noise = np.random.default_rng([zlib.crc32(name.encode()), seed]).standard_normal(out[name].shape)
        drawn = base * np.exp(spread * noise) if base else spread * noise
        out[name] = jnp.asarray(drawn.astype(out[name].dtype))
    for name, factor in factors.items():
        out[name] = (out[name] * factor).astype(out[name].dtype)
    return out
```

```python
from contextlib import ExitStack

import concourse.bass as bass
from concourse import mybir

ALU = mybir.AluOpType
ACT = mybir.ActivationFunctionType
AX = mybir.AxisListType
F32 = mybir.dt.float32
BF16 = mybir.dt.bfloat16
U32 = mybir.dt.uint32

P = 128
D = 256
DC = D // P
SEQ = 256
TOKENS = 8 * SEQ
GROUP = 512
ROUNDS = TOKENS // GROUP
TILES = GROUP // P
SEQS = GROUP // SEQ
EPS = 1e-5
MASKED = -1e30

HEADS = 32
STATE = 64
HEADDIM = D // HEADS
TAPS = 4
PAIRS = HEADS // 2
PROJ = 2 * D + 2 * HEADS * STATE + HEADS
QUADS = HEADS // 4
TRI = 3 * P
FF = 1024
EXPERTS0, RANK, LORA_ALPHA = 8, 16, 16.0
LW = D + EXPERTS0 + EXPERTS0 * RANK
AHEADS = 16
DK = D // AHEADS
E1, TOPK, F1, CAP = 64, 4, 64, 32
SHF = 512
SLOTS = E1 * CAP
EG = P // CAP
EGROUPS = E1 // EG


class BankPlan:

    def __init__(self, banks, full, drained):
        self.banks, self.full, self.drained = banks, full, drained
        self.place, self.count = {}, [0] * len(banks)
        self.base = [0] * len(banks)

    def use(self, key, bank):
        self.place[key] = (bank, self.count[bank])
        self.count[bank] += 1

    def __getitem__(self, key):
        return self.banks[self.place[key][0]]

    def wait_empty(self, eng, key, r):
        b, n = self.place[key]
        eng.wait_ge(self.drained[b], self.value(b, n, r) + 1)

    def wait_full(self, eng, key, r):
        b, n = self.place[key]
        eng.wait_ge(self.full[b], self.value(b, n + 1, r))

    def wait_drained(self, eng, key, r):
        b, n = self.place[key]
        eng.wait_ge(self.drained[b], self.value(b, n + 1, r) + 1)

    def value(self, b, n, r):
        return r * self.count[b] + self.base[b] + n

    def filled(self, ins, key):
        ins.then_inc(self.full[self.place[key][0]], 1)

    def read(self, ins, key):
        ins.then_inc(self.drained[self.place[key][0]], 1)


class Signal:

    def __init__(self, sem, per):
        self.sem, self.per = sem, per

    def wait(self, eng, r, n):
        eng.wait_ge(self.sem, r * self.per + n)

    def after(self, ins):
        ins.then_inc(self.sem, 1)


def sandwich(nc, A, out):
    with ExitStack() as ctx:
        def sb(name, shape, dt=F32):
            return ctx.enter_context(nc.sbuf_tensor(name, shape, dt))

        def sem(name):
            return ctx.enter_context(nc.semaphore(name))

        consts_cast = sem("consts_cast")
        settled = sem("settled")

        def settle(eng):
            eng.sem_inc(settled, 1)

        def signal(name, per):
            return Signal(sem(name), per)

        banks = [ctx.enter_context(nc.psum_tensor(f"bank{i}", [P, 512], F32)) for i in range(8)]
        full = [sem(f"bank_full{i}") for i in range(8)]
        drained = [sem(f"bank_drained{i}") for i in range(8)]

        xg_dram = nc.dram_tensor("xg_dram", (SLOTS, D), F32, kind="Internal").ap()
        y_dram = nc.dram_tensor("y_dram", (SLOTS + P, D), F32, kind="Internal").ap()
        x3_dram = nc.dram_tensor("x3_dram", (TOKENS, D), F32, kind="Internal").ap()
        sh_dram = nc.dram_tensor("sh_dram", (TOKENS, D), F32, kind="Internal").ap()

        ident = sb("ident", [P, P])
        ident_bf = sb("ident_bf", [P, P], BF16)
        keyq_mask = sb("keyq_mask", [P, TRI], BF16)
        qkey_mask = sb("qkey_mask", [P, TRI], BF16)
        earlier = sb("earlier", [P, P], BF16)
        ones_bf = sb("ones_bf", [P, P], BF16)
        zeros_bf = sb("zeros_bf", [P, 512], BF16)
        neg_sel = sb("neg_sel", [96, HEADS], BF16)
        ones = sb("ones", [P, SEQ])
        iota = sb("iota", [P, E1])
        half = sb("half", [P, TILES])
        parity = sb("parity", [P, 2])
        neg_in = sb("neg_in", [96, HEADS])
        w_in = sb("w_in", [P, DC, PROJ])
        conv_w = sb("conv_w", [P, 34, TAPS])
        conv_b = sb("conv_b", [P, 34])
        chan = sb("chan", [P, DC, 8])
        kbias = sb("kbias", [P, DC, 2])
        qbias = sb("qbias", [P, DC])
        w_out = sb("w_out", [P, DC, D])
        w_gu = sb("w_gu", [P, DC, 2 * FF])
        w_dn = sb("w_dn", [P, FF // P, D])
        w_lora = sb("w_lora", [P, DC, LW])
        w_lb = sb("w_lb", [P, D])
        w_att = sb("w_att", [P, DC, 4, D])
        att_rows = sb("att_rows", [1, 2, D])
        w_rt = sb("w_rt", [P, DC, E1])
        rt_bias = sb("rt_bias", [P, E1])
        w_sgu = sb("w_sgu", [P, DC, 2 * SHF])
        w_sdn = sb("w_sdn", [P, SHF // P, D])

        xin = sb("xin", [P, TILES, D])
        hn = sb("hn", [P, TILES, D])
        u = sb("u", [P, TILES, D])
        uT = sb("uT", [P, DC, GROUP])
        h1 = sb("h1", [P, TILES, D])
        cstage = h1[:, :, :].rearrange("p (a t) d -> p a (t d)", a=2)
        x1 = sb("x1", [P, TILES, D])
        tmp = sb("tmp", [P, TILES, D])
        xf = sb("xf", [P, TILES, D])
        stats = sb("stats", [P, TILES, 6])
        mv = sb("mv", [P, TILES, 2])
        ve = sb("ve", [P, TILES])
        rs = sb("rs", [P, TILES])
        r1 = sb("r1", [P, TILES])
        sm = sb("sm", [P, TILES])
        hf = sb("hf", [P, FF // P, GROUP])
        xc = sb("xc", [P, DC, GROUP])
        sz = sb("sz", [P, DC, GROUP])
        yg = sb("yg", [P, DC, GROUP])
        x_pad = sb("x_pad", [P, TILES, QUADS, 4, 32])
        bc = hf[:, 0:4, :].rearrange("p (s w) l -> p s w l", s=2)
        dec = sb("dec", [P, 3, TRI])
        sc = sb("sc", [P, 3, TRI])
        sp_a = hf[0:HEADS, 6, :]
        sp_b = hf[0:HEADS, 7, :]
        cumP = hf[0:HEADS, 5, :]
        mid0 = sb("mid0", [HEADS, GROUP], BF16)
        cum3 = sb("cum3", [96, SEQS, TRI], BF16)
        cum_tok = sb("cum_tok", [P, TILES, HEADS])
        sg = u[:, :, :].rearrange("p (a t) d -> p a (t d)", a=2)
        lg0 = sb("lg0", [P, TILES, EXPERTS0])
        mx = sb("mx", [P, TILES, 8])
        ix = sb("ix", [P, TILES, 8], U32)
        ixf = sb("ixf", [P, TILES, TOPK])
        oh0 = sb("oh0", [P, TILES, 2, EXPERTS0])
        wk = sb("wk", [P, TILES, TOPK])
        wsum = sb("wsum", [P, TILES])
        wm = sb("wm", [P, TILES, EXPERTS0])
        hw = yg[:, 0, :].rearrange("p (t j) -> p t j", t=TILES)
        hwT = yg[:, 1, :]
        qT = xc
        kT = [sz, yg]
        v_pad = sb("v_pad", [P, TILES, AHEADS // 2, 2, 32])
        nmax = sb("nmax", [P, 4, 2])
        esum = sb("esum", [P, 4, 2])
        pr = dec
        prT = sc
        oT = hf[:, 0:2, :]
        lgt = sb("lgt", [P, TILES, E1])
        biased = sb("biased", [P, TILES, E1])
        oh = hf[:, 4:6, :].rearrange("p a (b e) -> p (a b) e", e=E1).rearrange("p (t k) e -> p t k e", t=TILES)
        prod = hf[:, 6:8, :].rearrange("p a (b e) -> p (a b) e", e=E1).rearrange("p (t k) e -> p t k e", t=TILES)
        chosen = sb("chosen", [P, TILES, E1], BF16)
        before = sb("before", [P, TILES + 1, E1], BF16)
        lk = sb("lk", [P, TILES, TOPK])
        slot = sb("slot", [P, TILES, TOPK])
        over = sb("over", [P, TILES, TOPK])
        sidx = sb("sidx", [P, TILES * TOPK], U32)
        gidx = sb("gidx", [P, ROUNDS, TILES * TOPK], U32)
        wts = sb("wts", [P, ROUNDS, TILES * TOPK])

        plan = BankPlan(banks, full, drained)
        for c in range(DC):
            plan.use(("T", "mix", c), c)
        for c in range(DC):
            plan.use(("Z", c), 2 + c)
        for c in range(DC):
            plan.use(("X", c), 4 + c)
        plan.use("dt", 0)
        for c in range(DC):
            plan.use(("Y", c), 6 + c)
        plan.use("cumT", 1)
        for c in range(DC):
            plan.use(("XT", c), 2 + c)
        uses = [(p, b, e) for p in range(PAIRS) for b in range(SEQS) for e in range(2)]
        for p in range(PAIRS):
            for w in range(2):
                plan.use(("BC", p, w), w)
            for b in range(SEQS):
                for e in range(2):
                    plan.use(("A", p, b, e), 2 + e)
                    plan.use(("CB", p, b, e), 4 + e)
        for j in range(2):
            plan.use(("O", j), j)
        for c in range(DC):
            plan.use(("T", "ffn", c), 2 + c)
        for f in range(FF // P):
            plan.use(("G", f), 4 + f % 2)
            plan.use(("U", f), f % 2)
        for j in range(2):
            plan.use(("F", j), 2 + j)
        for c in range(DC):
            plan.use(("T", "lora", c), 4 + c)
        for t in range(TILES):
            plan.use(("L", t), t)
        plan.use("LT", 4)
        for c in range(DC):
            plan.use(("T", "att", c), 6 + c)
        for c in range(DC):
            plan.use(("Q", c), c)
            plan.use(("K", c), 2 + c)
            plan.use(("V", c), 4 + c)
        for c in range(DC):
            plan.use(("OT", c), 6 + c)
        auses = [(h, b) for h in range(AHEADS) for b in range(SEQS)]
        for n, (h, b) in enumerate(auses):
            plan.use(("S", n), n % 3)
            plan.use(("PT", n), 3 + n % 3)
        for j in range(2):
            plan.use(("W", j), j)
        for c in range(DC):
            plan.use(("T", "moe", c), 2 + c)
        plan.use("R", 4)
        for f in range(SHF // P):
            plan.use(("SG", f), f % 2)
            plan.use(("SU", f), 6 + f % 2)
        for j in range(2):
            plan.use(("SD", j), 2 + j)
        plan.use("pos", 5)

        CREDIT = 16
        consts_in = sem("consts_in")
        w_sem = {k: sem("in_" + k) for k in ("proj", "out", "ffn", "lora", "att", "moe")}
        pads_zero = sem("pads_zero")
        x_in = sem("x_in")
        x_free = signal("x_free", 1)
        var_ready = signal("var_ready", 9)
        rstd_ready = signal("rstd_ready", 9)
        u_ready = signal("u_ready", 5)
        tap0 = signal("tap0", 34)
        dt_abs = signal("dt_abs", 1)
        dt_log = signal("dt_log", 1)
        exp_dt = signal("exp_dt", 1)
        cum_ready = signal("cum_ready", 1)
        cum3_ready = signal("cum3_ready", 1)
        y_added = signal("y_added", 64)
        yg_ready = signal("yg_ready", DC)
        sumsq = signal("sumsq", TILES)
        gated = signal("gated", FF // P)
        hw_ready = signal("hw_ready", 1)
        lora_top = signal("lora_top", 1)
        lora_exp = signal("lora_exp", 1)
        lora_added = signal("lora_added", TILES)
        lora_lg = signal("lora_lg", TILES)
        k_even = signal("k_even", DC)
        nmax_ready = signal("nmax_ready", 32)
        exps = signal("exps", 32)
        probs = signal("probs", 32)
        o_added = signal("o_added", 32)
        sgated = signal("sgated", SHF // P)
        top_ready = signal("top_ready", 1)
        top_exp = signal("top_exp", 1)
        chosen_ready = signal("chosen_ready", 1)
        sidx_ready = signal("sidx_ready", 1)
        scattered = sem("scattered")
        xf_stored = sem("xf_stored")
        zero_filled = sem("zero_filled")
        chain = signal("dve_chain", 152)
        x3_ready = signal("x3_ready", 1)

        area = w_in[:, :, :].rearrange("p k n -> p (k n)")
        marks = [0]

        def carve(n):
            marks[0] += n
            return area[:, marks[0] - n:marks[0]]

        xg = [carve(D) for _ in range(2)]
        xgT = [carve(DC * P).rearrange("p (k s) -> p k s", k=DC) for _ in range(2)]
        egu = [carve(DC * EG * P).rearrange("p (k e j) -> p k e j", k=DC, e=EG) for _ in range(2)]
        edn = [carve(EG * D)[0:F1, :].rearrange("p (e d) -> p e d", e=EG) for _ in range(2)]
        esg = [carve(F1) for _ in range(2)]
        eh = [carve(F1) for _ in range(2)]
        ehT = [carve(P)[0:F1, :] for _ in range(2)]
        yt = [carve(D) for _ in range(2)]
        yk = [hf[:, 2 * s:2 * s + 2, :].rearrange("p a b -> p (a b)").rearrange("p (k d) -> p k d", k=TOPK)
              for s in range(2)]
        shx = [h1[:, 2 * s:2 * s + 2, :] for s in range(2)]
        acc = [tmp[:, s, :] for s in range(2)]
        ot = [tmp[:, 2 + s, :] for s in range(2)]
        gi = sb("gi", [P, 2, TOPK], U32)
        wt = sb("wt", [P, 2, TOPK])
        HALF = EGROUPS // 2
        TWO = TOKENS // P // 2

        tail = BankPlan(banks, full, drained)
        tail.base = [ROUNDS * n for n in plan.count]
        for s in range(2):
            tail.use(("XG", s), s)
            tail.use(("GU", s), 2 + s)
            tail.use(("HT", s), 4 + s)
            tail.use(("YO", s), 6 + s)
        e_in = [sem(f"e_in{s}") for s in range(2)]
        e_silu = signal("e_silu", 2)
        y_out = [sem(f"y_out{s}") for s in range(2)]
        gi_ready = signal("gi_ready", 2)
        gathered = [sem(f"gathered{s}") for s in range(2)]
        shx_in = [sem(f"shx_in{s}") for s in range(2)]
        var2 = signal("var2", 2)
        rstd2 = signal("rstd2", 2)
        out_ready = signal("out_ready", 2)
        stored = [sem(f"stored{s}") for s in range(2)]
        chain2 = signal("dve_chain2", 14)

        def tail_sync(sp):
            sp.wait_ge(scattered, 16 * TILES * TOPK * ROUNDS + CREDIT)
            with sp.Fori(0, HALF) as r:
                for s in range(2):
                    tail.wait_empty(sp, ("YO", s), r)
                    settle(sp)
                    g = 2 * r + s
                    sp.dma_start(xg[s], xg_dram[bass.ds(g * P, P), :]).then_inc(e_in[s], 16)
                    sp.dma_start(egu[s], A["w_egu"][:, :, bass.ds(g * EG, EG), :]).then_inc(e_in[s], 16)
                    sp.dma_start(edn[s], A["w_edn"][:, bass.ds(g * EG, EG), :]).then_inc(e_in[s], 16)
            sp.wait_ge(xf_stored, 32 * ROUNDS)
            with sp.Fori(0, TWO) as r:
                for s in range(2):
                    i = 2 * r + s
                    out_ready.wait(sp, r, 1)
                    settle(sp)
                    sp.wait_ge(stored[s], r * 16 + CREDIT)
                    settle(sp)
                    sp.dma_start(shx[s][:, 0, :], sh_dram[bass.ds(i * P, P), :]).then_inc(shx_in[s], 16)
                    sp.dma_start(shx[s][:, 1, :], x3_dram[bass.ds(i * P, P), :]).then_inc(shx_in[s], 16)
                for s in range(2):
                    i = 2 * r + s
                    out_ready.wait(sp, r, s + 2)
                    settle(sp)
                    sp.dma_start(out[bass.ds(i * P, P), :], ot[s]).then_inc(stored[s], 16)
            for s in range(2):
                sp.wait_ge(stored[s], 16 * TWO + CREDIT)

        def tail_tensor(pe):
            with pe.Fori(0, HALF) as r:
                for s in range(2):
                    pe.wait_ge(e_in[s], r * 48 + 48)
                    tail.wait_empty(pe, ("XG", s), r)
                    for k in range(DC):
                        mm = pe.transpose(tail[("XG", s)][:, k * P:(k + 1) * P], xg[s][:, k * P:(k + 1) * P],
                                          ident[:, :])
                    tail.filled(mm, ("XG", s))
                for s in range(2):
                    tail.wait_drained(pe, ("XG", s), r)
                    tail.wait_empty(pe, ("GU", s), r)
                    for e in range(EG):
                        rows = slice(CAP * e, CAP * (e + 1))
                        for k in range(DC):
                            mm = pe.matmul(tail[("GU", s)][rows, 0:P], xgT[s][:, k, rows], egu[s][:, k, e, :],
                                           start=k == 0, stop=k == DC - 1)
                    tail.filled(mm, ("GU", s))
                for s in range(2):
                    tail.wait_drained(pe, ("GU", s), r)
                    tail.wait_empty(pe, ("HT", s), r)
                    settle(pe)
                    tail.filled(pe.transpose(tail[("HT", s)][0:F1, 0:P], eh[s], ident[:, :]), ("HT", s))
                for s in range(2):
                    tail.wait_drained(pe, ("HT", s), r)
                    tail.wait_empty(pe, ("YO", s), r)
                    settle(pe)
                    for e in range(EG):
                        rows = slice(CAP * e, CAP * (e + 1))
                        mm = pe.matmul(tail[("YO", s)][rows, 0:D], ehT[s][:, rows], edn[s][:, e, :],
                                       start=True, stop=True)
                    tail.filled(mm, ("YO", s))

        def tail_scalar(act):
            with act.Fori(0, HALF) as r:
                for s in range(2):
                    tail.wait_full(act, ("XG", s), r)
                    tail.read(act.activation(xgT[s], tail[("XG", s)][:, 0:DC * P]
                                             .rearrange("p (k s) -> p k s", k=DC), ACT.Copy), ("XG", s))
                for s in range(2):
                    tail.wait_full(act, ("GU", s), r)
                    e_silu.after(act.activation(esg[s], tail[("GU", s)][:, 0:F1], ACT.Silu))
                for s in range(2):
                    tail.wait_full(act, ("HT", s), r)
                    tail.read(act.activation(ehT[s], tail[("HT", s)][0:F1, 0:P], ACT.Copy), ("HT", s))

        def tail_pool(pool):
            with pool.Fori(0, HALF) as r:
                for s in range(2):
                    tail.wait_drained(pool, ("YO", s), r)
                    settle(pool)
                    pool.dma_start(y_dram[bass.ds((2 * r + s) * P, P), :], yt[s]).then_inc(y_out[s], 16)
            for s in range(2):
                pool.wait_ge(y_out[s], 16 * HALF + CREDIT)
            with pool.Fori(0, TWO) as r:
                for s in range(2):
                    gi_ready.wait(pool, r, s + 1)
                    settle(pool)
                    for k in range(TOPK):
                        pool.indirect_dma_start(
                            out=yk[s][:, k, :], out_offset=None, in_=y_dram,
                            in_offset=bass.IndirectOffsetOnAxis(ap=gi[:, s, k:k + 1], axis=0))\
                            .then_inc(gathered[s], 16)
                for s in range(2):
                    var2.wait(pool, r, s + 1)
                    rstd2.after(pool.tensor_tensor(rs[:, s:s + 1], ve[:, s:s + 1], half[:, 0:1], ALU.pow))

        def tail_vector(dve):
            with dve.Fori(0, HALF) as r:
                for s in range(2):
                    e_silu.wait(dve, r, s + 1)
                    tail.read(dve.tensor_tensor(eh[s], esg[s], tail[("GU", s)][:, F1:P], ALU.mult), ("GU", s))
                for s in range(2):
                    tail.wait_full(dve, ("YO", s), r)
                    dve.wait_ge(y_out[s], r * 16 + CREDIT)
                    tail.read(dve.tensor_copy(yt[s], tail[("YO", s)][:, 0:D]), ("YO", s))
            with dve.Fori(0, TWO) as r:
                count = [0]

                def link(ins):
                    count[0] += 1
                    chain2.after(ins)
                    chain2.wait(dve, r, count[0])

                idx = gidx[:, :, :].rearrange("p r k -> p (r k)")
                w = wts[:, :, :].rearrange("p r k -> p (r k)")
                for s in range(2):
                    dve.tensor_copy(wt[:, s, :], w[:, bass.ds((2 * r + s) * TOPK, TOPK)])
                    gi_ready.after(dve.tensor_copy(gi[:, s, :], idx[:, bass.ds((2 * r + s) * TOPK, TOPK)]))
                gi_ready.wait(dve, r, 2)
                for s in range(2):
                    dve.wait_ge(shx_in[s], r * 32 + 32)
                    dve.wait_ge(gathered[s], r * 64 + 64)
                    for k in range(TOPK):
                        link(dve.scalar_tensor_tensor(acc[s], yk[s][:, k, :], wt[:, s, k:k + 1],
                                                      shx[s][:, 0, :] if k == 0 else acc[s], ALU.mult, ALU.add))
                    link(dve.bn_stats(stats[:, s, :], acc[s]))
                    settle(dve)
                    link(dve.bn_aggr(mv[:, s, :], stats[:, s, :]))
                    var2.after(dve.tensor_scalar(ve[:, s:s + 1], mv[:, s, 1:2], EPS, None, ALU.add))
                for s in range(2):
                    rstd2.wait(dve, r, s + 1)
                    dve.wait_ge(stored[s], r * 16 + CREDIT)
                    link(dve.tensor_scalar(acc[s], acc[s], mv[:, s, 0:1], rs[:, s:s + 1], ALU.subtract,
                                           ALU.mult))
                    out_ready.after(dve.tensor_tensor(ot[s], shx[s][:, 1, :], acc[s], ALU.add))
            if count[0] != chain2.per:
                raise ValueError(f"dve_chain2 is raised {count[0]} times in a round")

        block = ctx.enter_context(nc.Block())

        def tok(r, n=GROUP, o=0):
            return bass.ds(r * GROUP + o, n)

        STORES = 2
        WSLOTS = 2



        @block.sync
        def _(sp):
            for b in drained:
                sp.sem_inc(b, 1)
            for free in stored:
                sp.sem_inc(free, CREDIT)
            sp.sem_inc(out_ready.sem, 1)
            sp.dma_start(xin[:, :, :], A["x"][0:GROUP, :].rearrange("(t p) d -> p t d", p=P)).then_inc(x_in, 16)
            for dst, name in ((ident[:, :], "ident"), (iota[:, :], "iota"), (parity[:, :], "parity"),
                              (cstage[:, 0, 0:TRI], "keyq_mask"), (cstage[:, 1, 0:TRI], "qkey_mask"),
                              (cstage[:, 0, TRI:512], "earlier"),
                              (neg_in[:, :], "neg_sel"),
                              (chan[:, :, :], "chan"), (conv_w[:, :, :], "conv_w"), (conv_b[:, :], "conv_b")):
                sp.dma_start(dst, A[name]).then_inc(consts_in, 16)
            sp.dma_start(w_in[:, :, :], A["w_in"]).then_inc(w_sem["proj"], 16)
            sp.dma_start(w_out[:, :, :], A["w_out"]).then_inc(w_sem["out"], 16)
            sp.dma_start(w_gu[:, :, :], A["w_gu"]).then_inc(w_sem["ffn"], 16)
            sp.dma_start(w_dn[:, :, :], A["w_dn"]).then_inc(w_sem["ffn"], 16)
            sp.dma_start(w_lora[:, :, :], A["w_lora"]).then_inc(w_sem["lora"], 16)
            sp.dma_start(w_lb[:, :], A["w_lb"]).then_inc(w_sem["lora"], 16)
            sp.dma_start(w_att[:, :, :, :], A["w_att"]).then_inc(w_sem["att"], 16)
            sp.dma_start(att_rows[:, :, :], A["att_rows"]).then_inc(w_sem["att"], 16)
            sp.dma_start(w_rt[:, :, :], A["w_rt"]).then_inc(w_sem["moe"], 16)
            sp.dma_start(rt_bias[:, :], A["rt_bias"].broadcast_to([P, E1])).then_inc(w_sem["moe"], 16)
            sp.dma_start(w_sgu[:, :, :], A["w_sgu"]).then_inc(w_sem["moe"], 16)
            sp.dma_start(w_sdn[:, :, :], A["w_sdn"]).then_inc(w_sem["moe"], 16)
            sp.wait_ge(pads_zero, 5)
            for g in range(SLOTS // GROUP - 1):
                sp.dma_start(xg_dram[g * GROUP:(g + 1) * GROUP, :].rearrange("(t p) d -> p t d", p=P),
                             tmp[:, :, :]).then_inc(zero_filled, 16)
            with sp.Fori(0, ROUNDS - 1) as r:
                x_free.wait(sp, r, 1)
                settle(sp)
                sp.dma_start(xin[:, :, :], A["x"][bass.ds(r * GROUP + GROUP, GROUP), :]
                             .rearrange("(t p) d -> p t d", p=P)).then_inc(x_in, 16)
            tail_sync(sp)

        def transposes(pe, stage, n, src, r):
            u_ready.wait(pe, r, n)
            for c in range(DC):
                plan.wait_empty(pe, ("T", stage, c), r)
                for t in range(TILES):
                    mm = pe.transpose(plan[("T", stage, c)][:, t * P:(t + 1) * P],
                                      src[:, t, c * P:(c + 1) * P], ident[:, :])
                plan.filled(mm, ("T", stage, c))
            for c in range(DC):
                plan.wait_drained(pe, ("T", stage, c), r)

        def linear(pe, key, w, cols, r):
            plan.wait_empty(pe, key, r)
            n = cols.stop - cols.start
            for k in range(DC):
                mm = pe.matmul(plan[key][0:n, :], w[:, k, cols], uT[:, k, :], start=k == 0, stop=k == DC - 1)
            plan.filled(mm, key)

        def head_rows(h):
            return slice(32 * (h // 2 % 4), 32 * (h // 2 % 4) + 32)

        @block.tensor
        def _(pe):
            pe.wait_ge(consts_cast, 1)
            pe.wait_ge(w_sem["proj"], 16)
            with pe.Fori(0, ROUNDS) as r:
                transposes(pe, "mix", 1, u, r)
                for c in range(DC):
                    linear(pe, ("Z", c), w_in, slice(c * P, (c + 1) * P), r)
                for c in range(DC):
                    linear(pe, ("X", c), w_in, slice(D + c * P, D + (c + 1) * P), r)
                linear(pe, "dt", w_in, slice(PROJ - HEADS, PROJ), r)

                def project_bc(p):
                    for w in range(2):
                        o = 2 * D + w * HEADS * STATE + p * P
                        linear(pe, ("BC", p, w), w_in, slice(o, o + P), r)

                for c in range(DC):
                    plan.wait_empty(pe, ("Y", c), r)
                    plan.filled(pe.matmul(plan[("Y", c)][:, :], zeros_bf[:, 0:P], zeros_bf[:, :], start=True,
                                          stop=False, skip_group_check=True), ("Y", c))
                cum_ready.wait(pe, r, 1)
                plan.wait_empty(pe, "cumT", r)
                settle(pe)
                for t in range(TILES):
                    mm = pe.transpose(plan["cumT"][:, t * HEADS:(t + 1) * HEADS],
                                      cumP[:, t * P:(t + 1) * P], ident[0:HEADS, 0:HEADS])
                plan.filled(mm, "cumT")
                project_bc(0)
                for c in range(DC):
                    plan.wait_drained(pe, ("X", c), r)
                    plan.wait_empty(pe, ("XT", c), r)
                    for t in range(TILES):
                        mm = pe.transpose(plan[("XT", c)][:, t * P:(t + 1) * P],
                                          xc[:, c, t * P:(t + 1) * P], ident[:, :])
                    plan.filled(mm, ("XT", c))
                for c in range(DC):
                    plan.wait_drained(pe, ("XT", c), r)
                cum3_ready.wait(pe, r, 1)

                def decay_and_cb(n):
                    p, b, e = uses[n]
                    h = 2 * p + e
                    ka, kc = ("A", p, b, e), ("CB", p, b, e)
                    plan.wait_empty(pe, ka, r)
                    pe.matmul(plan[ka][:, 0:TRI], ident_bf[:, :], keyq_mask[:, :], start=True, stop=False)
                    plan.filled(pe.matmul(plan[ka][:, 0:TRI], neg_sel[:, h:h + 1].broadcast_to([96, P]), cum3[:, b, :],
                                          start=False, stop=True), ka)
                    plan.wait_empty(pe, kc, r)
                    rows = slice(e * STATE, (e + 1) * STATE)
                    B, C = bc[rows, p % 2, 0, :], bc[rows, p % 2, 1, :]
                    o = b * SEQ
                    pe.matmul(plan[kc][:, 0:SEQ], B[:, o:o + P], C[:, o:o + SEQ], start=True, stop=True)
                    plan.filled(pe.matmul(plan[kc][:, SEQ:TRI], B[:, o + P:o + SEQ], C[:, o + P:o + SEQ],
                                          start=True, stop=True), kc)

                def add_y(n):
                    p, b, e = uses[n]
                    q, hq = p // 2, 2 * (p % 2) + e
                    plan.wait_drained(pe, ("CB", p, b, e), r)
                    y = plan[("Y", q // 4)][32 * (q % 4):32 * (q % 4) + 32, :]
                    s = sc[:, n % 3, :]
                    o = b * SEQ
                    pe.matmul(y[:, o:o + SEQ], x_pad[:, 2 * b, q, hq, :], s[:, 0:SEQ], start=False, stop=False,
                              skip_group_check=True)
                    y_added.after(pe.matmul(y[:, o + P:o + SEQ], x_pad[:, 2 * b + 1, q, hq, :], s[:, SEQ:TRI],
                                            start=False, stop=True, skip_group_check=True))

                for p in range(PAIRS):
                    for w in range(2):
                        plan.wait_drained(pe, ("BC", p, w), r)
                    if p + 1 < PAIRS:
                        project_bc(p + 1)
                    for i in range(4):
                        n = 4 * p + i
                        decay_and_cb(n)
                        if n >= 2:
                            add_y(n - 2)
                add_y(62)
                add_y(63)

                pe.wait_ge(w_sem["out"], 16)
                for c in range(DC):
                    yg_ready.wait(pe, r, c + 1)
                for j in range(2):
                    plan.wait_empty(pe, ("O", j), r)
                    for i in range(2):
                        t = 2 * j + i
                        for c in range(DC):
                            mm = pe.matmul(plan[("O", j)][:, i * D:(i + 1) * D], yg[:, c, t * P:(t + 1) * P],
                                           w_out[:, c, :], start=c == 0, stop=c == DC - 1)
                    plan.filled(mm, ("O", j))

                transposes(pe, "ffn", 2, u, r)
                pe.wait_ge(w_sem["ffn"], 32)
                for f in range(FF // P):
                    linear(pe, ("G", f), w_gu, slice(f * P, (f + 1) * P), r)
                    linear(pe, ("U", f), w_gu, slice(FF + f * P, FF + (f + 1) * P), r)
                for f in range(FF // P - 2, FF // P):
                    plan.wait_drained(pe, ("U", f), r)
                for j in range(2):
                    plan.wait_empty(pe, ("F", j), r)
                    for i in range(2):
                        t = 2 * j + i
                        for f in range(FF // P):
                            mm = pe.matmul(plan[("F", j)][:, i * D:(i + 1) * D], hf[:, f, t * P:(t + 1) * P],
                                           w_dn[:, f, :], start=f == 0, stop=f == FF // P - 1)
                    plan.filled(mm, ("F", j))

                transposes(pe, "lora", 3, u, r)
                pe.wait_ge(w_sem["lora"], 32)
                for t in range(TILES):
                    plan.wait_empty(pe, ("L", t), r)
                    for k in range(DC):
                        mm = pe.matmul(plan[("L", t)][:, 0:LW], uT[:, k, t * P:(t + 1) * P], w_lora[:, k, :],
                                       start=k == 0, stop=k == DC - 1)
                    plan.filled(mm, ("L", t))
                hw_ready.wait(pe, r, 1)
                plan.wait_empty(pe, "LT", r)
                for t in range(TILES):
                    mm = pe.transpose(plan["LT"][:, t * P:(t + 1) * P], hw[:, t, :], ident[:, :])
                plan.filled(mm, "LT")
                plan.wait_drained(pe, "LT", r)
                for t in range(TILES):
                    lora_added.after(pe.matmul(plan[("L", t)][:, 0:D], hwT[:, t * P:(t + 1) * P], w_lb[:, :],
                                               start=False, stop=True, skip_group_check=True))

                transposes(pe, "att", 4, u, r)
                pe.wait_ge(w_sem["att"], 32)
                for c in range(DC):
                    linear(pe, ("Q", c), w_att[:, :, 0, :], slice(c * P, (c + 1) * P), r)
                    linear(pe, ("K", c), w_att[:, :, 1, :], slice(c * P, (c + 1) * P), r)
                for j in range(2):
                    plan.wait_empty(pe, ("V", j), r)
                    for i in range(2):
                        t = 2 * j + i
                        for k in range(DC):
                            pe.matmul(plan[("V", j)][:, i * D:(i + 1) * D], uT[:, k, t * P:(t + 1) * P],
                                      w_att[:, k, 2, :], start=k == 0, stop=False)
                        mm = pe.matmul(plan[("V", j)][:, i * D:(i + 1) * D], ones[0:1, 0:P], att_rows[:, 0, :],
                                       start=False, stop=True)
                    plan.filled(mm, ("V", j))
                for c in range(DC):
                    plan.wait_empty(pe, ("OT", c), r)
                    plan.filled(pe.matmul(plan[("OT", c)][:, :], zeros_bf[:, 0:P], zeros_bf[:, :], start=True,
                                          stop=False, skip_group_check=True), ("OT", c))
                for c in range(DC):
                    plan.wait_drained(pe, ("Q", c), r)
                    plan.wait_drained(pe, ("K", c), r)
                    plan.wait_drained(pe, ("V", c), r)

                def scores(n):
                    h, b = auses[n]
                    key, rows, o = ("S", n), head_rows(h), b * SEQ
                    q = qT[rows, h // 8, o:o + SEQ]
                    k = kT[h % 2][rows, h // 8, o:o + SEQ]
                    plan.wait_empty(pe, key, r)
                    pe.matmul(plan[key][:, 0:TRI], ident_bf[:, :], qkey_mask[:, :], start=True, stop=False,
                              skip_group_check=True)
                    pe.matmul(plan[key][:, 0:P], q[:, 0:P], k[:, 0:P], start=False, stop=True,
                              skip_group_check=True)
                    plan.filled(pe.matmul(plan[key][:, P:TRI], q[:, P:SEQ], k[:, 0:SEQ], start=False, stop=True,
                                          skip_group_check=True), key)

                def turn_probs(n):
                    key = ("PT", n)
                    plan.wait_empty(pe, key, r)
                    probs.wait(pe, r, n + 1)
                    for i in range(3):
                        mm = pe.transpose(plan[key][:, i * P:(i + 1) * P], pr[:, n % 3, i * P:(i + 1) * P],
                                          ident[:, :])
                    plan.filled(mm, key)

                def add_o(n):
                    h, b = auses[n]
                    plan.wait_drained(pe, ("PT", n), r)
                    o = plan[("OT", h // 8)][head_rows(h), :]
                    s = prT[:, n % 3, :]
                    pe.matmul(o[:, b * SEQ:(b + 1) * SEQ], v_pad[:, 2 * b, h // 2, h % 2, :], s[:, 0:SEQ],
                              start=False, stop=False, skip_group_check=True)
                    o_added.after(pe.matmul(o[:, b * SEQ + P:(b + 1) * SEQ],
                                            v_pad[:, 2 * b + 1, h // 2, h % 2, :], s[:, SEQ:TRI],
                                            start=False, stop=True, skip_group_check=True))

                for n in range(32 + 3):
                    if n < 32:
                        scores(n)
                    if 2 <= n < 34:
                        turn_probs(n - 2)
                    if 3 <= n:
                        add_o(n - 3)
                for c in range(DC):
                    plan.wait_drained(pe, ("OT", c), r)
                for j in range(2):
                    plan.wait_empty(pe, ("W", j), r)
                    for i in range(2):
                        t = 2 * j + i
                        for c in range(DC):
                            pe.matmul(plan[("W", j)][:, i * D:(i + 1) * D], oT[:, c, t * P:(t + 1) * P],
                                      w_att[:, c, 3, :], start=c == 0, stop=False)
                        mm = pe.matmul(plan[("W", j)][:, i * D:(i + 1) * D], ones[0:1, 0:P], att_rows[:, 1, :],
                                       start=False, stop=True)
                    plan.filled(mm, ("W", j))

                transposes(pe, "moe", 5, xf, r)
                pe.wait_ge(w_sem["moe"], 64)
                plan.wait_empty(pe, "R", r)
                for t in range(TILES):
                    for k in range(DC):
                        mm = pe.matmul(plan["R"][:, t * E1:(t + 1) * E1], uT[:, k, t * P:(t + 1) * P],
                                       w_rt[:, k, :], start=k == 0, stop=k == DC - 1)
                plan.filled(mm, "R")
                for f in range(SHF // P):
                    linear(pe, ("SG", f), w_sgu, slice(f * P, (f + 1) * P), r)
                    linear(pe, ("SU", f), w_sgu, slice(SHF + f * P, SHF + (f + 1) * P), r)
                for f in range(SHF // P - 2, SHF // P):
                    plan.wait_drained(pe, ("SU", f), r)
                for j in range(2):
                    plan.wait_empty(pe, ("SD", j), r)
                    for i in range(2):
                        t = 2 * j + i
                        for f in range(SHF // P):
                            mm = pe.matmul(plan[("SD", j)][:, i * D:(i + 1) * D], hf[:, f, t * P:(t + 1) * P],
                                           w_sdn[:, f, :], start=f == 0, stop=f == SHF // P - 1)
                    plan.filled(mm, ("SD", j))
                chosen_ready.wait(pe, r, 1)
                plan.wait_empty(pe, "pos", r)
                for t in range(TILES):
                    pe.matmul(plan["pos"][:, t * E1:(t + 1) * E1], earlier[:, :], chosen[:, t, :],
                              start=True, stop=False)
                    mm = pe.matmul(plan["pos"][:, t * E1:(t + 1) * E1], ones_bf[:, :], before[:, t, :],
                                   start=False, stop=True)
                plan.filled(mm, "pos")
            tail_tensor(pe)

        @block.scalar
        def _(act):
            act.wait_ge(consts_cast, 1)
            with act.Fori(0, ROUNDS) as r:
                def turned(stage, scale=None):
                    for c in range(DC):
                        key = ("T", stage, c)
                        plan.wait_full(act, key, r)
                        plan.read(act.activation(uT[:, c, :], plan[key][:, :], ACT.Copy,
                                                 scale=1.0 if scale is None else chan[:, c, scale:scale + 1]), key)

                def first_tap(key, dst, j):
                    plan.wait_full(act, key, r)
                    tap0.after(act.activation(dst, plan[key][:, :], ACT.Identity, bias=conv_b[:, j:j + 1],
                                              scale=conv_w[:, j, TAPS - 1:TAPS]))

                turned("mix", 2)
                for c in range(DC):
                    key = ("Z", c)
                    plan.wait_full(act, key, r)
                    plan.read(act.activation(sz[:, c, :], plan[key][:, :], ACT.Silu, bias=chan[:, c, 0:1]), key)
                for c in range(DC):
                    first_tap(("X", c), xc[:, c, :], c)
                plan.wait_full(act, "dt", r)
                dt_abs.after(act.activation(sp_a[:, :], plan["dt"][0:HEADS, :], ACT.Abs))
                dt_abs.wait(act, r, 1)
                exp_dt.after(act.activation(sp_b[:, :], sp_a[:, :], ACT.Exp, scale=-1.0))
                exp_dt.wait(act, r, 1)
                dt_log.after(act.activation(sp_a[:, :], sp_b[:, :], ACT.Ln, bias=1.0))
                plan.wait_full(act, "cumT", r)
                plan.read(act.activation(cum_tok[:, :, :], plan["cumT"][:, 0:TILES * HEADS]
                                         .rearrange("p (t h) -> p t h", t=TILES), ACT.Copy), "cumT")
                for w in range(2):
                    first_tap(("BC", 0, w), bc[:, 0, w, :], 2 + 16 * w)
                plan.wait_drained(act, "cumT", r)
                for p in range(PAIRS):
                    if p + 1 < PAIRS:
                        for w in range(2):
                            first_tap(("BC", p + 1, w), bc[:, (p + 1) % 2, w, :], 2 + 16 * w + p + 1)
                    for i in range(4):
                        n = 4 * p + i
                        _, b, e = uses[n]
                        h = 2 * p + e
                        key = ("A", p, b, e)
                        plan.wait_full(act, key, r)
                        if n >= 3:
                            plan.wait_drained(act, ("CB", *uses[n - 3]), r)
                        act.activation(dec[:, n % 3, 0:SEQ], plan[key][:, 0:SEQ], ACT.Exp,
                                       bias=cum_tok[:, 2 * b, h:h + 1])
                        plan.read(act.activation(dec[:, n % 3, SEQ:TRI], plan[key][:, SEQ:TRI], ACT.Exp,
                                                 bias=cum_tok[:, 2 * b + 1, h:h + 1]), key)
                for t in range(TILES):
                    if t % 2 == 0:
                        plan.wait_drained(act, ("O", t // 2), r)
                    sumsq.after(act.activation(tmp[:, t, :], h1[:, t, :], ACT.Square, scale=1.0 / 16,
                                               accum_out=sm[:, t:t + 1]))
                turned("ffn", 3)

                def silu_gate(gk, uk, f):
                    plan.wait_full(act, (gk, f), r)
                    if f >= 2:
                        plan.wait_drained(act, (uk, f - 2), r)
                    plan.read(act.activation(sg[:, f % 2, :], plan[(gk, f)][:, :], ACT.Silu), (gk, f))

                for f in range(FF // P):
                    silu_gate("G", "U", f)
                turned("lora")
                for t in range(TILES):
                    plan.wait_full(act, ("L", t), r)
                    lora_lg.after(act.activation(lg0[:, t, :], plan[("L", t)][:, D:D + EXPERTS0], ACT.Copy))
                lora_top.wait(act, r, 1)
                lora_exp.after(act.activation(wk[:, :, 0:2], wk[:, :, 0:2], ACT.Exp))
                plan.wait_full(act, "LT", r)
                plan.read(act.activation(hwT, plan["LT"][:, :], ACT.Copy), "LT")
                turned("att")
                for c in range(DC):
                    plan.wait_full(act, ("Q", c), r)
                    plan.read(act.activation(qT[:, c, :], plan[("Q", c)][:, :], ACT.Identity,
                                             bias=qbias[:, c:c + 1], scale=0.25), ("Q", c))
                    plan.wait_full(act, ("K", c), r)
                    act.activation(kT[0][:, c, :], plan[("K", c)][:, :], ACT.Identity,
                                   bias=kbias[:, c, 0:1], scale=parity[:, 0:1])
                    plan.read(act.activation(kT[1][:, c, :], plan[("K", c)][:, :], ACT.Identity,
                                             bias=kbias[:, c, 1:2], scale=parity[:, 1:2]), ("K", c))
                for n in range(32 + 2):
                    if n < 32:
                        nmax_ready.wait(act, r, n + 1)
                        if n >= 3:
                            plan.wait_full(act, ("PT", n - 3), r)
                        for i, cols in enumerate((slice(0, P), slice(P, TRI))):
                            mm = act.activation(pr[:, n % 3, cols], plan[("S", n)][:, cols], ACT.Exp,
                                                bias=nmax[:, n % 4, i:i + 1], accum_out=esum[:, n % 4, i:i + 1])
                        plan.read(mm, ("S", n))
                    if n >= 2:
                        m = n - 2
                        plan.wait_full(act, ("PT", m), r)
                        if m >= 3:
                            o_added.wait(act, r, m - 2)
                        plan.read(act.activation(prT[:, m % 3, :], plan[("PT", m)][:, 0:TRI], ACT.Copy),
                                  ("PT", m))
                for c in range(DC):
                    o_added.wait(act, r, 16 * (c + 1))
                    plan.read(act.activation(oT[:, c, :], plan[("OT", c)][:, :], ACT.Copy), ("OT", c))
                turned("moe")
                for f in range(SHF // P):
                    silu_gate("SG", "SU", f)
                top_ready.wait(act, r, 1)
                top_exp.after(act.activation(wk[:, :, :], lk[:, :, :], ACT.Exp))
            tail_scalar(act)

        @block.gpsimd
        def _(pool):
            pool.memset(half[:, :], -0.5).then_inc(pads_zero, 1)
            pool.memset(tmp[:, :, :], 0.0).then_inc(pads_zero, 1)
            pool.memset(x_pad[:, :, :, :, :], 0.0).then_inc(pads_zero, 1)
            pool.memset(v_pad[:, :, :, :, :], 0.0).then_inc(pads_zero, 1)
            pool.memset(before[:, :, :], 0.0).then_inc(pads_zero, 1)
            pool.wait_ge(pads_zero, 5)
            pool.dma_start(xg_dram[SLOTS - GROUP:SLOTS, :].rearrange("(t p) d -> p t d", p=P),
                           tmp[:, :, :]).then_inc(scattered, CREDIT)
            for s in range(2):
                pool.dma_start(y_dram[SLOTS + s * (P // 2):SLOTS + (s + 1) * (P // 2), :],
                               tmp[0:P // 2, 0, :]).then_inc(y_out[s], CREDIT)
            pool.wait_ge(zero_filled, 16 * (SLOTS // GROUP - 1))
            for zeroed in (scattered, *y_out):
                pool.wait_ge(zeroed, CREDIT)
            with pool.Fori(0, ROUNDS) as r:
                for n in range(9):
                    var_ready.wait(pool, r, n + 1)
                    rstd_ready.after(pool.tensor_tensor(rs[:, :], ve[:, :], half[:, :], ALU.pow))
                    if n == 8:
                        x3_ready.wait(pool, r, 1)
                        settle(pool)
                        pool.dma_start(x3_dram[tok(r), :].rearrange("(t p) d -> p t d", p=P),
                                       x1[:, :, :]).then_inc(xf_stored, 16)
                sidx_ready.wait(pool, r, 1)
                settle(pool)
                for i in range(TILES * TOPK):
                    pool.indirect_dma_start(
                        out=xg_dram, out_offset=bass.IndirectOffsetOnAxis(ap=sidx[:, i:i + 1], axis=0),
                        in_=xf[:, i // TOPK, :], in_offset=None, bounds_check=SLOTS - 1,
                        oob_is_err=False).then_inc(scattered, 16)
                for j in range(2):
                    plan.wait_drained(pool, ("SD", j), r)
                settle(pool)
                pool.dma_start(sh_dram[tok(r), :].rearrange("(t p) d -> p t d", p=P),
                               hn[:, :, :]).then_inc(xf_stored, 16)
            tail_pool(pool)

        @block.vector
        def _(dve):
            dve.wait_ge(pads_zero, 5)
            dve.wait_ge(consts_in, 160)
            dve.tensor_copy(ident_bf[:, :], ident[:, :])
            dve.tensor_copy(keyq_mask[:, :], cstage[:, 0, 0:TRI])
            dve.tensor_copy(qkey_mask[:, :], cstage[:, 1, 0:TRI])
            dve.tensor_copy(earlier[:, :], cstage[:, 0, TRI:512])
            dve.memset(ones_bf[:, :], 1.0)
            dve.memset(zeros_bf[:, :], 0.0)
            dve.memset(ones[:, :], 1.0)
            dve.tensor_copy(neg_sel[:, :], neg_in[:, :])
            for c in range(DC):
                for e in range(2):
                    dve.tensor_tensor(kbias[:, c, e:e + 1], chan[:, c, 5:6], parity[:, e:e + 1], ALU.mult)
                dve.tensor_scalar(qbias[:, c:c + 1], chan[:, c, 4:5], 0.25, None, ALU.mult)
            dve.memset(stats[:, 0, 0:1], 0.0).then_inc(consts_cast, 1)
            dve.wait_ge(consts_cast, 1)
            for zeroed, n in ((zero_filled, 16 * (SLOTS // GROUP - 1)), (scattered, CREDIT),
                              (y_out[0], CREDIT), (y_out[1], CREDIT)):
                dve.wait_ge(zeroed, n)

            with dve.Fori(0, ROUNDS) as r:
                count = [0]

                def link(ins):
                    count[0] += 1
                    chain.after(ins)
                    chain.wait(dve, r, count[0])

                norms = [0]

                def inv_std(variance, eps=True):
                    norms[0] += 1
                    var_ready.after(dve.tensor_scalar(ve[:, :], variance, EPS, None, ALU.add))
                    rstd_ready.wait(dve, r, norms[0])

                def moments(srcs):
                    for t, s in enumerate(srcs):
                        ins = dve.bn_stats(stats[:, t, :], s)
                    link(ins)
                    settle(dve)
                    for t in range(TILES):
                        ins = dve.bn_aggr(mv[:, t, :], stats[:, t, :])
                    link(ins)

                def norm(srcs, dst):
                    moments(srcs)
                    inv_std(mv[:, :, 1])
                    for t, s in enumerate(srcs):
                        ins = dve.tensor_scalar(dst[:, t, :], s, mv[:, t, 0:1], rs[:, t:t + 1],
                                                ALU.subtract, ALU.mult)
                    return ins

                def tiles(x):
                    return [x[:, t, :] for t in range(TILES)]

                def taps(keys):
                    for s in range(1, TAPS):
                        for n, (key, dst, j) in enumerate(keys):
                            if s == 1:
                                tap0.wait(dve, r, taps_done[0] + n + 1)
                            d = dst.rearrange("p (b l) -> p b l", b=SEQS)[:, :, s:SEQ]
                            x = plan[key][:, :].rearrange("p (b l) -> p b l", b=SEQS)[:, :, 0:SEQ - s]
                            ins = dve.scalar_tensor_tensor(d, x, conv_w[:, j, TAPS - 1 - s:TAPS - s], d,
                                                           ALU.mult, ALU.add)
                            if s < TAPS - 1:
                                chain.after(ins)
                                count[0] += 1
                            else:
                                plan.read(ins, key)
                        if s < TAPS - 1:
                            chain.wait(dve, r, count[0])
                    taps_done[0] += len(keys)

                taps_done = [0]

                dve.wait_ge(x_in, r * 16 + 16)
                moments(tiles(xin))
                inv_std(mv[:, :, 1])
                link(dve.tensor_copy(r1[:, :], rs[:, :]))
                for t in range(TILES):
                    dve.tensor_scalar(hn[:, t, :], xin[:, t, :], mv[:, t, 0:1], r1[:, t:t + 1],
                                      ALU.subtract, ALU.mult)
                link(dve.tensor_tensor(sm[:, :], mv[:, :, 1], r1[:, :], ALU.mult))
                link(dve.tensor_tensor(sm[:, :], sm[:, :], r1[:, :], ALU.mult))
                inv_std(sm[:, :])
                for t in range(TILES):
                    ins = dve.tensor_scalar(u[:, t, :], hn[:, t, :], rs[:, t:t + 1], None, ALU.mult)
                u_ready.after(ins)

                taps([(("X", c), xc[:, c, :], c) for c in range(DC)])
                plan.wait_full(dve, "dt", r)
                dt = plan["dt"][0:HEADS, :]
                dt_log.wait(dve, r, 1)
                plan.read(dve.scalar_tensor_tensor(sp_b[:, :], dt, 0.0, sp_a[:, :], ALU.max, ALU.add), "dt")
                plan.wait_drained(dve, "dt", r)
                for b in range(SEQS):
                    ins = dve.tensor_tensor_scan(cumP[:, b * SEQ:(b + 1) * SEQ], ones[0:HEADS, :],
                                                 sp_b[:, b * SEQ:(b + 1) * SEQ], 0.0, ALU.mult, ALU.add)
                cum_ready.after(ins)
                cum_ready.wait(dve, r, 1)
                by_seq = cumP[:, :].rearrange("p (b l) -> p b l", b=SEQS)
                rest = sp_a[:, :].rearrange("p (b l) -> p b l", b=SEQS)
                mid = mid0[:, :].rearrange("p (b l) -> p b l", b=SEQS)
                link(dve.tensor_copy(cum3[0:HEADS, :, 0:SEQ], by_seq))
                link(dve.tensor_tensor(rest, by_seq, cum3[0:HEADS, :, 0:SEQ], ALU.subtract))
                link(dve.tensor_copy(mid, rest))
                dve.tensor_copy(cum3[HEADS:2 * HEADS, :, 0:SEQ], mid)
                link(dve.tensor_tensor(rest, rest, mid, ALU.subtract))
                link(dve.tensor_copy(cum3[2 * HEADS:96, :, 0:SEQ], rest))
                cum3_ready.after(dve.tensor_copy(cum3[:, :, SEQ:TRI], cum3[:, :, P:SEQ]))
                taps([(("BC", 0, w), bc[:, 0, w, :], 2 + 16 * w) for w in range(2)])
                for c in range(DC):
                    plan.wait_full(dve, ("XT", c), r)
                    src = plan[("XT", c)][:, :].rearrange("p (t q h d) -> p t q h d", t=TILES, q=4, h=4)
                    for t in range(TILES):
                        for hq in range(4):
                            ins = dve.tensor_copy(x_pad[:, t, 4 * c:4 * c + 4, hq, 8 * hq:8 * hq + 8],
                                                  src[:, t, :, hq, :])
                    plan.read(ins, ("XT", c))
                for p in range(PAIRS):
                    if p + 1 < PAIRS:
                        taps([(("BC", p + 1, w), bc[:, (p + 1) % 2, w, :], 2 + 16 * w + p + 1)
                              for w in range(2)])
                    for i in range(4):
                        n = 4 * p + i
                        key = ("CB", *uses[n])
                        plan.wait_drained(dve, ("A", *uses[n]), r)
                        plan.wait_full(dve, key, r)
                        if n >= 3:
                            y_added.wait(dve, r, n - 2)
                        plan.read(dve.tensor_tensor(sc[:, n % 3, :], dec[:, n % 3, :], plan[key][:, 0:TRI],
                                                    ALU.mult), key)
                for c in range(DC):
                    y_added.wait(dve, r, 32 * (c + 1))
                    plan.read(dve.scalar_tensor_tensor(yg[:, c, :], xc[:, c, :], chan[:, c, 1:2],
                                                       plan[("Y", c)][:, :], ALU.mult, ALU.add), ("Y", c))
                for c in range(DC):
                    plan.wait_drained(dve, ("Y", c), r)
                    yg_ready.after(dve.tensor_tensor(yg[:, c, :], yg[:, c, :], sz[:, c, :], ALU.mult))
                flat = h1[:, :, :].rearrange("p t d -> p (t d)")
                for j in range(2):
                    plan.wait_full(dve, ("O", j), r)
                    plan.read(dve.tensor_tensor(flat[:, j * 512:(j + 1) * 512], plan[("O", j)][:, :],
                                                hn[:, :, :].rearrange("p t d -> p (t d)")[:, j * 512:(j + 1) * 512],
                                                ALU.add), ("O", j))
                sumsq.wait(dve, r, TILES)
                inv_std(sm[:, :])
                for t in range(TILES):
                    ins = dve.tensor_scalar(u[:, t, :], h1[:, t, :], rs[:, t:t + 1], None, ALU.mult)
                u_ready.after(ins)

                def gate(gk, uk, f):
                    plan.wait_drained(dve, (gk, f), r)
                    plan.wait_full(dve, (uk, f), r)
                    plan.read(dve.tensor_tensor(hf[:, f, :], sg[:, f % 2, :], plan[(uk, f)][:, :], ALU.mult),
                              (uk, f))

                for f in range(FF // P):
                    gate("G", "U", f)
                for j in range(2):
                    plan.wait_full(dve, ("F", j), r)
                    plan.read(dve.tensor_tensor(flat[:, j * 512:(j + 1) * 512], plan[("F", j)][:, :],
                                                flat[:, j * 512:(j + 1) * 512], ALU.add), ("F", j))
                for j in range(2):
                    plan.wait_drained(dve, ("F", j), r)
                link(norm(tiles(h1), tmp))
                x_free.after(dve.tensor_tensor(x1[:, :, :], xin[:, :, :], tmp[:, :, :], ALU.add))
                x_free.wait(dve, r, 1)

                u_ready.after(norm(tiles(x1), u))
                lora_lg.wait(dve, r, TILES)
                settle(dve)
                for t in range(TILES):
                    ins = dve.max(mx[:, t, :], lg0[:, t, :])
                link(ins)
                settle(dve)
                lora_top.after(dve.tensor_tensor(wk[:, :, 0:2], mx[:, :, 0:2],
                                                 mx[:, :, 0:1].broadcast_to([P, TILES, 2]), ALU.subtract))
                for t in range(TILES):
                    ins = dve.max_index(ix[:, t, :], mx[:, t, :], lg0[:, t, :])
                link(ins)
                link(dve.tensor_copy(ixf[:, :, 0:2], ix[:, :, 0:2]))
                dve.tensor_tensor(oh0[:, :, :, :],
                                  ixf[:, :, 0:2].unsqueeze(3).broadcast_to([P, TILES, 2, EXPERTS0]),
                                  iota[:, 0:EXPERTS0].unsqueeze(1).unsqueeze(1)
                                  .broadcast_to([P, TILES, 2, EXPERTS0]), ALU.is_equal)
                lora_exp.wait(dve, r, 1)
                link(dve.tensor_tensor(wsum[:, :], wk[:, :, 0], wk[:, :, 1], ALU.add))
                link(dve.reciprocal(wsum[:, :], wsum[:, :]))
                link(dve.scalar_tensor_tensor(wk[:, :, 0:2], wk[:, :, 0:2], LORA_ALPHA,
                                              wsum[:, :].unsqueeze(2).broadcast_to([P, TILES, 2]),
                                              ALU.mult, ALU.mult))
                link(dve.tensor_tensor(oh0[:, :, :, :], oh0[:, :, :, :],
                                       wk[:, :, 0:2].unsqueeze(3).broadcast_to([P, TILES, 2, EXPERTS0]),
                                       ALU.mult))
                link(dve.tensor_tensor(wm[:, :, :], oh0[:, :, 0, :], oh0[:, :, 1, :], ALU.add))
                for t in range(TILES):
                    ins = dve.tensor_tensor(
                        hw[:, t, :].rearrange("p (e r) -> p e r", e=EXPERTS0),
                        plan[("L", t)][:, D + EXPERTS0:LW].rearrange("p (e r) -> p e r", e=EXPERTS0),
                        wm[:, t, :].unsqueeze(2).broadcast_to([P, EXPERTS0, RANK]), ALU.mult)
                hw_ready.after(ins)
                lora_added.wait(dve, r, TILES)
                moments([plan[("L", t)][:, 0:D] for t in range(TILES)])
                inv_std(mv[:, :, 1])
                for t in range(TILES):
                    plan.read(dve.tensor_scalar(tmp[:, t, :], plan[("L", t)][:, 0:D], mv[:, t, 0:1],
                                                rs[:, t:t + 1], ALU.subtract, ALU.mult), ("L", t))
                for t in range(TILES):
                    plan.wait_drained(dve, ("L", t), r)
                link(dve.tensor_tensor(x1[:, :, :], x1[:, :, :], tmp[:, :, :], ALU.add))

                u_ready.after(norm(tiles(x1), u))
                for j in range(2):
                    plan.wait_full(dve, ("V", j), r)
                    for i in range(2):
                        src = plan[("V", j)][:, i * D:(i + 1) * D].rearrange("p (g e d) -> p g e d", e=2, d=DK)
                        for e in range(2):
                            ins = dve.tensor_copy(v_pad[:, 2 * j + i, :, e, DK * e:DK * e + DK], src[:, :, e, :])
                    plan.read(ins, ("V", j))
                for n in range(32 + 1):
                    if n < 32:
                        plan.wait_full(dve, ("S", n), r)
                        for i, cols in enumerate((slice(0, P), slice(P, TRI))):
                            ins = dve.tensor_reduce(nmax[:, n % 4, i:i + 1], plan[("S", n)][:, cols], AX.X,
                                                    ALU.max, negate=True)
                        nmax_ready.after(ins)
                    if n >= 1:
                        m = n - 1
                        plan.wait_drained(dve, ("S", m), r)
                        link(dve.reciprocal(esum[:, m % 4, :], esum[:, m % 4, :]))
                        for i, cols in enumerate((slice(0, P), slice(P, TRI))):
                            ins = dve.tensor_scalar(pr[:, m % 3, cols], pr[:, m % 3, cols],
                                                    esum[:, m % 4, i:i + 1], None, ALU.mult)
                        probs.after(ins)
                for j in range(2):
                    plan.wait_full(dve, ("W", j), r)
                for j in range(2):
                    plan.read(dve.tensor_copy(flat[:, j * 512:(j + 1) * 512], plan[("W", j)][:, :]), ("W", j))
                for j in range(2):
                    plan.wait_drained(dve, ("W", j), r)
                link(norm(tiles(h1), tmp))
                x3_ready.after(dve.tensor_tensor(x1[:, :, :], x1[:, :, :], tmp[:, :, :], ALU.add))
                x3_ready.wait(dve, r, 1)

                dve.wait_ge(scattered, r * (TILES * TOPK * 16) + CREDIT)
                u_ready.after(norm(tiles(x1), xf))
                plan.wait_full(dve, "R", r)
                plan.read(dve.tensor_copy(lgt[:, :, :].rearrange("p t e -> p (t e)"),
                                          plan["R"][:, 0:TILES * E1]), "R")
                plan.wait_drained(dve, "R", r)
                for f in range(SHF // P):
                    gate("SG", "SU", f)
                link(dve.tensor_tensor(biased[:, :, :], lgt[:, :, :],
                                       rt_bias[:, :].unsqueeze(1).broadcast_to([P, TILES, E1]), ALU.add))
                settle(dve)
                for t in range(TILES):
                    ins = dve.max(mx[:, t, :], biased[:, t, :])
                link(ins)
                settle(dve)
                for t in range(TILES):
                    ins = dve.max_index(ix[:, t, :], mx[:, t, :], biased[:, t, :])
                link(ins)
                link(dve.tensor_copy(ixf[:, :, :], ix[:, :, 0:TOPK]))
                link(dve.tensor_tensor(oh, ixf[:, :, :].unsqueeze(3).broadcast_to([P, TILES, TOPK, E1]),
                                       iota[:, :].unsqueeze(1).unsqueeze(1).broadcast_to([P, TILES, TOPK, E1]),
                                       ALU.is_equal))
                with nc.allow_low_precision(reason="sums of zeros and ones up to one are exact"):
                    link(dve.tensor_reduce(chosen[:, :, :], oh.rearrange("p t k e -> p t e k"), AX.X, ALU.add))
                for t in range(TILES):
                    ins = dve.tensor_tensor(before[:, t + 1, :], before[:, t, :], chosen[:, t, :], ALU.add)
                    if t < TILES - 1:
                        link(ins)
                chosen_ready.after(ins)
                link(dve.tensor_tensor(prod, oh, lgt[:, :, :].unsqueeze(2).broadcast_to([P, TILES, TOPK, E1]),
                                       ALU.mult))
                link(dve.tensor_reduce(lk[:, :, :], prod, AX.X, ALU.add))
                link(dve.tensor_reduce(wsum[:, :], lk[:, :, :], AX.X, ALU.max))
                top_ready.after(dve.tensor_tensor(lk[:, :, :], lk[:, :, :],
                                                  wsum[:, :].unsqueeze(2).broadcast_to([P, TILES, TOPK]),
                                                  ALU.subtract))
                top_exp.wait(dve, r, 1)
                link(dve.tensor_reduce(wsum[:, :], wk[:, :, :], AX.X, ALU.add))
                link(dve.reciprocal(wsum[:, :], wsum[:, :]))
                dve.tensor_tensor(wts[:, bass.ds(r, 1), :].rearrange("p o (t k) -> p (o t) k", t=TILES),
                                  wk[:, :, :], wsum[:, :].unsqueeze(2).broadcast_to([P, TILES, TOPK]), ALU.mult)
                plan.wait_full(dve, "pos", r)
                plan.read(dve.tensor_tensor(
                    prod, oh, plan["pos"][:, 0:TILES * E1].rearrange("p (t e) -> p t e", t=TILES)
                    .unsqueeze(2).broadcast_to([P, TILES, TOPK, E1]), ALU.mult), "pos")
                plan.wait_drained(dve, "pos", r)
                link(dve.tensor_copy(before[:, 0, :], before[:, TILES, :]))
                link(dve.tensor_reduce(slot[:, :, :], prod, AX.X, ALU.add))
                link(dve.tensor_scalar(over[:, :, :], slot[:, :, :], float(CAP), float(4 * SLOTS),
                                       ALU.is_ge, ALU.mult))
                link(dve.scalar_tensor_tensor(slot[:, :, :], ixf[:, :, :], float(CAP), slot[:, :, :],
                                              ALU.mult, ALU.add))
                link(dve.tensor_tensor(slot[:, :, :], slot[:, :, :], over[:, :, :], ALU.add))
                dve.tensor_scalar(gidx[:, bass.ds(r, 1), :].rearrange("p o (t k) -> p (o t) k", t=TILES),
                                  slot[:, :, :], float(SLOTS), None, ALU.min)
                sidx_ready.after(dve.tensor_copy(sidx[:, :].rearrange("p (t k) -> p t k", t=TILES),
                                                 slot[:, :, :]))
                for j in range(2):
                    plan.wait_full(dve, ("SD", j), r)
                    ins = dve.tensor_copy(hn[:, :, :].rearrange("p t d -> p (t d)")[:, j * 512:(j + 1) * 512],
                                          plan[("SD", j)][:, :])
                    plan.read(ins, ("SD", j))
                dve.wait_ge(xf_stored, r * 32 + 32)
            if count[0] != chain.per:
                raise ValueError(f"dve_chain is raised {count[0]} times in a round")
            tail_vector(dve)


_SHAPE = (8, 256, 256)


def _layouts(np, i):
    f = np.float32

    def chunks(w):
        return np.ascontiguousarray(w.reshape(-1, 128, w.shape[1]).transpose(1, 0, 2))

    def channels(*vs):
        out = np.zeros((128, 2, 8), f)
        for n, v in enumerate(vs):
            out[:, :, n] = v.reshape(2, 128).T
        return out

    k, q = np.arange(128)[:, None], np.arange(128)[None, :]
    low = np.where(q >= k, 0.0, -1e30).astype(f)
    none = np.zeros((128, 128), f)
    att = [i["L1_attn_" + n] for n in ("Wq", "Wk", "Wv", "Wo")]
    perm = np.arange(256)
    gu = np.concatenate([i["L1_ffn_gate_w"], i["L1_ffn_up_w"]], 1)
    a = {
        "x": np.ascontiguousarray(i["L0_attn_hidden_states"].reshape(-1, 256)),
        "ident": np.eye(128, dtype=f),
        "iota": np.tile(np.arange(64, dtype=f), (128, 1)),
        "parity": np.stack([(np.arange(128) % 32 < 16), (np.arange(128) % 32 >= 16)], 1).astype(f),
        "keyq_mask": np.concatenate([low, none, low], 1),
        "qkey_mask": np.concatenate([low.T, none, low.T], 1),
        "earlier": (k < q).astype(f),
        "neg_sel": -np.tile(np.eye(32, dtype=f), (3, 1)),
        "chan": channels(i["L0_attn_z_bias"], np.repeat(i["L0_attn_D"], 8), i["L0_attn_norm1_w"],
                         i["L0_attn_norm2_w"], i["L1_attn_bq"], i["L1_attn_bk"]),
        "conv_w": np.ascontiguousarray(i["L0_attn_conv_w"].reshape(34, 128, 4).transpose(1, 0, 2)),
        "conv_b": np.ascontiguousarray(i["L0_attn_conv_b"].reshape(34, 128).T),
        "w_in": chunks(i["L0_attn_in_proj_w"].T),
        "w_out": chunks(i["L0_attn_out_proj_w"].T),
        "w_gu": chunks(np.concatenate([i["L0_attn_gate_w"], i["L0_attn_up_w"]], 0).T),
        "w_dn": chunks(i["L0_attn_down_w"].T),
        "w_lora": chunks(np.concatenate([i["L0_ffn_W"], i["L0_ffn_gate_w"],
                                         i["L0_ffn_A"].reshape(128, 256)], 0).T),
        "w_lb": np.ascontiguousarray(i["L0_ffn_B"].transpose(0, 2, 1).reshape(128, 256)),
        "w_att": np.ascontiguousarray(np.stack(att, 1).reshape(2, 128, 4, 256).transpose(1, 0, 2, 3)),
        "att_rows": np.stack([i["L1_attn_bv"], i["L1_attn_bo"]])[None],
        "w_rt": chunks(i["L1_ffn_router_w"].T),
        "rt_bias": i["L1_ffn_router_bias"][None, :],
        "w_sgu": chunks(np.concatenate([i["L1_ffn_sh_gate_w"].reshape(512, 256),
                                        i["L1_ffn_sh_up_w"].reshape(512, 256)], 0).T),
        "w_sdn": chunks(i["L1_ffn_sh_down_w"].transpose(0, 2, 1).reshape(512, 256)),
        "w_egu": np.ascontiguousarray(gu.transpose(2, 0, 1).reshape(2, 128, 64, 128).transpose(1, 0, 2, 3)),
        "w_edn": np.ascontiguousarray(i["L1_ffn_down_w"].transpose(2, 0, 1)),
    }
    return {n: np.ascontiguousarray(v) for n, v in a.items()}


def kernel(**inputs):
    import numpy as _np
    import concourse.bacc as _bacc
    from concourse import mybir as _mybir
    from concourse.bass_utils import run_bass_kernel_spmd as _run

    nc = _bacc.Bacc("TRN2", target_bir_lowering=False, num_devices=1)
    arrays = _layouts(_np, {n: _np.asarray(v) for n, v in inputs.items()})
    aps = {n: nc.dram_tensor("in_" + n, v.shape, _mybir.dt.from_np(v.dtype), kind="ExternalInput").ap()
           for n, v in arrays.items()}
    out = nc.dram_tensor("out_dram", (TOKENS, D), F32, kind="ExternalOutput").ap()
    sandwich(nc, aps, out)
    r = _run(nc, [{"in_" + n: v for n, v in arrays.items()}], core_ids=[0])
    return r.results[0]["out_dram"].reshape(_SHAPE)
```

```python
from contextlib import ExitStack

import concourse.bass as bass
from concourse import mybir

ALU = mybir.AluOpType
ACT = mybir.ActivationFunctionType
AX = mybir.AxisListType
F32 = mybir.dt.float32
BF16 = mybir.dt.bfloat16
U32 = mybir.dt.uint32

P = 128
D = 256
DC = D // P
SEQ = 256
TOKENS = 8 * SEQ
GROUP = 512
ROUNDS = TOKENS // GROUP
TILES = GROUP // P
SEQS = GROUP // SEQ
EPS = 1e-5
MASKED = -1e30

HEADS = 32
STATE = 64
HEADDIM = D // HEADS
TAPS = 4
PAIRS = HEADS // 2
PROJ = 2 * D + 2 * HEADS * STATE + HEADS
QUADS = HEADS // 4
HALF = GROUP // 2
TRI = 3 * P
FF = 1024
EXPERTS0, RANK, LORA_ALPHA = 8, 16, 16.0
LW = D + EXPERTS0 + EXPERTS0 * RANK
AHEADS = 16
DK = D // AHEADS
E1, TOPK, F1, CAP = 64, 4, 64, 32
SHF = 512
SLOTS = E1 * CAP
EG = P // CAP
EGROUPS = E1 // EG


class BankPlan:

    def __init__(self, banks, full, drained):
        self.banks, self.full, self.drained = banks, full, drained
        self.place, self.count = {}, [0] * len(banks)
        self.base = [0] * len(banks)

    def use(self, key, bank):
        self.place[key] = (bank, self.count[bank])
        self.count[bank] += 1

    def __getitem__(self, key):
        return self.banks[self.place[key][0]]

    def wait_empty(self, eng, key, r):
        b, n = self.place[key]
        eng.wait_ge(self.drained[b], self.value(b, n, r) + 1)

    def wait_full(self, eng, key, r):
        b, n = self.place[key]
        eng.wait_ge(self.full[b], self.value(b, n + 1, r))

    def wait_drained(self, eng, key, r):
        b, n = self.place[key]
        eng.wait_ge(self.drained[b], self.value(b, n + 1, r) + 1)

    def value(self, b, n, r):
        return r * self.count[b] + self.base[b] + n

    def filled(self, ins, key):
        ins.then_inc(self.full[self.place[key][0]], 1)

    def read(self, ins, key):
        ins.then_inc(self.drained[self.place[key][0]], 1)


class Signal:

    def __init__(self, sem, per):
        self.sem, self.per = sem, per

    def wait(self, eng, r, n):
        eng.wait_ge(self.sem, r * self.per + n)

    def after(self, ins):
        ins.then_inc(self.sem, 1)


def sandwich(nc, A, out):
    with ExitStack() as ctx:
        def sb(name, shape, dt=F32):
            return ctx.enter_context(nc.sbuf_tensor(name, shape, dt))

        def sem(name):
            return ctx.enter_context(nc.semaphore(name))

        consts_cast = sem("consts_cast")
        settled = sem("settled")

        def settle(eng):
            eng.sem_inc(settled, 1)

        def signal(name, per):
            return Signal(sem(name), per)

        banks = [ctx.enter_context(nc.psum_tensor(f"bank{i}", [P, 512], F32)) for i in range(8)]
        full = [sem(f"bank_full{i}") for i in range(8)]
        drained = [sem(f"bank_drained{i}") for i in range(8)]

        xg_dram = nc.dram_tensor("xg_dram", (SLOTS, D), F32, kind="Internal").ap()
        y_dram = nc.dram_tensor("y_dram", (SLOTS + P, D), F32, kind="Internal").ap()
        x3_dram = nc.dram_tensor("x3_dram", (TOKENS, D), F32, kind="Internal").ap()
        sh_dram = nc.dram_tensor("sh_dram", (TOKENS, D), F32, kind="Internal").ap()

        ident = sb("ident", [P, P])
        ident_bf = sb("ident_bf", [P, P], BF16)
        keyq_mask = sb("keyq_mask", [P, TRI], BF16)
        qkey_mask = sb("qkey_mask", [P, TRI], BF16)
        earlier = sb("earlier", [P, P], BF16)
        ones_bf = sb("ones_bf", [P, P], BF16)
        zeros_bf = sb("zeros_bf", [P, 512], BF16)
        neg_sel = sb("neg_sel", [96, HEADS], BF16)
        ones = sb("ones", [P, SEQ])
        iota = sb("iota", [P, E1])
        half = sb("half", [P, TILES])
        parity = sb("parity", [P, 2])
        neg_in = sb("neg_in", [96, HEADS])
        w_in = sb("w_in", [P, DC, PROJ])
        conv_w = sb("conv_w", [P, 34, TAPS])
        conv_b = sb("conv_b", [P, 34])
        chan = sb("chan", [P, DC, 8])
        kbias = sb("kbias", [P, DC, 2])
        qbias = sb("qbias", [P, DC])
        w_out = sb("w_out", [P, DC, D])
        w_gu = sb("w_gu", [P, DC, 2 * FF])
        w_dn = sb("w_dn", [P, FF // P, D])
        w_lora = sb("w_lora", [P, DC, LW])
        w_lb = sb("w_lb", [P, D])
        w_att = sb("w_att", [P, DC, 4, D])
        att_rows = sb("att_rows", [P, 2, D])
        w_rt = sb("w_rt", [P, DC, E1])
        rt_bias = sb("rt_bias", [P, E1])
        w_sgu = sb("w_sgu", [P, DC, 2 * SHF])
        w_sdn = sb("w_sdn", [P, SHF // P, D])

        xin = sb("xin", [P, TILES, D])
        hn = sb("hn", [P, TILES, D])
        u = sb("u", [P, TILES, D])
        uT = sb("uT", [P, DC, GROUP])
        h1 = sb("h1", [P, TILES, D])
        cstage = h1[:, :, :].rearrange("p (a t) d -> p a (t d)", a=2)
        x1 = sb("x1", [P, TILES, D])
        tmp = sb("tmp", [P, TILES, D])
        xf = sb("xf", [P, TILES, D])
        stats = sb("stats", [P, TILES, 6])
        mv = sb("mv", [P, TILES, 2])
        ve = sb("ve", [P, TILES])
        rs = sb("rs", [P, TILES])
        r1 = sb("r1", [P, TILES])
        sm = sb("sm", [P, TILES])
        hf = sb("hf", [P, FF // P, GROUP])
        xc = sb("xc", [P, DC, GROUP])
        sz = sb("sz", [P, DC, GROUP])
        yg = sb("yg", [P, DC, GROUP])
        x_pad = sb("x_pad", [P, TILES, QUADS, 4, 32])
        bc = hf[:, 0:6, :].rearrange("p (s w) l -> p s w l", s=3)
        dec = sb("dec", [P, 4, TRI])
        sc = sb("sc", [P, 4, TRI])
        sp_a = hf[0:HEADS, 6, :]
        sp_b = hf[0:HEADS, 7, :]
        cumP = hf[0:HEADS, 5, :]
        mid0 = sb("mid0", [HEADS, GROUP], BF16)
        cum3 = sb("cum3", [96, SEQS, TRI], BF16)
        cum_tok = sb("cum_tok", [P, TILES, HEADS])
        sg = xc
        lg0 = sb("lg0", [P, TILES, EXPERTS0])
        mx = sb("mx", [P, TILES, 8])
        ix = sb("ix", [P, TILES, 8], U32)
        ixf = sb("ixf", [P, TILES, TOPK])
        oh0 = sb("oh0", [P, TILES, 2, EXPERTS0])
        wk = sb("wk", [P, TILES, TOPK])
        wsum = sb("wsum", [P, TILES])
        wm = sb("wm", [P, TILES, EXPERTS0])
        hw = yg[:, 0, :].rearrange("p (t j) -> p t j", t=TILES)
        hwT = yg[:, 1, :]
        qT = xc
        kT = [sz, yg]
        v_pad = sb("v_pad", [P, TILES, AHEADS // 2, 2, 32])
        nmax = sb("nmax", [P, 4, 2])
        esum = sb("esum", [P, 4, 2])
        pr = dec
        prT = sc
        oT = hf[:, 0:2, :]
        lgt = sb("lgt", [P, TILES, E1])
        biased = sb("biased", [P, TILES, E1])
        oh = hf[:, 4:6, :].rearrange("p a (b e) -> p (a b) e", e=E1).rearrange("p (t k) e -> p t k e", t=TILES)
        prod = hf[:, 6:8, :].rearrange("p a (b e) -> p (a b) e", e=E1).rearrange("p (t k) e -> p t k e", t=TILES)
        chosen = sb("chosen", [P, TILES, E1], BF16)
        before = sb("before", [P, TILES + 1, E1], BF16)
        lk = sb("lk", [P, TILES, TOPK])
        slot = sb("slot", [P, TILES, TOPK])
        over = sb("over", [P, TILES, TOPK])
        sidx = sb("sidx", [P, TILES * TOPK], U32)
        gidx = sb("gidx", [P, ROUNDS, TILES * TOPK], U32)
        wts = sb("wts", [P, ROUNDS, TILES * TOPK])

        plan = BankPlan(banks, full, drained)
        for j in range(2):
            plan.use(("T", "mix", j), j)
        for c in range(DC):
            plan.use(("Z", c), 2 + c)
        for c in range(DC):
            plan.use(("X", c), 4 + c)
        plan.use("dt", 0)
        for c in range(DC):
            plan.use(("Y", c), 6 + c)
        plan.use("cumT", 1)
        for c in range(DC):
            plan.use(("XT", c), 2 + c)
        uses = [(p, b, e) for p in range(PAIRS) for b in range(SEQS) for e in range(2)]
        for p in range(PAIRS):
            for w in range(2):
                plan.use(("BC", p, w), w)
        for p in range(PAIRS):
            for b in range(SEQS):
                for e in range(2):
                    plan.use(("A", p, b, e), 2 + e)
                    plan.use(("CB", p, b, e), 4 + e)
        for j in range(2):
            plan.use(("O", j), j)
        for j in range(2):
            plan.use(("T", "ffn", j), 2 + j)
        for f in range(FF // P):
            plan.use(("G", f), 4 + f % 2)
            plan.use(("U", f), f % 2)
        for j in range(2):
            plan.use(("F", j), 2 + j)
        for j in range(2):
            plan.use(("T", "lora", j), 4 + j)
        for t in range(TILES):
            plan.use(("L", t), t)
        plan.use("LT", 4)
        for j in range(2):
            plan.use(("T", "att", j), 6 + j)
        for c in range(DC):
            plan.use(("Q", c), c)
            plan.use(("K", c), 2 + c)
            plan.use(("V", c), 4 + c)
        for c in range(DC):
            plan.use(("OT", c), 6 + c)
        auses = [(h, b) for h0 in range(0, AHEADS, 4) for e in range(2) for b in range(SEQS)
                 for h in (h0 + e, h0 + 2 + e)]
        for n in range(len(auses)):
            plan.use(("S", n), n % 4)
            plan.use(("PT", n), 4 + n % 2)
        for j in range(2):
            plan.use(("W", j), j)
        for j in range(2):
            plan.use(("T", "moe", j), 2 + j)
        plan.use("R", 4)
        for f in range(SHF // P):
            plan.use(("SG", f), f % 2)
            plan.use(("SU", f), 6 + f % 2)
        for j in range(2):
            plan.use(("SD", j), 2 + j)
        plan.use("pos", 5)

        CREDIT = 16
        ALL = slice(0, TILES)
        H = [slice(0, 2), slice(2, 4)]
        POWERS = [H[0], H[1]] + 3 * [H[0], H[0], H[1], H[1]]
        consts_in = sem("consts_in")
        w_sem = {k: sem("in_" + k) for k in ("proj", "out", "ffn", "lora", "att", "moe")}
        pads_zero = sem("pads_zero")
        x_in = sem("x_in")
        x_free = signal("x_free", 2)
        var_ready = signal("var_ready", 16)
        rstd_ready = signal("rstd_ready", 16)
        u_ready = signal("u_ready", 10)
        tap0 = signal("tap0", 34)
        dt_abs = signal("dt_abs", 1)
        dt_log = signal("dt_log", 1)
        exp_dt = signal("exp_dt", 1)
        cum_ready = signal("cum_ready", 1)
        cum3_ready = signal("cum3_ready", 1)
        y_added = signal("y_added", 64)
        yg_ready = signal("yg_ready", DC)
        sumsq = signal("sumsq", TILES)
        gated = signal("gated", FF // P)
        hw_ready = signal("hw_ready", 1)
        lora_top = signal("lora_top", 1)
        lora_exp = signal("lora_exp", 1)
        lora_added = signal("lora_added", TILES)
        lora_lg = signal("lora_lg", TILES)
        k_even = signal("k_even", DC)
        nmax_ready = signal("nmax_ready", 32)
        exps = signal("exps", 32)
        probs = signal("probs", 32)
        o_added = signal("o_added", 32)
        sgated = signal("sgated", SHF // P)
        top_ready = signal("top_ready", 1)
        top_exp = signal("top_exp", 1)
        chosen_ready = signal("chosen_ready", 1)
        sidx_ready = signal("sidx_ready", 1)
        scattered = sem("scattered")
        xf_stored = sem("xf_stored")
        zero_filled = sem("zero_filled")
        chain = signal("dve_chain", 160)
        x3_ready = signal("x3_ready", 2)
        x2_ready = signal("x2_ready", 2)
        ahead_chain = signal("ahead_chain", 5)

        area = w_in[:, :, :].rearrange("p k n -> p (k n)")
        marks = [0]

        def carve(n):
            marks[0] += n
            return area[:, marks[0] - n:marks[0]]

        xg = [carve(D) for _ in range(2)]
        xgT = [carve(DC * P).rearrange("p (k s) -> p k s", k=DC) for _ in range(2)]
        egu = [carve(DC * EG * P).rearrange("p (k e j) -> p k e j", k=DC, e=EG) for _ in range(2)]
        edn = [carve(EG * D)[0:F1, :].rearrange("p (e d) -> p e d", e=EG) for _ in range(2)]
        esg = [carve(F1) for _ in range(2)]
        eh = [carve(F1) for _ in range(2)]
        ehT = [carve(P)[0:F1, :] for _ in range(2)]
        yt = [carve(D) for _ in range(2)]
        yk = [hf[:, 2 * s:2 * s + 2, :].rearrange("p a b -> p (a b)").rearrange("p (k d) -> p k d", k=TOPK)
              for s in range(2)]
        shx = [h1[:, 2 * s:2 * s + 2, :] for s in range(2)]
        acc = [tmp[:, s, :] for s in range(2)]
        ot = [tmp[:, 2 + s, :] for s in range(2)]
        gi = sb("gi", [P, 2, TOPK], U32)
        wt = sb("wt", [P, 2, TOPK])
        EROUNDS = EGROUPS // 2
        TWO = TOKENS // P // 2

        tail = BankPlan(banks, full, drained)
        tail.base = [ROUNDS * n for n in plan.count]
        for s in range(2):
            tail.use(("XG", s), s)
            tail.use(("GU", s), 2 + s)
            tail.use(("HT", s), 4 + s)
            tail.use(("YO", s), 6 + s)
        e_in = [sem(f"e_in{s}") for s in range(2)]
        e_silu = signal("e_silu", 2)
        y_out = [sem(f"y_out{s}") for s in range(2)]
        gi_ready = signal("gi_ready", 2)
        gathered = [sem(f"gathered{s}") for s in range(2)]
        shx_in = [sem(f"shx_in{s}") for s in range(2)]
        var2 = signal("var2", 2)
        rstd2 = signal("rstd2", 2)
        out_ready = signal("out_ready", 2)
        stored = [sem(f"stored{s}") for s in range(2)]
        chain2 = signal("dve_chain2", 14)

        def tail_sync(sp):
            sp.wait_ge(scattered, 16 * TILES * TOPK * ROUNDS + CREDIT)
            with sp.Fori(0, EROUNDS) as r:
                for s in range(2):
                    tail.wait_empty(sp, ("YO", s), r)
                    settle(sp)
                    g = 2 * r + s
                    sp.dma_start(xg[s], xg_dram[bass.ds(g * P, P), :]).then_inc(e_in[s], 16)
                    sp.dma_start(egu[s], A["w_egu"][:, :, bass.ds(g * EG, EG), :]).then_inc(e_in[s], 16)
                    sp.dma_start(edn[s], A["w_edn"][:, bass.ds(g * EG, EG), :]).then_inc(e_in[s], 16)
            sp.wait_ge(xf_stored, 32 * ROUNDS)
            with sp.Fori(0, TWO) as r:
                for s in range(2):
                    i = 2 * r + s
                    out_ready.wait(sp, r, 1)
                    settle(sp)
                    sp.wait_ge(stored[s], r * 16 + CREDIT)
                    settle(sp)
                    sp.dma_start(shx[s][:, 0, :], sh_dram[bass.ds(i * P, P), :]).then_inc(shx_in[s], 16)
                    sp.dma_start(shx[s][:, 1, :], x3_dram[bass.ds(i * P, P), :]).then_inc(shx_in[s], 16)
                for s in range(2):
                    i = 2 * r + s
                    out_ready.wait(sp, r, s + 2)
                    settle(sp)
                    sp.dma_start(out[bass.ds(i * P, P), :], ot[s]).then_inc(stored[s], 16)
            for s in range(2):
                sp.wait_ge(stored[s], 16 * TWO + CREDIT)

        def tail_tensor(pe):
            with pe.Fori(0, EROUNDS) as r:
                for s in range(2):
                    pe.wait_ge(e_in[s], r * 48 + 48)
                    tail.wait_empty(pe, ("XG", s), r)
                    for k in range(DC):
                        mm = pe.transpose(tail[("XG", s)][:, k * P:(k + 1) * P], xg[s][:, k * P:(k + 1) * P],
                                          ident[:, :])
                    tail.filled(mm, ("XG", s))
                for s in range(2):
                    tail.wait_drained(pe, ("XG", s), r)
                    tail.wait_empty(pe, ("GU", s), r)
                    for e in range(EG):
                        rows = slice(CAP * e, CAP * (e + 1))
                        for k in range(DC):
                            mm = pe.matmul(tail[("GU", s)][rows, 0:P], xgT[s][:, k, rows], egu[s][:, k, e, :],
                                           start=k == 0, stop=k == DC - 1)
                    tail.filled(mm, ("GU", s))
                for s in range(2):
                    tail.wait_drained(pe, ("GU", s), r)
                    tail.wait_empty(pe, ("HT", s), r)
                    settle(pe)
                    tail.filled(pe.transpose(tail[("HT", s)][0:F1, 0:P], eh[s], ident[:, :]), ("HT", s))
                for s in range(2):
                    tail.wait_drained(pe, ("HT", s), r)
                    tail.wait_empty(pe, ("YO", s), r)
                    settle(pe)
                    for e in range(EG):
                        rows = slice(CAP * e, CAP * (e + 1))
                        mm = pe.matmul(tail[("YO", s)][rows, 0:D], ehT[s][:, rows], edn[s][:, e, :],
                                       start=True, stop=True)
                    tail.filled(mm, ("YO", s))

        def tail_scalar(act):
            with act.Fori(0, EROUNDS) as r:
                for s in range(2):
                    tail.wait_full(act, ("XG", s), r)
                    tail.read(act.activation(xgT[s], tail[("XG", s)][:, 0:DC * P]
                                             .rearrange("p (k s) -> p k s", k=DC), ACT.Copy), ("XG", s))
                for s in range(2):
                    tail.wait_full(act, ("GU", s), r)
                    e_silu.after(act.activation(esg[s], tail[("GU", s)][:, 0:F1], ACT.Silu))
                for s in range(2):
                    tail.wait_full(act, ("HT", s), r)
                    tail.read(act.activation(ehT[s], tail[("HT", s)][0:F1, 0:P], ACT.Copy), ("HT", s))

        def tail_pool(pool):
            with pool.Fori(0, EROUNDS) as r:
                for s in range(2):
                    tail.wait_drained(pool, ("YO", s), r)
                    settle(pool)
                    pool.dma_start(y_dram[bass.ds((2 * r + s) * P, P), :], yt[s]).then_inc(y_out[s], 16)
            for s in range(2):
                pool.wait_ge(y_out[s], 16 * EROUNDS + CREDIT)
            with pool.Fori(0, TWO) as r:
                for s in range(2):
                    gi_ready.wait(pool, r, s + 1)
                    settle(pool)
                    for k in range(TOPK):
                        pool.indirect_dma_start(
                            out=yk[s][:, k, :], out_offset=None, in_=y_dram,
                            in_offset=bass.IndirectOffsetOnAxis(ap=gi[:, s, k:k + 1], axis=0))\
                            .then_inc(gathered[s], 16)
                for s in range(2):
                    var2.wait(pool, r, s + 1)
                    rstd2.after(pool.tensor_tensor(rs[:, s:s + 1], ve[:, s:s + 1], half[:, 0:1], ALU.pow))

        def tail_vector(dve):
            with dve.Fori(0, EROUNDS) as r:
                for s in range(2):
                    e_silu.wait(dve, r, s + 1)
                    tail.read(dve.tensor_tensor(eh[s], esg[s], tail[("GU", s)][:, F1:P], ALU.mult), ("GU", s))
                for s in range(2):
                    tail.wait_full(dve, ("YO", s), r)
                    dve.wait_ge(y_out[s], r * 16 + CREDIT)
                    tail.read(dve.tensor_copy(yt[s], tail[("YO", s)][:, 0:D]), ("YO", s))
            with dve.Fori(0, TWO) as r:
                count = [0]

                def link(ins):
                    count[0] += 1
                    chain2.after(ins)
                    chain2.wait(dve, r, count[0])

                idx = gidx[:, :, :].rearrange("p r k -> p (r k)")
                w = wts[:, :, :].rearrange("p r k -> p (r k)")
                for s in range(2):
                    dve.tensor_copy(wt[:, s, :], w[:, bass.ds((2 * r + s) * TOPK, TOPK)])
                    gi_ready.after(dve.tensor_copy(gi[:, s, :], idx[:, bass.ds((2 * r + s) * TOPK, TOPK)]))
                gi_ready.wait(dve, r, 2)
                for s in range(2):
                    dve.wait_ge(shx_in[s], r * 32 + 32)
                    dve.wait_ge(gathered[s], r * 64 + 64)
                    for k in range(TOPK):
                        link(dve.scalar_tensor_tensor(acc[s], yk[s][:, k, :], wt[:, s, k:k + 1],
                                                      shx[s][:, 0, :] if k == 0 else acc[s], ALU.mult, ALU.add))
                    link(dve.bn_stats(stats[:, s, :], acc[s]))
                    settle(dve)
                    link(dve.bn_aggr(mv[:, s, :], stats[:, s, :]))
                    var2.after(dve.tensor_scalar(ve[:, s:s + 1], mv[:, s, 1:2], EPS, None, ALU.add))
                for s in range(2):
                    rstd2.wait(dve, r, s + 1)
                    dve.wait_ge(stored[s], r * 16 + CREDIT)
                    link(dve.tensor_scalar(acc[s], acc[s], mv[:, s, 0:1], rs[:, s:s + 1], ALU.subtract,
                                           ALU.mult))
                    out_ready.after(dve.tensor_tensor(ot[s], shx[s][:, 1, :], acc[s], ALU.add))
            if count[0] != chain2.per:
                raise ValueError(f"dve_chain2 is raised {count[0]} times in a round")

        block = ctx.enter_context(nc.Block())

        def tok(r, n=GROUP, o=0):
            return bass.ds(r * GROUP + o, n)

        STORES = 2
        WSLOTS = 2



        @block.sync
        def _(sp):
            for b in drained:
                sp.sem_inc(b, 1)
            for free in stored:
                sp.sem_inc(free, CREDIT)
            sp.sem_inc(out_ready.sem, 1)
            sp.dma_start(xin[:, :, :], A["x"][0:GROUP, :].rearrange("(t p) d -> p t d", p=P)).then_inc(x_in, 16)
            for dst, name in ((ident[:, :], "ident"), (iota[:, :], "iota"), (parity[:, :], "parity"),
                              (cstage[:, 0, 0:TRI], "keyq_mask"), (cstage[:, 1, 0:TRI], "qkey_mask"),
                              (cstage[:, 0, TRI:512], "earlier"),
                              (neg_in[:, :], "neg_sel"),
                              (chan[:, :, :], "chan"), (conv_w[:, :, :], "conv_w"), (conv_b[:, :], "conv_b")):
                sp.dma_start(dst, A[name]).then_inc(consts_in, 16)
            sp.dma_start(w_in[:, :, :], A["w_in"]).then_inc(w_sem["proj"], 16)
            sp.dma_start(w_out[:, :, :], A["w_out"]).then_inc(w_sem["out"], 16)
            sp.dma_start(w_gu[:, :, :], A["w_gu"]).then_inc(w_sem["ffn"], 16)
            sp.dma_start(w_dn[:, :, :], A["w_dn"]).then_inc(w_sem["ffn"], 16)
            sp.dma_start(w_lora[:, :, :], A["w_lora"]).then_inc(w_sem["lora"], 16)
            sp.dma_start(w_lb[:, :], A["w_lb"]).then_inc(w_sem["lora"], 16)
            sp.dma_start(w_att[:, :, :, :], A["w_att"]).then_inc(w_sem["att"], 16)
            sp.dma_start(att_rows[:, :, :], A["att_rows"].broadcast_to([P, 2, D])).then_inc(w_sem["att"], 16)
            sp.dma_start(w_rt[:, :, :], A["w_rt"]).then_inc(w_sem["moe"], 16)
            sp.dma_start(rt_bias[:, :], A["rt_bias"].broadcast_to([P, E1])).then_inc(w_sem["moe"], 16)
            sp.dma_start(w_sgu[:, :, :], A["w_sgu"]).then_inc(w_sem["moe"], 16)
            sp.dma_start(w_sdn[:, :, :], A["w_sdn"]).then_inc(w_sem["moe"], 16)
            sp.wait_ge(pads_zero, 5)
            for g in range(SLOTS // GROUP - 1):
                sp.dma_start(xg_dram[g * GROUP:(g + 1) * GROUP, :].rearrange("(t p) d -> p t d", p=P),
                             tmp[:, :, :]).then_inc(zero_filled, 16)
            with sp.Fori(0, ROUNDS - 1) as r:
                x_free.wait(sp, r, 2)
                settle(sp)
                sp.dma_start(xin[:, :, :], A["x"][bass.ds(r * GROUP + GROUP, GROUP), :]
                             .rearrange("(t p) d -> p t d", p=P)).then_inc(x_in, 16)
            x_free.wait(sp, ROUNDS - 1, 2)
            sp.dma_start(xin[:, :, :], A["x"][0:GROUP, :].rearrange("(t p) d -> p t d", p=P)).then_inc(x_in, 16)
            sp.wait_ge(x_in, 16 * (ROUNDS + 1))
            tail_sync(sp)

        def transposes(pe, stage, n, src, j, r):
            key = ("T", stage, j)
            u_ready.wait(pe, r, 2 * n - 1 + j)
            plan.wait_empty(pe, key, r)
            for c in range(DC):
                for i in range(2):
                    mm = pe.transpose(plan[key][:, c * HALF + i * P:c * HALF + (i + 1) * P],
                                      src[:, 2 * j + i, c * P:(c + 1) * P], ident[:, :])
            plan.filled(mm, key)

        def linear(pe, key, w, cols, r):
            plan.wait_empty(pe, key, r)
            n = cols.stop - cols.start
            for k in range(DC):
                mm = pe.matmul(plan[key][0:n, :], w[:, k, cols], uT[:, k, :], start=k == 0, stop=k == DC - 1)
            plan.filled(mm, key)

        def head_of(p, e):
            return 4 * (2 * (p // 4) + e) + p % 4

        def head_rows(h):
            return slice(32 * (h // 2 % 4), 32 * (h // 2 % 4) + 32)

        @block.tensor
        def _(pe):
            pe.wait_ge(consts_cast, 1)
            pe.wait_ge(w_sem["proj"], 16)
            with pe.Fori(0, ROUNDS) as r:
                for j in range(2):
                    transposes(pe, "mix", 1, u, j, r)
                for j in range(2):
                    plan.wait_drained(pe, ("T", "mix", j), r)
                for c in range(DC):
                    linear(pe, ("Z", c), w_in, slice(c * P, (c + 1) * P), r)
                for c in range(DC):
                    linear(pe, ("X", c), w_in, slice(D + c * P, D + (c + 1) * P), r)
                linear(pe, "dt", w_in, slice(PROJ - HEADS, PROJ), r)

                def project_bc(p, w):
                    o = 2 * D + w * HEADS * STATE + p * P
                    linear(pe, ("BC", p, w), w_in, slice(o, o + P), r)

                for c in range(DC):
                    plan.wait_empty(pe, ("Y", c), r)
                    plan.filled(pe.matmul(plan[("Y", c)][:, :], zeros_bf[:, 0:P], zeros_bf[:, :], start=True,
                                          stop=False, skip_group_check=True), ("Y", c))
                cum_ready.wait(pe, r, 1)
                plan.wait_empty(pe, "cumT", r)
                settle(pe)
                for t in range(TILES):
                    mm = pe.transpose(plan["cumT"][:, t * HEADS:(t + 1) * HEADS],
                                      cumP[:, t * P:(t + 1) * P], ident[0:HEADS, 0:HEADS])
                plan.filled(mm, "cumT")
                for w in range(2):
                    project_bc(0, w)
                for c in range(DC):
                    plan.wait_drained(pe, ("X", c), r)
                    plan.wait_empty(pe, ("XT", c), r)
                    for t in range(TILES):
                        mm = pe.transpose(plan[("XT", c)][:, t * P:(t + 1) * P],
                                          xc[:, c, t * P:(t + 1) * P], ident[:, :])
                    plan.filled(mm, ("XT", c))
                for c in range(DC):
                    plan.wait_drained(pe, ("XT", c), r)
                cum3_ready.wait(pe, r, 1)
                for w in range(2):
                    project_bc(1, w)

                def decays(n):
                    p, b, e = uses[n]
                    key = ("A", p, b, e)
                    plan.wait_empty(pe, key, r)
                    pe.matmul(plan[key][:, 0:TRI], ident_bf[:, :], keyq_mask[:, :], start=True, stop=False)
                    h = head_of(p, e)
                    plan.filled(pe.matmul(plan[key][:, 0:TRI], neg_sel[:, h:h + 1].broadcast_to([96, P]),
                                          cum3[:, b, :], start=False, stop=True), key)

                def products(n):
                    p, b, e = uses[n]
                    key = ("CB", p, b, e)
                    rows = slice(e * STATE, (e + 1) * STATE)
                    B, C = bc[rows, p % 3, 0, :], bc[rows, p % 3, 1, :]
                    o = b * SEQ
                    pe.matmul(plan[key][:, 0:SEQ], B[:, o:o + P], C[:, o:o + SEQ], start=True, stop=True)
                    return key, lambda: pe.matmul(plan[key][:, SEQ:TRI], B[:, o + P:o + SEQ],
                                                  C[:, o + P:o + SEQ], start=True, stop=True)

                def add_y(ns):
                    for n in ns:
                        plan.wait_drained(pe, ("CB", *uses[n]), r)
                    for i in range(2):
                        for n in ns:
                            p, b, e = uses[n]
                            q, hq = divmod(head_of(p, e), 4)
                            y = plan[("Y", q // 4)][32 * (q % 4):32 * (q % 4) + 32, :]
                            s = sc[:, n % 4, :]
                            o = b * SEQ
                            if i == 0:
                                pe.matmul(y[:, o:o + SEQ], x_pad[:, 2 * b, q, hq, :], s[:, 0:SEQ],
                                          start=False, stop=False, skip_group_check=True)
                            else:
                                y_added.after(pe.matmul(y[:, o + P:o + SEQ], x_pad[:, 2 * b + 1, q, hq, :],
                                                        s[:, SEQ:TRI], start=False, stop=True,
                                                        skip_group_check=True))

                for g in range(2 * PAIRS):
                    p, b = divmod(g, SEQS)
                    ns = (2 * g, 2 * g + 1)
                    for n in ns:
                        decays(n)
                    if b == 0:
                        for w in range(2):
                            plan.wait_drained(pe, ("BC", p, w), r)
                    for n in ns:
                        plan.wait_empty(pe, ("CB", *uses[n]), r)
                    for key, second in [products(n) for n in ns]:
                        plan.filled(second(), key)
                    if p + 2 < PAIRS:
                        project_bc(p + 2, b)
                    if g >= 1:
                        add_y((2 * g - 2, 2 * g - 1))
                add_y((62, 63))

                pe.wait_ge(w_sem["out"], 16)
                for c in range(DC):
                    yg_ready.wait(pe, r, c + 1)
                for j in range(2):
                    plan.wait_empty(pe, ("O", j), r)
                    for i in range(2):
                        t = 2 * j + i
                        for c in range(DC):
                            mm = pe.matmul(plan[("O", j)][:, i * D:(i + 1) * D], yg[:, c, t * P:(t + 1) * P],
                                           w_out[:, c, :], start=c == 0, stop=c == DC - 1)
                    plan.filled(mm, ("O", j))

                for j in range(2):
                    transposes(pe, "ffn", 2, u, j, r)
                for j in range(2):
                    plan.wait_drained(pe, ("T", "ffn", j), r)
                pe.wait_ge(w_sem["ffn"], 32)
                for f in range(FF // P):
                    linear(pe, ("G", f), w_gu, slice(f * P, (f + 1) * P), r)
                    linear(pe, ("U", f), w_gu, slice(FF + f * P, FF + (f + 1) * P), r)
                for f in range(FF // P - 2, FF // P):
                    plan.wait_drained(pe, ("U", f), r)
                for j in range(2):
                    plan.wait_empty(pe, ("F", j), r)
                    for i in range(2):
                        t = 2 * j + i
                        for f in range(FF // P):
                            mm = pe.matmul(plan[("F", j)][:, i * D:(i + 1) * D], hf[:, f, t * P:(t + 1) * P],
                                           w_dn[:, f, :], start=f == 0, stop=f == FF // P - 1)
                    plan.filled(mm, ("F", j))

                pe.wait_ge(w_sem["lora"], 32)
                for j in range(2):
                    transposes(pe, "lora", 3, u, j, r)
                    plan.wait_drained(pe, ("T", "lora", j), r)
                    for t in (2 * j, 2 * j + 1):
                        plan.wait_empty(pe, ("L", t), r)
                        for k in range(DC):
                            mm = pe.matmul(plan[("L", t)][:, 0:LW], uT[:, k, t * P:(t + 1) * P],
                                           w_lora[:, k, :], start=k == 0, stop=k == DC - 1)
                        plan.filled(mm, ("L", t))
                hw_ready.wait(pe, r, 1)
                plan.wait_empty(pe, "LT", r)
                for t in range(TILES):
                    mm = pe.transpose(plan["LT"][:, t * P:(t + 1) * P], hw[:, t, :], ident[:, :])
                plan.filled(mm, "LT")
                plan.wait_drained(pe, "LT", r)
                for t in range(TILES):
                    lora_added.after(pe.matmul(plan[("L", t)][:, 0:D], hwT[:, t * P:(t + 1) * P], w_lb[:, :],
                                               start=False, stop=True, skip_group_check=True))

                pe.wait_ge(w_sem["att"], 32)
                for j in range(2):
                    transposes(pe, "att", 4, u, j, r)
                    plan.wait_drained(pe, ("T", "att", j), r)
                    cols = slice(j * HALF, (j + 1) * HALF)
                    for c in range(DC):
                        for n, key in enumerate((("Q", c), ("K", c))):
                            if j == 0:
                                plan.wait_empty(pe, key, r)
                            for k in range(DC):
                                mm = pe.matmul(plan[key][:, cols], w_att[:, k, n, c * P:(c + 1) * P],
                                               uT[:, k, cols], start=k == 0, stop=k == DC - 1)
                            if j == 1:
                                plan.filled(mm, key)
                    plan.wait_empty(pe, ("V", j), r)
                    for i in range(2):
                        t = 2 * j + i
                        for k in range(DC):
                            mm = pe.matmul(plan[("V", j)][:, i * D:(i + 1) * D], uT[:, k, t * P:(t + 1) * P],
                                           w_att[:, k, 2, :], start=k == 0, stop=k == DC - 1)
                    plan.filled(mm, ("V", j))
                for c in range(DC):
                    plan.wait_empty(pe, ("OT", c), r)
                    plan.filled(pe.matmul(plan[("OT", c)][:, :], zeros_bf[:, 0:P], zeros_bf[:, :], start=True,
                                          stop=False, skip_group_check=True), ("OT", c))
                for c in range(DC):
                    plan.wait_drained(pe, ("Q", c), r)
                    plan.wait_drained(pe, ("K", c), r)
                    plan.wait_drained(pe, ("V", c), r)

                def scores(ns):
                    for n in ns:
                        plan.wait_empty(pe, ("S", n), r)
                        pe.matmul(plan[("S", n)][:, 0:TRI], ident_bf[:, :], qkey_mask[:, :], start=True,
                                  stop=False, skip_group_check=True)
                    for i in range(2):
                        for n in ns:
                            h, b = auses[n]
                            rows, o = head_rows(h), b * SEQ
                            q = qT[rows, h // 8, o:o + SEQ]
                            k = kT[h % 2][rows, h // 8, o:o + SEQ]
                            if i == 0:
                                pe.matmul(plan[("S", n)][:, 0:P], q[:, 0:P], k[:, 0:P], start=False,
                                          stop=True, skip_group_check=True)
                            else:
                                plan.filled(pe.matmul(plan[("S", n)][:, P:TRI], q[:, P:SEQ], k[:, 0:SEQ],
                                                      start=False, stop=True, skip_group_check=True),
                                            ("S", n))

                def turn_probs(n):
                    key = ("PT", n)
                    plan.wait_empty(pe, key, r)
                    probs.wait(pe, r, n + 1)
                    for i in range(3):
                        mm = pe.transpose(plan[key][:, i * P:(i + 1) * P], pr[:, n % 4, i * P:(i + 1) * P],
                                          ident[:, :])
                    plan.filled(mm, key)

                def add_o(ns):
                    for n in ns:
                        plan.wait_drained(pe, ("PT", n), r)
                    for i in range(2):
                        for n in ns:
                            h, b = auses[n]
                            o = plan[("OT", h // 8)][head_rows(h), :]
                            s = prT[:, n % 4, :]
                            if i == 0:
                                pe.matmul(o[:, b * SEQ:(b + 1) * SEQ], v_pad[:, 2 * b, h // 2, h % 2, :],
                                          s[:, 0:SEQ], start=False, stop=False, skip_group_check=True)
                            else:
                                o_added.after(pe.matmul(o[:, b * SEQ + P:(b + 1) * SEQ],
                                                        v_pad[:, 2 * b + 1, h // 2, h % 2, :], s[:, SEQ:TRI],
                                                        start=False, stop=True, skip_group_check=True))

                for g in range(16 + 2):
                    if g < 16:
                        scores((2 * g, 2 * g + 1))
                    if 1 <= g < 17:
                        turn_probs(2 * g - 2)
                        turn_probs(2 * g - 1)
                    if 2 <= g:
                        add_o((2 * g - 4, 2 * g - 3))
                for c in range(DC):
                    plan.wait_drained(pe, ("OT", c), r)
                for j in range(2):
                    plan.wait_empty(pe, ("W", j), r)
                    for i in range(2):
                        t = 2 * j + i
                        for c in range(DC):
                            mm = pe.matmul(plan[("W", j)][:, i * D:(i + 1) * D], oT[:, c, t * P:(t + 1) * P],
                                           w_att[:, c, 3, :], start=c == 0, stop=c == DC - 1)
                    plan.filled(mm, ("W", j))

                pe.wait_ge(w_sem["moe"], 64)
                plan.wait_empty(pe, "R", r)
                for j in range(2):
                    transposes(pe, "moe", 5, xf, j, r)
                    plan.wait_drained(pe, ("T", "moe", j), r)
                    for t in (2 * j, 2 * j + 1):
                        for k in range(DC):
                            mm = pe.matmul(plan["R"][:, t * E1:(t + 1) * E1], uT[:, k, t * P:(t + 1) * P],
                                           w_rt[:, k, :], start=k == 0, stop=k == DC - 1)
                plan.filled(mm, "R")
                for f in range(SHF // P):
                    linear(pe, ("SG", f), w_sgu, slice(f * P, (f + 1) * P), r)
                    linear(pe, ("SU", f), w_sgu, slice(SHF + f * P, SHF + (f + 1) * P), r)
                for f in range(SHF // P - 2, SHF // P):
                    plan.wait_drained(pe, ("SU", f), r)
                for j in range(2):
                    plan.wait_empty(pe, ("SD", j), r)
                    for i in range(2):
                        t = 2 * j + i
                        for f in range(SHF // P):
                            mm = pe.matmul(plan[("SD", j)][:, i * D:(i + 1) * D], hf[:, f, t * P:(t + 1) * P],
                                           w_sdn[:, f, :], start=f == 0, stop=f == SHF // P - 1)
                    plan.filled(mm, ("SD", j))
                chosen_ready.wait(pe, r, 1)
                plan.wait_empty(pe, "pos", r)
                for t in range(TILES):
                    pe.matmul(plan["pos"][:, t * E1:(t + 1) * E1], earlier[:, :], chosen[:, t, :],
                              start=True, stop=False)
                    mm = pe.matmul(plan["pos"][:, t * E1:(t + 1) * E1], ones_bf[:, :], before[:, t, :],
                                   start=False, stop=True)
                plan.filled(mm, "pos")
            tail_tensor(pe)

        @block.scalar
        def _(act):
            act.wait_ge(consts_cast, 1)
            with act.Fori(0, ROUNDS) as r:
                def turned(stage, j, scale=None):
                    key = ("T", stage, j)
                    plan.wait_full(act, key, r)
                    cols = slice(j * HALF, (j + 1) * HALF)
                    if scale is None:
                        ins = act.activation(uT[:, :, cols], plan[key][:, :]
                                             .rearrange("p (c n) -> p c n", c=DC), ACT.Copy)
                    else:
                        for c in range(DC):
                            ins = act.activation(uT[:, c, cols], plan[key][:, c * HALF:(c + 1) * HALF],
                                                 ACT.Copy, scale=chan[:, c, scale:scale + 1])
                    plan.read(ins, key)

                def first_tap(key, dst, j):
                    plan.wait_full(act, key, r)
                    tap0.after(act.activation(dst, plan[key][:, :], ACT.Identity, bias=conv_b[:, j:j + 1],
                                              scale=conv_w[:, j, TAPS - 1:TAPS]))

                for j in range(2):
                    turned("mix", j, 2)
                for c in range(DC):
                    key = ("Z", c)
                    plan.wait_full(act, key, r)
                    plan.read(act.activation(sz[:, c, :], plan[key][:, :], ACT.Silu, bias=chan[:, c, 0:1]), key)
                for c in range(DC):
                    first_tap(("X", c), xc[:, c, :], c)
                plan.wait_full(act, "dt", r)
                dt_abs.after(act.activation(sp_a[:, :], plan["dt"][0:HEADS, :], ACT.Abs))
                dt_abs.wait(act, r, 1)
                exp_dt.after(act.activation(sp_b[:, :], sp_a[:, :], ACT.Exp, scale=-1.0))
                exp_dt.wait(act, r, 1)
                dt_log.after(act.activation(sp_a[:, :], sp_b[:, :], ACT.Ln, bias=1.0))
                plan.wait_full(act, "cumT", r)
                plan.read(act.activation(cum_tok[:, :, :], plan["cumT"][:, 0:TILES * HEADS]
                                         .rearrange("p (t h) -> p t h", t=TILES), ACT.Copy), "cumT")
                for w in range(2):
                    first_tap(("BC", 0, w), bc[:, 0, w, :], 2 + 16 * w)
                for w in range(2):
                    first_tap(("BC", 1, w), bc[:, 1, w, :], 3 + 16 * w)
                plan.wait_drained(act, "cumT", r)
                for p in range(PAIRS):
                    for i in range(4):
                        n = 4 * p + i
                        _, b, e = uses[n]
                        h = head_of(p, e)
                        key = ("A", p, b, e)
                        plan.wait_full(act, key, r)
                        if n >= 4:
                            plan.wait_drained(act, ("CB", *uses[n - 4]), r)
                        act.activation(dec[:, n % 4, 0:SEQ], plan[key][:, 0:SEQ], ACT.Exp,
                                       bias=cum_tok[:, 2 * b, h:h + 1])
                        plan.read(act.activation(dec[:, n % 4, SEQ:TRI], plan[key][:, SEQ:TRI], ACT.Exp,
                                                 bias=cum_tok[:, 2 * b + 1, h:h + 1]), key)
                        if e == 1 and p + 2 < PAIRS:
                            first_tap(("BC", p + 2, b), bc[:, (p + 2) % 3, b, :], 2 + 16 * b + p + 2)
                for t in range(TILES):
                    if t % 2 == 0:
                        plan.wait_drained(act, ("O", t // 2), r)
                    sumsq.after(act.activation(tmp[:, t, :], h1[:, t, :], ACT.Square, scale=1.0 / 16,
                                               accum_out=sm[:, t:t + 1]))
                for j in range(2):
                    turned("ffn", j, 3)

                def silu_gate(gk, uk, f):
                    plan.wait_full(act, (gk, f), r)
                    if f >= 2:
                        plan.wait_drained(act, (uk, f - 2), r)
                    plan.read(act.activation(sg[:, f % 2, :], plan[(gk, f)][:, :], ACT.Silu), (gk, f))

                for f in range(FF // P):
                    silu_gate("G", "U", f)
                for j in range(2):
                    turned("lora", j)
                    for t in (2 * j, 2 * j + 1):
                        plan.wait_full(act, ("L", t), r)
                        lora_lg.after(act.activation(lg0[:, t, :], plan[("L", t)][:, D:D + EXPERTS0], ACT.Copy))
                lora_top.wait(act, r, 1)
                lora_exp.after(act.activation(wk[:, :, 0:2], wk[:, :, 0:2], ACT.Exp))
                plan.wait_full(act, "LT", r)
                plan.read(act.activation(hwT, plan["LT"][:, :], ACT.Copy), "LT")
                for j in range(2):
                    turned("att", j)
                for c in range(DC):
                    plan.wait_full(act, ("Q", c), r)
                    plan.read(act.activation(qT[:, c, :], plan[("Q", c)][:, :], ACT.Identity,
                                             bias=qbias[:, c:c + 1], scale=0.25), ("Q", c))
                    plan.wait_full(act, ("K", c), r)
                    act.activation(kT[0][:, c, :], plan[("K", c)][:, :], ACT.Identity,
                                   bias=kbias[:, c, 0:1], scale=parity[:, 0:1])
                    plan.read(act.activation(kT[1][:, c, :], plan[("K", c)][:, :], ACT.Identity,
                                             bias=kbias[:, c, 1:2], scale=parity[:, 1:2]), ("K", c))
                for n in range(32 + 2):
                    if n < 32:
                        nmax_ready.wait(act, r, n + 1)
                        if n >= 4:
                            plan.wait_full(act, ("PT", n - 4), r)
                        for i, cols in enumerate((slice(0, P), slice(P, TRI))):
                            ins = act.activation(pr[:, n % 4, cols], plan[("S", n)][:, cols], ACT.Exp,
                                                 bias=nmax[:, n % 4, i:i + 1], accum_out=esum[:, n % 4, i:i + 1])
                        plan.read(ins, ("S", n))
                    if n >= 2:
                        m = n - 2
                        plan.wait_full(act, ("PT", m), r)
                        if m >= 4:
                            o_added.wait(act, r, m - 3)
                        plan.read(act.activation(prT[:, m % 4, :], plan[("PT", m)][:, 0:TRI], ACT.Copy),
                                  ("PT", m))
                for c in range(DC):
                    o_added.wait(act, r, 16 * (c + 1))
                    plan.read(act.activation(oT[:, c, :], plan[("OT", c)][:, :], ACT.Copy), ("OT", c))
                for j in range(2):
                    turned("moe", j)
                for f in range(SHF // P):
                    silu_gate("SG", "SU", f)
                top_ready.wait(act, r, 1)
                top_exp.after(act.activation(wk[:, :, :], lk[:, :, :], ACT.Exp))
            tail_scalar(act)

        @block.gpsimd
        def _(pool):
            pool.memset(half[:, :], -0.5).then_inc(pads_zero, 1)
            pool.memset(tmp[:, :, :], 0.0).then_inc(pads_zero, 1)
            pool.memset(x_pad[:, :, :, :, :], 0.0).then_inc(pads_zero, 1)
            pool.memset(v_pad[:, :, :, :, :], 0.0).then_inc(pads_zero, 1)
            pool.memset(before[:, :, :], 0.0).then_inc(pads_zero, 1)
            pool.wait_ge(pads_zero, 5)
            pool.dma_start(xg_dram[SLOTS - GROUP:SLOTS, :].rearrange("(t p) d -> p t d", p=P),
                           tmp[:, :, :]).then_inc(scattered, CREDIT)
            for s in range(2):
                pool.dma_start(y_dram[SLOTS + s * (P // 2):SLOTS + (s + 1) * (P // 2), :],
                               tmp[0:P // 2, 0, :]).then_inc(y_out[s], CREDIT)
            pool.wait_ge(zero_filled, 16 * (SLOTS // GROUP - 1))
            for zeroed in (scattered, *y_out):
                pool.wait_ge(zeroed, CREDIT)
            def power(n, cols, r):
                var_ready.wait(pool, r, n)
                rstd_ready.after(pool.tensor_tensor(rs[:, cols], ve[:, cols], half[:, cols], ALU.pow))

            for n in (1, 2):
                power(n, ALL, 0)
            with pool.Fori(0, ROUNDS) as r:
                for n, cols in enumerate(POWERS):
                    power(n + 3, cols, r)
                    if n == len(POWERS) - 1:
                        for j in range(2):
                            x3_ready.wait(pool, r, j + 1)
                        settle(pool)
                        pool.dma_start(x3_dram[tok(r), :].rearrange("(t p) d -> p t d", p=P),
                                       x1[:, :, :]).then_inc(xf_stored, 16)
                for n in (1, 2):
                    power(n, ALL, r + 1)
                sidx_ready.wait(pool, r, 1)
                settle(pool)
                for i in range(TILES * TOPK):
                    pool.indirect_dma_start(
                        out=xg_dram, out_offset=bass.IndirectOffsetOnAxis(ap=sidx[:, i:i + 1], axis=0),
                        in_=xf[:, i // TOPK, :], in_offset=None, bounds_check=SLOTS - 1,
                        oob_is_err=False).then_inc(scattered, 16)
                for j in range(2):
                    plan.wait_drained(pool, ("SD", j), r)
                settle(pool)
                pool.dma_start(sh_dram[tok(r), :].rearrange("(t p) d -> p t d", p=P),
                               tmp[:, :, :]).then_inc(xf_stored, 16)
            tail_pool(pool)

        @block.vector
        def _(dve):
            dve.wait_ge(pads_zero, 5)
            dve.wait_ge(consts_in, 160)
            dve.tensor_copy(ident_bf[:, :], ident[:, :])
            dve.tensor_copy(keyq_mask[:, :], cstage[:, 0, 0:TRI])
            dve.tensor_copy(qkey_mask[:, :], cstage[:, 1, 0:TRI])
            dve.tensor_copy(earlier[:, :], cstage[:, 0, TRI:512])
            dve.memset(ones_bf[:, :], 1.0)
            dve.memset(zeros_bf[:, :], 0.0)
            dve.memset(ones[:, :], 1.0)
            dve.tensor_copy(neg_sel[:, :], neg_in[:, :])
            for c in range(DC):
                for e in range(2):
                    dve.tensor_tensor(kbias[:, c, e:e + 1], chan[:, c, 5:6], parity[:, e:e + 1], ALU.mult)
                dve.tensor_scalar(qbias[:, c:c + 1], chan[:, c, 4:5], 0.25, None, ALU.mult)
            dve.memset(stats[:, 0, 0:1], 0.0).then_inc(consts_cast, 1)
            dve.wait_ge(consts_cast, 1)
            for zeroed, n in ((zero_filled, 16 * (SLOTS // GROUP - 1)), (scattered, CREDIT),
                              (y_out[0], CREDIT), (y_out[1], CREDIT)):
                dve.wait_ge(zeroed, n)

            def ask_power(variance, cols, n, r):
                var_ready.after(dve.tensor_scalar(ve[:, cols], variance, EPS, None, ALU.add))
                rstd_ready.wait(dve, r, n)

            def first_norms(r):
                links = [0]

                def link(ins):
                    links[0] += 1
                    ahead_chain.after(ins)
                    ahead_chain.wait(dve, r, links[0])

                dve.wait_ge(x_in, r * 16 + 16)
                for t in range(TILES):
                    ins = dve.bn_stats(stats[:, t, :], xin[:, t, :])
                link(ins)
                settle(dve)
                for t in range(TILES):
                    ins = dve.bn_aggr(mv[:, t, :], stats[:, t, :])
                link(ins)
                ask_power(mv[:, :, 1], ALL, 1, r)
                link(dve.tensor_copy(r1[:, :], rs[:, :]))
                link(dve.tensor_tensor(sm[:, :], mv[:, :, 1], r1[:, :], ALU.mult))
                for t in range(TILES):
                    dve.tensor_scalar(hn[:, t, :], xin[:, t, :], mv[:, t, 0:1], r1[:, t:t + 1],
                                      ALU.subtract, ALU.mult)
                link(dve.tensor_tensor(sm[:, :], sm[:, :], r1[:, :], ALU.mult))
                ask_power(sm[:, :], ALL, 2, r)
                for t in range(TILES):
                    ins = dve.tensor_scalar(u[:, t, :], hn[:, t, :], rs[:, t:t + 1], None, ALU.mult)
                    if t % 2:
                        u_ready.after(ins)

            first_norms(0)
            with dve.Fori(0, ROUNDS) as r:
                count = [0]

                def link(ins):
                    count[0] += 1
                    chain.after(ins)
                    chain.wait(dve, r, count[0])

                norms = [2]

                def inv_std(variance, cols):
                    norms[0] += 1
                    ask_power(variance, cols, norms[0], r)

                def moments(srcs, cols):
                    for t, s in zip(range(cols.start, cols.stop), srcs):
                        ins = dve.bn_stats(stats[:, t, :], s)
                    link(ins)
                    settle(dve)
                    for t in range(cols.start, cols.stop):
                        ins = dve.bn_aggr(mv[:, t, :], stats[:, t, :])
                    link(ins)

                def norm(srcs, dst, cols):
                    moments(srcs, cols)
                    inv_std(mv[:, cols, 1], cols)
                    for t, s in zip(range(cols.start, cols.stop), srcs):
                        ins = dve.tensor_scalar(dst[:, t, :], s, mv[:, t, 0:1], rs[:, t:t + 1],
                                                ALU.subtract, ALU.mult)
                    return ins

                def tiles(x, cols):
                    return [x[:, t, :] for t in range(cols.start, cols.stop)]

                taps_done = [0]

                def tap(s, chunks):
                    for n, (key, dst, j) in enumerate(chunks):
                        if s == 1:
                            taps_done[0] += 1
                            tap0.wait(dve, r, taps_done[0])
                        else:
                            chain.wait(dve, r, last_tap[0])
                    for n, (key, dst, j) in enumerate(chunks):
                        d = dst.rearrange("p (b l) -> p b l", b=SEQS)[:, :, s:SEQ]
                        x = plan[key][:, :].rearrange("p (b l) -> p b l", b=SEQS)[:, :, 0:SEQ - s]
                        ins = dve.scalar_tensor_tensor(d, x, conv_w[:, j, TAPS - 1 - s:TAPS - s], d,
                                                       ALU.mult, ALU.add)
                        if s < TAPS - 1:
                            chain.after(ins)
                            count[0] += 1
                            last_tap[0] = count[0]
                        else:
                            plan.read(ins, key)

                last_tap = [0]

                def bc_chunk(p, w):
                    return (("BC", p, w), bc[:, p % 3, w, :], 2 + 16 * w + p)

                for s in range(1, TAPS):
                    tap(s, [(("X", c), xc[:, c, :], c) for c in range(DC)])
                plan.wait_full(dve, "dt", r)
                dt = plan["dt"][0:HEADS, :]
                dt_log.wait(dve, r, 1)
                plan.read(dve.scalar_tensor_tensor(sp_b[:, :], dt, 0.0, sp_a[:, :], ALU.max, ALU.add), "dt")
                plan.wait_drained(dve, "dt", r)
                for b in range(SEQS):
                    ins = dve.tensor_tensor_scan(cumP[:, b * SEQ:(b + 1) * SEQ], ones[0:HEADS, :],
                                                 sp_b[:, b * SEQ:(b + 1) * SEQ], 0.0, ALU.mult, ALU.add)
                cum_ready.after(ins)
                cum_ready.wait(dve, r, 1)
                by_seq = cumP[:, :].rearrange("p (b l) -> p b l", b=SEQS)
                rest = sp_a[:, :].rearrange("p (b l) -> p b l", b=SEQS)
                mid = mid0[:, :].rearrange("p (b l) -> p b l", b=SEQS)
                link(dve.tensor_copy(cum3[0:HEADS, :, 0:SEQ], by_seq))
                link(dve.tensor_tensor(rest, by_seq, cum3[0:HEADS, :, 0:SEQ], ALU.subtract))
                link(dve.tensor_copy(mid, rest))
                dve.tensor_copy(cum3[HEADS:2 * HEADS, :, 0:SEQ], mid)
                link(dve.tensor_tensor(rest, rest, mid, ALU.subtract))
                link(dve.tensor_copy(cum3[2 * HEADS:96, :, 0:SEQ], rest))
                cum3_ready.after(dve.tensor_copy(cum3[:, :, SEQ:TRI], cum3[:, :, P:SEQ]))
                for s in range(1, TAPS):
                    tap(s, [bc_chunk(0, w) for w in range(2)])
                for c in range(DC):
                    plan.wait_full(dve, ("XT", c), r)
                    src = plan[("XT", c)][:, :].rearrange("p (t q h d) -> p t q h d", t=TILES, q=4, h=4)
                    for t in range(TILES):
                        for hq in range(4):
                            ins = dve.tensor_copy(x_pad[:, t, 4 * c:4 * c + 4, hq, 8 * hq:8 * hq + 8],
                                                  src[:, t, :, hq, :])
                    plan.read(ins, ("XT", c))
                for s in range(1, TAPS):
                    tap(s, [bc_chunk(1, w) for w in range(2)])
                for n in range(4 * PAIRS):
                    p, b, e = uses[n]
                    key = ("CB", p, b, e)
                    plan.wait_drained(dve, ("A", p, b, e), r)
                    plan.wait_full(dve, key, r)
                    if n >= 4:
                        y_added.wait(dve, r, n - 3)
                    plan.read(dve.tensor_tensor(sc[:, n % 4, :], dec[:, n % 4, :], plan[key][:, 0:TRI],
                                                ALU.mult), key)
                    if n >= 1 and uses[n - 1][2] == 1 and uses[n - 1][0] + 2 < PAIRS:
                        tap(2, [bc_chunk(uses[n - 1][0] + 2, uses[n - 1][1])])
                        tap(3, [bc_chunk(uses[n - 1][0] + 2, uses[n - 1][1])])
                    if e == 1 and p + 2 < PAIRS:
                        tap(1, [bc_chunk(p + 2, b)])
                for c in range(DC):
                    y_added.wait(dve, r, 32 * (c + 1))
                    plan.read(dve.scalar_tensor_tensor(yg[:, c, :], xc[:, c, :], chan[:, c, 1:2],
                                                       plan[("Y", c)][:, :], ALU.mult, ALU.add), ("Y", c))
                for c in range(DC):
                    plan.wait_drained(dve, ("Y", c), r)
                    yg_ready.after(dve.tensor_tensor(yg[:, c, :], yg[:, c, :], sz[:, c, :], ALU.mult))
                def half_of(x, j):
                    return x[:, 2 * j:2 * j + 2, :].rearrange("p t d -> p (t d)")

                for j in range(2):
                    plan.wait_full(dve, ("O", j), r)
                    plan.read(dve.tensor_tensor(half_of(h1, j), plan[("O", j)][:, :], half_of(hn, j), ALU.add),
                              ("O", j))
                for j in range(2):
                    sumsq.wait(dve, r, 2 * j + 2)
                    inv_std(sm[:, H[j]], H[j])
                    for t in (2 * j, 2 * j + 1):
                        ins = dve.tensor_scalar(u[:, t, :], h1[:, t, :], rs[:, t:t + 1], None, ALU.mult)
                    u_ready.after(ins)

                def gate(gk, uk, f):
                    plan.wait_drained(dve, (gk, f), r)
                    plan.wait_full(dve, (uk, f), r)
                    plan.read(dve.tensor_tensor(hf[:, f, :], sg[:, f % 2, :], plan[(uk, f)][:, :], ALU.mult),
                              (uk, f))

                for f in range(FF // P):
                    gate("G", "U", f)
                for j in range(2):
                    plan.wait_full(dve, ("F", j), r)
                    plan.read(dve.tensor_tensor(half_of(h1, j), plan[("F", j)][:, :], half_of(h1, j), ALU.add),
                              ("F", j))
                    plan.wait_drained(dve, ("F", j), r)
                    link(norm(tiles(h1, H[j]), tmp, H[j]))
                    x_free.after(dve.tensor_tensor(half_of(x1, j), half_of(xin, j), half_of(tmp, j), ALU.add))
                    x_free.wait(dve, r, j + 1)
                    u_ready.after(norm(tiles(x1, H[j]), u, H[j]))
                lora_lg.wait(dve, r, TILES)
                settle(dve)
                for t in range(TILES):
                    ins = dve.max(mx[:, t, :], lg0[:, t, :])
                link(ins)
                settle(dve)
                lora_top.after(dve.tensor_tensor(wk[:, :, 0:2], mx[:, :, 0:2],
                                                 mx[:, :, 0:1].broadcast_to([P, TILES, 2]), ALU.subtract))
                for t in range(TILES):
                    ins = dve.max_index(ix[:, t, :], mx[:, t, :], lg0[:, t, :])
                link(ins)
                link(dve.tensor_copy(ixf[:, :, 0:2], ix[:, :, 0:2]))
                dve.tensor_tensor(oh0[:, :, :, :],
                                  ixf[:, :, 0:2].unsqueeze(3).broadcast_to([P, TILES, 2, EXPERTS0]),
                                  iota[:, 0:EXPERTS0].unsqueeze(1).unsqueeze(1)
                                  .broadcast_to([P, TILES, 2, EXPERTS0]), ALU.is_equal)
                lora_exp.wait(dve, r, 1)
                link(dve.tensor_tensor(wsum[:, :], wk[:, :, 0], wk[:, :, 1], ALU.add))
                link(dve.reciprocal(wsum[:, :], wsum[:, :]))
                link(dve.scalar_tensor_tensor(wk[:, :, 0:2], wk[:, :, 0:2], LORA_ALPHA,
                                              wsum[:, :].unsqueeze(2).broadcast_to([P, TILES, 2]),
                                              ALU.mult, ALU.mult))
                link(dve.tensor_tensor(oh0[:, :, :, :], oh0[:, :, :, :],
                                       wk[:, :, 0:2].unsqueeze(3).broadcast_to([P, TILES, 2, EXPERTS0]),
                                       ALU.mult))
                link(dve.tensor_tensor(wm[:, :, :], oh0[:, :, 0, :], oh0[:, :, 1, :], ALU.add))
                for t in range(TILES):
                    ins = dve.tensor_tensor(
                        hw[:, t, :].rearrange("p (e r) -> p e r", e=EXPERTS0),
                        plan[("L", t)][:, D + EXPERTS0:LW].rearrange("p (e r) -> p e r", e=EXPERTS0),
                        wm[:, t, :].unsqueeze(2).broadcast_to([P, EXPERTS0, RANK]), ALU.mult)
                hw_ready.after(ins)
                for j in range(2):
                    lora_added.wait(dve, r, 2 * j + 2)
                    moments([plan[("L", t)][:, 0:D] for t in (2 * j, 2 * j + 1)], H[j])
                    inv_std(mv[:, H[j], 1], H[j])
                    for t in (2 * j, 2 * j + 1):
                        plan.read(dve.tensor_scalar(tmp[:, t, :], plan[("L", t)][:, 0:D], mv[:, t, 0:1],
                                                    rs[:, t:t + 1], ALU.subtract, ALU.mult), ("L", t))
                    for t in (2 * j, 2 * j + 1):
                        plan.wait_drained(dve, ("L", t), r)
                    x2_ready.after(dve.tensor_tensor(half_of(x1, j), half_of(x1, j), half_of(tmp, j), ALU.add))
                    x2_ready.wait(dve, r, j + 1)
                    u_ready.after(norm(tiles(x1, H[j]), u, H[j]))
                by_head = att_rows[:, 0, :].rearrange("p (g e d) -> p g e d", e=2, d=DK)
                for j in range(2):
                    plan.wait_full(dve, ("V", j), r)
                    for i in range(2):
                        src = plan[("V", j)][:, i * D:(i + 1) * D].rearrange("p (g e d) -> p g e d", e=2, d=DK)
                        for e in range(2):
                            ins = dve.tensor_tensor(v_pad[:, 2 * j + i, :, e, DK * e:DK * e + DK],
                                                    src[:, :, e, :], by_head[:, :, e, :], ALU.add)
                    plan.read(ins, ("V", j))
                for n in range(32 + 1):
                    if n < 32:
                        plan.wait_full(dve, ("S", n), r)
                        for i, cols in enumerate((slice(0, P), slice(P, TRI))):
                            ins = dve.tensor_reduce(nmax[:, n % 4, i:i + 1], plan[("S", n)][:, cols], AX.X,
                                                    ALU.max, negate=True)
                        nmax_ready.after(ins)
                    if n >= 1:
                        m = n - 1
                        plan.wait_drained(dve, ("S", m), r)
                        link(dve.reciprocal(esum[:, m % 4, :], esum[:, m % 4, :]))
                        for i, cols in enumerate((slice(0, P), slice(P, TRI))):
                            ins = dve.tensor_scalar(pr[:, m % 4, cols], pr[:, m % 4, cols],
                                                    esum[:, m % 4, i:i + 1], None, ALU.mult)
                        probs.after(ins)
                dve.wait_ge(scattered, r * (TILES * TOPK * 16) + CREDIT)
                for j in range(2):
                    plan.wait_full(dve, ("W", j), r)
                    plan.read(dve.tensor_tensor(h1[:, H[j], :],
                                                plan[("W", j)][:, :].rearrange("p (t d) -> p t d", t=2),
                                                att_rows[:, 1, :].unsqueeze(1).broadcast_to([P, 2, D]),
                                                ALU.add), ("W", j))
                    plan.wait_drained(dve, ("W", j), r)
                    link(norm(tiles(h1, H[j]), tmp, H[j]))
                    x3_ready.after(dve.tensor_tensor(half_of(x1, j), half_of(x1, j), half_of(tmp, j), ALU.add))
                    x3_ready.wait(dve, r, j + 1)
                    u_ready.after(norm(tiles(x1, H[j]), xf, H[j]))
                plan.wait_full(dve, "R", r)
                plan.read(dve.tensor_copy(lgt[:, :, :].rearrange("p t e -> p (t e)"),
                                          plan["R"][:, 0:TILES * E1]), "R")
                plan.wait_drained(dve, "R", r)
                first_norms(r + 1)
                gate("SG", "SU", 0)
                gate("SG", "SU", 1)
                link(dve.tensor_tensor(biased[:, :, :], lgt[:, :, :],
                                       rt_bias[:, :].unsqueeze(1).broadcast_to([P, TILES, E1]), ALU.add))
                settle(dve)
                for t in range(TILES):
                    ins = dve.max(mx[:, t, :], biased[:, t, :])
                link(ins)
                settle(dve)
                for t in range(TILES):
                    ins = dve.max_index(ix[:, t, :], mx[:, t, :], biased[:, t, :])
                link(ins)
                gate("SG", "SU", 2)
                gate("SG", "SU", 3)
                link(dve.tensor_copy(ixf[:, :, :], ix[:, :, 0:TOPK]))
                link(dve.tensor_tensor(oh, ixf[:, :, :].unsqueeze(3).broadcast_to([P, TILES, TOPK, E1]),
                                       iota[:, :].unsqueeze(1).unsqueeze(1).broadcast_to([P, TILES, TOPK, E1]),
                                       ALU.is_equal))
                with nc.allow_low_precision(reason="sums of zeros and ones up to one are exact"):
                    link(dve.tensor_reduce(chosen[:, :, :], oh.rearrange("p t k e -> p t e k"), AX.X, ALU.add))
                for t in range(TILES):
                    ins = dve.tensor_tensor(before[:, t + 1, :], before[:, t, :], chosen[:, t, :], ALU.add)
                    if t < TILES - 1:
                        link(ins)
                chosen_ready.after(ins)
                link(dve.tensor_tensor(prod, oh, lgt[:, :, :].unsqueeze(2).broadcast_to([P, TILES, TOPK, E1]),
                                       ALU.mult))
                link(dve.tensor_reduce(lk[:, :, :], prod, AX.X, ALU.add))
                link(dve.tensor_reduce(wsum[:, :], lk[:, :, :], AX.X, ALU.max))
                top_ready.after(dve.tensor_tensor(lk[:, :, :], lk[:, :, :],
                                                  wsum[:, :].unsqueeze(2).broadcast_to([P, TILES, TOPK]),
                                                  ALU.subtract))
                top_exp.wait(dve, r, 1)
                link(dve.tensor_reduce(wsum[:, :], wk[:, :, :], AX.X, ALU.add))
                link(dve.reciprocal(wsum[:, :], wsum[:, :]))
                dve.tensor_tensor(wts[:, bass.ds(r, 1), :].rearrange("p o (t k) -> p (o t) k", t=TILES),
                                  wk[:, :, :], wsum[:, :].unsqueeze(2).broadcast_to([P, TILES, TOPK]), ALU.mult)
                plan.wait_full(dve, "pos", r)
                plan.read(dve.tensor_tensor(
                    prod, oh, plan["pos"][:, 0:TILES * E1].rearrange("p (t e) -> p t e", t=TILES)
                    .unsqueeze(2).broadcast_to([P, TILES, TOPK, E1]), ALU.mult), "pos")
                plan.wait_drained(dve, "pos", r)
                link(dve.tensor_copy(before[:, 0, :], before[:, TILES, :]))
                link(dve.tensor_reduce(slot[:, :, :], prod, AX.X, ALU.add))
                link(dve.tensor_scalar(over[:, :, :], slot[:, :, :], float(CAP), float(4 * SLOTS),
                                       ALU.is_ge, ALU.mult))
                link(dve.scalar_tensor_tensor(slot[:, :, :], ixf[:, :, :], float(CAP), slot[:, :, :],
                                              ALU.mult, ALU.add))
                link(dve.tensor_tensor(slot[:, :, :], slot[:, :, :], over[:, :, :], ALU.add))
                dve.tensor_scalar(gidx[:, bass.ds(r, 1), :].rearrange("p o (t k) -> p (o t) k", t=TILES),
                                  slot[:, :, :], float(SLOTS), None, ALU.min)
                sidx_ready.after(dve.tensor_copy(sidx[:, :].rearrange("p (t k) -> p t k", t=TILES),
                                                 slot[:, :, :]))
                for j in range(2):
                    plan.wait_full(dve, ("SD", j), r)
                    plan.read(dve.tensor_copy(half_of(tmp, j), plan[("SD", j)][:, :]), ("SD", j))
                dve.wait_ge(xf_stored, r * 32 + 32)
            if count[0] != chain.per:
                raise ValueError(f"dve_chain is raised {count[0]} times in a round")
            tail_vector(dve)


_SHAPE = (8, 256, 256)


def _layouts(np, i):
    f = np.float32

    def chunks(w):
        return np.ascontiguousarray(w.reshape(-1, 128, w.shape[1]).transpose(1, 0, 2))

    def channels(*vs):
        out = np.zeros((128, 2, 8), f)
        for n, v in enumerate(vs):
            out[:, :, n] = v.reshape(2, 128).T
        return out

    k, q = np.arange(128)[:, None], np.arange(128)[None, :]
    low = np.where(q >= k, 0.0, -1e30).astype(f)
    none = np.zeros((128, 128), f)
    att = [i["L1_attn_" + n] for n in ("Wq", "Wk", "Wv", "Wo")]
    heads = [4 * (2 * (p // 4) + e) + p % 4 for p in range(16) for e in range(2)]
    state = (np.array(heads)[:, None] * 64 + np.arange(64)).ravel()
    conv_rows = np.concatenate([np.arange(256), 256 + state, 2304 + state])
    proj_rows = np.concatenate([np.arange(256), 256 + conv_rows, np.arange(4608, 4640)])
    gu = np.concatenate([i["L1_ffn_gate_w"], i["L1_ffn_up_w"]], 1)
    a = {
        "x": np.ascontiguousarray(i["L0_attn_hidden_states"].reshape(-1, 256)),
        "ident": np.eye(128, dtype=f),
        "iota": np.tile(np.arange(64, dtype=f), (128, 1)),
        "parity": np.stack([(np.arange(128) % 32 < 16), (np.arange(128) % 32 >= 16)], 1).astype(f),
        "keyq_mask": np.concatenate([low, none, low], 1),
        "qkey_mask": np.concatenate([low.T, none, low.T], 1),
        "earlier": (k < q).astype(f),
        "neg_sel": -np.tile(np.eye(32, dtype=f), (3, 1)),
        "chan": channels(i["L0_attn_z_bias"], np.repeat(i["L0_attn_D"], 8), i["L0_attn_norm1_w"],
                         i["L0_attn_norm2_w"], i["L1_attn_bq"], i["L1_attn_bk"]),
        "conv_w": np.ascontiguousarray(i["L0_attn_conv_w"][conv_rows].reshape(34, 128, 4).transpose(1, 0, 2)),
        "conv_b": np.ascontiguousarray(i["L0_attn_conv_b"][conv_rows].reshape(34, 128).T),
        "w_in": chunks(i["L0_attn_in_proj_w"][proj_rows].T),
        "w_out": chunks(i["L0_attn_out_proj_w"].T),
        "w_gu": chunks(np.concatenate([i["L0_attn_gate_w"], i["L0_attn_up_w"]], 0).T),
        "w_dn": chunks(i["L0_attn_down_w"].T),
        "w_lora": chunks(np.concatenate([i["L0_ffn_W"], i["L0_ffn_gate_w"],
                                         i["L0_ffn_A"].reshape(128, 256)], 0).T),
        "w_lb": np.ascontiguousarray(i["L0_ffn_B"].transpose(0, 2, 1).reshape(128, 256)),
        "w_att": np.ascontiguousarray(np.stack(att, 1).reshape(2, 128, 4, 256).transpose(1, 0, 2, 3)),
        "att_rows": np.stack([i["L1_attn_bv"], i["L1_attn_bo"]])[None],
        "w_rt": chunks(i["L1_ffn_router_w"].T),
        "rt_bias": i["L1_ffn_router_bias"][None, :],
        "w_sgu": chunks(np.concatenate([i["L1_ffn_sh_gate_w"].reshape(512, 256),
                                        i["L1_ffn_sh_up_w"].reshape(512, 256)], 0).T),
        "w_sdn": chunks(i["L1_ffn_sh_down_w"].transpose(0, 2, 1).reshape(512, 256)),
        "w_egu": np.ascontiguousarray(gu.transpose(2, 0, 1).reshape(2, 128, 64, 128).transpose(1, 0, 2, 3)),
        "w_edn": np.ascontiguousarray(i["L1_ffn_down_w"].transpose(2, 0, 1)),
    }
    return {n: np.ascontiguousarray(v) for n, v in a.items()}


def kernel(**inputs):
    import numpy as _np
    import concourse.bacc as _bacc
    from concourse import mybir as _mybir
    from concourse.bass_utils import run_bass_kernel_spmd as _run

    nc = _bacc.Bacc("TRN2", target_bir_lowering=False, num_devices=1)
    arrays = _layouts(_np, {n: _np.asarray(v) for n, v in inputs.items()})
    aps = {n: nc.dram_tensor("in_" + n, v.shape, _mybir.dt.from_np(v.dtype), kind="ExternalInput").ap()
           for n, v in arrays.items()}
    out = nc.dram_tensor("out_dram", (TOKENS, D), F32, kind="ExternalOutput").ap()
    sandwich(nc, aps, out)
    r = _run(nc, [{"in_" + n: v for n, v in arrays.items()}], core_ids=[0])
    return r.results[0]["out_dram"].reshape(_SHAPE)
```

```python
from contextlib import ExitStack

import concourse.bass as bass
from concourse import mybir

ALU = mybir.AluOpType
ACT = mybir.ActivationFunctionType
AX = mybir.AxisListType
F32 = mybir.dt.float32
BF16 = mybir.dt.bfloat16
U32 = mybir.dt.uint32

P = 128
D = 256
DC = D // P
SEQ = 256
TOKENS = 8 * SEQ
GROUP = 512
ROUNDS = TOKENS // GROUP
TILES = GROUP // P
SEQS = GROUP // SEQ
EPS = 1e-5

HEADS = 32
STATE = 64
HEADDIM = D // HEADS
TAPS = 4
PAIRS = HEADS // 2
PROJ = 2 * D + 2 * HEADS * STATE + HEADS
QUADS = HEADS // 4
HALF = GROUP // 2
TRI = 3 * P
FF = 1024
EXPERTS0, RANK, LORA_ALPHA = 8, 16, 16.0
LW = D + EXPERTS0 + EXPERTS0 * RANK
AHEADS = 16
DK = D // AHEADS
E1, TOPK, F1, CAP = 64, 4, 64, 32
SHF = 512
SLOTS = E1 * CAP
EG = P // CAP
EGROUPS = E1 // EG


class BankPlan:

    def __init__(self, banks, full, drained):
        self.banks, self.full_sems, self.drained_sems = banks, full, drained
        self.place, self.count = {}, [0] * len(banks)
        self.base = [0] * len(banks)

    def use(self, key, bank):
        if key in self.place:
            raise ValueError(f"{key} has its bank already")
        self.place[key] = (bank, self.count[bank])
        self.count[bank] += 1

    def __getitem__(self, key):
        return self.banks[self.place[key][0]]

    def value(self, b, n, r):
        return r * self.count[b] + self.base[b] + n

    def before(self, key, r):
        b, n = self.place[key]
        return self.drained_sems[b], self.value(b, n, r) + 1

    def full(self, key, r):
        b, n = self.place[key]
        return self.full_sems[b], self.value(b, n + 1, r)

    def drained(self, key, r):
        b, n = self.place[key]
        return self.drained_sems[b], self.value(b, n + 1, r) + 1

    def fills(self, key):
        return self.full_sems[self.place[key][0]]

    def drains(self, key):
        return self.drained_sems[self.place[key][0]]


class Signal:

    def __init__(self, sem, per):
        self.sem, self.per = sem, per

    def at(self, r, n):
        return r * self.per + n


def sandwich(nc, A, out):
    with ExitStack() as ctx:
        def sb(name, shape, dt=F32):
            return ctx.enter_context(nc.sbuf_tensor(name, shape, dt))

        def sem(name):
            return ctx.enter_context(nc.semaphore(name))

        consts_cast = sem("consts_cast")
        settled = sem("settled")

        def settle(eng):
            eng.sem_inc(settled, 1)

        def signal(name, per):
            return Signal(sem(name), per)

        banks = [ctx.enter_context(nc.psum_tensor(f"bank{i}", [P, 512], F32)) for i in range(8)]
        full = [sem(f"bank_full{i}") for i in range(8)]
        drained = [sem(f"bank_drained{i}") for i in range(8)]

        xg_dram = nc.dram_tensor("xg_dram", (SLOTS, D), F32, kind="Internal").ap()
        y_dram = nc.dram_tensor("y_dram", (SLOTS + P, D), F32, kind="Internal").ap()
        x3_dram = nc.dram_tensor("x3_dram", (TOKENS, D), F32, kind="Internal").ap()
        sh_dram = nc.dram_tensor("sh_dram", (TOKENS, D), F32, kind="Internal").ap()

        ident = sb("ident", [P, P])
        ident_bf = sb("ident_bf", [P, P], BF16)
        keyq_mask = sb("keyq_mask", [P, 2 * P], BF16)
        qkey_mask = sb("qkey_mask", [P, 2 * P], BF16)
        earlier = sb("earlier", [P, P], BF16)
        ones_bf = sb("ones_bf", [P, P], BF16)
        zeros_bf = sb("zeros_bf", [P, 512], BF16)
        neg_sel = sb("neg_sel", [96, HEADS], BF16)
        ones = sb("ones", [P, SEQ])
        iota = sb("iota", [P, E1])
        half = sb("half", [P, TILES])
        parity = sb("parity", [P, 2])
        neg_in = sb("neg_in", [96, HEADS])
        w_in = sb("w_in", [P, DC, PROJ])
        conv_w = sb("conv_w", [P, 34, TAPS])
        conv_b = sb("conv_b", [P, 34])
        chan = sb("chan", [P, DC, 8])
        kbias = sb("kbias", [P, DC, 2])
        qbias = sb("qbias", [P, DC])
        w_out = sb("w_out", [P, DC, D])
        w_gu = sb("w_gu", [P, DC, 2 * FF])
        w_dn = sb("w_dn", [P, FF // P, D])
        w_lora = sb("w_lora", [P, DC, LW])
        w_lb = sb("w_lb", [P, D])
        w_att = sb("w_att", [P, DC, 4, D])
        att_rows = sb("att_rows", [P, 2, D])
        w_rt = sb("w_rt", [P, DC, E1])
        rt_bias = sb("rt_bias", [P, E1])
        w_sgu = sb("w_sgu", [P, DC, 2 * SHF])
        w_sdn = sb("w_sdn", [P, SHF // P, D])

        xin = sb("xin", [P, TILES, D])
        hn = sb("hn", [P, TILES, D])
        u = sb("u", [P, TILES, D])
        uT = sb("uT", [P, DC, GROUP])
        h1 = sb("h1", [P, TILES, D])
        cstage = h1[:, :, :].rearrange("p (a t) d -> p a (t d)", a=2)
        x1 = sb("x1", [P, TILES, D])
        tmp = sb("tmp", [P, TILES, D])
        xf = sb("xf", [P, TILES, D])
        stats = sb("stats", [P, TILES, 6])
        mv = sb("mv", [P, TILES, 2])
        ve = sb("ve", [P, TILES])
        rs = sb("rs", [P, TILES])
        stats1 = sb("stats1", [P, TILES, 6])
        mv1 = sb("mv1", [P, TILES, 2])
        ve1 = sb("ve1", [P, TILES])
        rs1 = sb("rs1", [P, TILES])
        r1 = sb("r1", [P, TILES])
        shift = sb("shift", [P, TILES])
        sm1 = sb("sm1", [P, TILES])
        sm = sb("sm", [P, TILES])
        hf = sb("hf", [P, FF // P, GROUP])
        xc = sb("xc", [P, DC, GROUP])
        sz = sb("sz", [P, DC, GROUP])
        yg = sb("yg", [P, DC, GROUP])
        x_pad = sb("x_pad", [P, TILES, QUADS * P + 32])
        bc = hf[:, 0:6, :].rearrange("p (s w) l -> p s w l", s=3)
        dec = sb("dec", [P, 6, TRI])
        sc = sb("sc", [P, 4, TRI])
        sp_a = hf[0:HEADS, 6, :]
        sp_b = hf[0:HEADS, 7, :]
        cumP = hf[0:HEADS, 5, :]
        mid0 = sb("mid0", [HEADS, GROUP], BF16)
        cum3 = sb("cum3", [96, SEQS, TRI], BF16)
        cum_tok = sb("cum_tok", [P, TILES, HEADS])
        sg = xc
        lg0 = sb("lg0", [P, TILES, EXPERTS0])
        mx = sb("mx", [P, TILES, 8])
        ix = sb("ix", [P, TILES, 8], U32)
        ixf = sb("ixf", [P, TILES, TOPK])
        oh0 = sb("oh0", [P, TILES, 2, EXPERTS0])
        wk = sb("wk", [P, TILES, TOPK])
        wsum = sb("wsum", [P, TILES])
        wm = sb("wm", [P, TILES, EXPERTS0])
        hw = yg[:, 0, :].rearrange("p (t j) -> p t j", t=TILES)
        hwT = yg[:, 1, :]
        qT = xc
        kT = [sz, yg]
        v_pad = sb("v_pad", [P, TILES, AHEADS // 2, 2, 32])
        nmax = sb("nmax", [P, 4, 2])
        esum = sb("esum", [P, 4, 2])
        pr = dec
        prT = sc
        oT = hf[:, 0:2, :]
        lgt = sb("lgt", [P, TILES, E1])
        biased = sb("biased", [P, TILES, E1])
        oh = hf[:, 4:6, :].rearrange("p a (b e) -> p (a b) e", e=E1).rearrange("p (t k) e -> p t k e", t=TILES)
        prod = hf[:, 6:8, :].rearrange("p a (b e) -> p (a b) e", e=E1).rearrange("p (t k) e -> p t k e", t=TILES)
        chosen = sb("chosen", [P, TILES, E1], BF16)
        before = sb("before", [P, TILES + 1, E1], BF16)
        lk = sb("lk", [P, TILES, TOPK])
        slot = sb("slot", [P, TILES, TOPK])
        over = sb("over", [P, TILES, TOPK])
        sidx = sb("sidx", [P, TILES * TOPK], U32)
        gidx = sb("gidx", [P, ROUNDS, TILES * TOPK], U32)
        wts = sb("wts", [P, ROUNDS, TILES * TOPK])

        plan = BankPlan(banks, full, drained)
        plan.use("dt", 6)
        for c in range(DC):
            plan.use(("X", c), 4 + c)
        for c in range(DC):
            plan.use(("Z", c), 2 + c)
        plan.use("cumT", 7)
        for w in range(2):
            plan.use(("BC", 1, w), 6 + w)
        for c in range(DC):
            plan.use(("Y", c), 6 + c)
        for c in range(DC):
            plan.use(("XT", c), 2 + c)
        uses = [(p, b, e) for p in range(PAIRS) for b in range(SEQS) for e in range(2)]
        for p in range(PAIRS):
            for w in range(2):
                if p != 1:
                    plan.use(("BC", p, w), w)
        for p in range(PAIRS):
            for b in range(SEQS):
                for e in range(2):
                    plan.use(("A", p, b, e), 2 + e)
                    plan.use(("CB", p, b, e), 4 + e)
        for j in range(2):
            plan.use(("O", j), j)
        for j in range(2):
            plan.use(("T", "ffn", j), 2 + j)
        for f in range(FF // P):
            plan.use(("G", f), 4 + f % 2)
            plan.use(("U", f), f % 2)
        for j in range(2):
            plan.use(("F", j), 2 + j)
        for j in range(2):
            plan.use(("T", "lora", j), 4 + j)
        for t in range(TILES):
            plan.use(("L", t), t)
        for j in range(2):
            plan.use(("LT", j), 4 + j)
        for j in range(2):
            plan.use(("T", "att", j), 6 + j)
        for c in range(DC):
            plan.use(("Q", c), c)
            plan.use(("K", c), 2 + c)
            plan.use(("V", c), 4 + c)
        for b in range(SEQS):
            plan.use(("OT", b), 6 + b)
        auses = [(h, b) for b in range(SEQS) for h0 in range(0, AHEADS, 4) for e in range(2)
                 for h in (h0 + e, h0 + 2 + e)]
        for n in range(len(auses)):
            plan.use(("S", n), n % 4)
            plan.use(("PT", n), 4 + n % 2)
        for j in range(2):
            plan.use(("W", j), 6 + j)
            plan.use(("T", "moe", j), 6 + j)
            plan.use(("R", j), 6 + j)
        for j in range(2):
            for g in range(SHF // P // 2):
                plan.use(("SG", g, j), g)
                plan.use(("SU", g, j), 2 + g)
        for j in range(2):
            plan.use(("SD", j), 4 + j)
        plan.use("pos", 6)
        for j in range(2):
            plan.use(("T", "mix", j), j)
            plan.base[j] = 1

        CREDIT = 16
        ALL = slice(0, TILES)
        H = [slice(0, 2), slice(2, 4)]
        POWERS = [H[0], H[1]] + 3 * [H[0], H[0], H[1], H[1]]
        consts_in = sem("consts_in")
        w_sem = {k: sem("in_" + k) for k in ("out", "ffn", "lora", "att", "moe")}
        w_proj = [sem(f"in_proj{i}") for i in range(3)]
        PROJ_PAIRS = (0, 2)
        pads_zero = sem("pads_zero")
        x_in = sem("x_in")
        x_free = signal("x_free", 2)
        var_ready = signal("var_ready", len(POWERS))
        rstd_ready = signal("rstd_ready", len(POWERS))
        ahead_var = signal("ahead_var", 2)
        ahead_rstd = signal("ahead_rstd", 2)
        mix_ready = signal("mix_ready", 2)
        u_ready = signal("u_ready", 8)
        tap0 = signal("tap0", 34)
        dt_abs = signal("dt_abs", 1)
        dt_log = signal("dt_log", 1)
        exp_dt = signal("exp_dt", 1)
        cum_ready = signal("cum_ready", 1)
        cum3_ready = signal("cum3_ready", 1)
        y_added = signal("y_added", 64)
        yg_ready = signal("yg_ready", DC)
        sumsq = signal("sumsq", TILES)
        hw_ready = signal("hw_ready", 2)
        lora_top = signal("lora_top", 2)
        lora_exp = signal("lora_exp", 2)
        lora_added = signal("lora_added", TILES)
        lora_lg = signal("lora_lg", TILES)
        nmax_ready = signal("nmax_ready", 32)
        probs = signal("probs", 32)
        o_added = signal("o_added", 32)
        top_ready = signal("top_ready", 1)
        top_exp = signal("top_exp", 1)
        chosen_ready = signal("chosen_ready", 1)
        sidx_ready = signal("sidx_ready", 1)
        scattered = sem("scattered")
        stored_round = sem("stored_round")
        zero_filled = sem("zero_filled")
        chain = signal("dve_chain", 176)
        x3_ready = signal("x3_ready", 2)
        ahead_chain = signal("ahead_chain", 7)

        ESLOTS = 8
        EROUNDS = EGROUPS // ESLOTS
        EPAIRS = ESLOTS // 2
        e_spare = sb("e_spare", [P, EG * D])

        def pieces(weights, n):
            flat = weights.rearrange("p k n -> p (k n)")
            return [flat[:, i * n:(i + 1) * n] for i in range(flat.shape[1] // n)]

        ew = pieces(w_in[:, :, :], EG * D) + pieces(w_gu[:, :, :], EG * D) + pieces(w_dn[:, :, :], EG * D) \
            + [e_spare[:, :]]
        egu = [ew[2 * s].rearrange("p (k e j) -> p k e j", k=DC, e=EG) for s in range(ESLOTS)]
        edn = [ew[2 * s + 1][0:F1, :].rearrange("p (e d) -> p e d", e=EG) for s in range(ESLOTS)]
        xg = [(xin, hn)[s // 4][:, s % 4, :] for s in range(ESLOTS)]
        xgT = [uT[:, 0, i * DC * P:(i + 1) * DC * P].rearrange("p (k s) -> p k s", k=DC) for i in range(2)]
        esg = [uT[:, 1, i * F1:(i + 1) * F1] for i in range(2)]
        eh = [uT[:, 1, (2 + i) * F1:(3 + i) * F1] for i in range(2)]
        ehT = [uT[0:F1, 1, 4 * F1 + i * P:4 * F1 + (i + 1) * P] for i in range(2)]
        yt = [u[:, i, :] for i in range(4)]
        yk = [hf[:, 2 * s:2 * s + 2, :].rearrange("p a b -> p (a b)").rearrange("p (k d) -> p k d", k=TOPK)
              for s in range(TILES)]
        shx = [x_pad[:, s, 0:2 * D].rearrange("p (a d) -> p a d", a=2) for s in range(TILES)]
        acc = [tmp[:, s, :] for s in range(2)]
        ot = [tmp[:, 2 + s, :] for s in range(2)]
        gi = sb("gi", [P, TILES, TOPK], U32)
        wt = sb("wt", [P, TILES, TOPK])

        tail = BankPlan(banks, full, drained)
        tail.base = [ROUNDS * n + b for n, b in zip(plan.count, plan.base)]
        for s in range(ESLOTS):
            tail.use(("XG", s), s % 2)
            tail.use(("GU", s), 2 + s % 2)
            tail.use(("HT", s), 4 + s % 2)
            tail.use(("YO", s), 6 + s % 2)
        e_in = [sem(f"e_in{s}") for s in range(ESLOTS)]
        xg_in = [sem(f"xg_in{s}") for s in range(ESLOTS)]
        e_silu = signal("e_silu", ESLOTS)
        y_out = [sem(f"y_out{s}") for s in range(4)]
        gi_ready = signal("gi_ready", TILES)
        gathered = [sem(f"gathered{s}") for s in range(TILES)]
        shx_in = [sem(f"shx_in{s}") for s in range(TILES)]
        var2 = signal("var2", TILES)
        rstd2 = signal("rstd2", TILES)
        out_ready = signal("out_ready", TILES)
        stored = [sem(f"stored{s}") for s in range(2)]
        chain2 = signal("dve_chain2", 7 * TILES)

        def load_experts(sp, s, g):
            sp.dma_start(egu[s], A["w_egu"][:, :, bass.ds(g * EG, EG), :]).then_inc(e_in[s], 16)
            sp.dma_start(edn[s], A["w_edn"][:, bass.ds(g * EG, EG), :]).then_inc(e_in[s], 16)

        def load_tokens(sp, s, g):
            sp.dma_start(xg[s], xg_dram[bass.ds(g * P, P), :]).then_inc(xg_in[s], 16)

        def load_sums(sp, s, i):
            sp.dma_start(shx[s][:, 0, :], sh_dram[bass.ds(i * P, P), :]).then_inc(shx_in[s], 16)
            sp.dma_start(shx[s][:, 1, :], x3_dram[bass.ds(i * P, P), :]).then_inc(shx_in[s], 16)

        def tail_sync(sp):
            sp.wait_ge(stored_round, 32 * ROUNDS + CREDIT)
            for s in range(TILES):
                load_sums(sp, s, s)
            sp.wait_ge(scattered, 16 * TILES * TOPK * ROUNDS + CREDIT)
            for s in range(ESLOTS):
                load_tokens(sp, s, s)

            for r in range(EROUNDS):
                for s in range(ESLOTS):
                    sp.wait_ge(*tail.drained(("YO", s), r))
                    g = r * ESLOTS + s
                    sp.dma_start(y_dram[g * P:(g + 1) * P, :], yt[s % 4]).then_inc(y_out[s % 4], 16)
                    if r < EROUNDS - 1:
                        load_experts(sp, s, g + ESLOTS)
                        load_tokens(sp, s, g + ESLOTS)

            def combination(r, last):
                for s in range(TILES):
                    sp.wait_ge(out_ready.sem, out_ready.at(r, s + 1))
                    settle(sp)
                    sp.dma_start(out[bass.ds((TILES * r + s) * P, P), :], ot[s % 2]).then_inc(stored[s % 2], 16)
                    if not last:
                        load_sums(sp, s, TILES * r + TILES + s)

            with sp.Fori(0, ROUNDS - 1) as r:
                combination(r, False)
            combination(ROUNDS - 1, True)
            for s in range(2):
                sp.wait_ge(stored[s], 16 * TILES // 2 * ROUNDS + CREDIT)

        def tail_tensor(pe):
            def turn(s, r):
                pe.wait_ge(xg_in[s], r * 16 + 16)
                pe.wait_ge(*tail.before(("XG", s), r))
                for k in range(DC):
                    mm = pe.transpose(tail[("XG", s)][:, k * P:(k + 1) * P], xg[s][:, k * P:(k + 1) * P],
                                      ident[:, :])
                mm.then_inc(tail.fills(("XG", s)), 1)

            def gate_up(s, r):
                pe.wait_ge(*tail.drained(("XG", s), r))
                pe.wait_ge(*tail.before(("GU", s), r))
                settle(pe)
                pe.wait_ge(e_in[s], r * 32 + 32)
                for e in range(EG):
                    rows = slice(CAP * e, CAP * (e + 1))
                    for k in range(DC):
                        mm = pe.matmul(tail[("GU", s)][rows, 0:P], xgT[s % 2][:, k, rows], egu[s][:, k, e, :],
                                       start=k == 0, stop=k == DC - 1)
                mm.then_inc(tail.fills(("GU", s)), 1)

            def turn_hidden(s, r):
                pe.wait_ge(*tail.drained(("GU", s), r))
                pe.wait_ge(*tail.before(("HT", s), r))
                settle(pe)
                pe.transpose(tail[("HT", s)][0:F1, 0:P], eh[s % 2], ident[:, :])\
                    .then_inc(tail.fills(("HT", s)), 1)

            def down(s, r):
                pe.wait_ge(*tail.drained(("HT", s), r))
                pe.wait_ge(*tail.before(("YO", s), r))
                settle(pe)
                for e in range(EG):
                    rows = slice(CAP * e, CAP * (e + 1))
                    mm = pe.matmul(tail[("YO", s)][rows, 0:D], ehT[s % 2][:, rows], edn[s][:, e, :],
                                   start=True, stop=True)
                mm.then_inc(tail.fills(("YO", s)), 1)

            with pe.Fori(0, EROUNDS) as r:
                def both(stage, pair):
                    stage(2 * pair, r)
                    stage(2 * pair + 1, r)

                both(turn, 0)
                both(gate_up, 0)
                for pair in range(EPAIRS):
                    if pair + 1 < EPAIRS:
                        both(turn, pair + 1)
                    both(turn_hidden, pair)
                    if pair + 1 < EPAIRS:
                        both(gate_up, pair + 1)
                    both(down, pair)

        def tail_scalar(act):
            def turned_tokens(s, r):
                act.wait_ge(*tail.full(("XG", s), r))
                act.activation(xgT[s % 2], tail[("XG", s)][:, 0:DC * P]
                               .rearrange("p (k s) -> p k s", k=DC), ACT.Copy)\
                                   .then_inc(tail.drains(("XG", s)), 1)

            def gate(s, r):
                act.wait_ge(*tail.full(("GU", s), r))
                act.activation(esg[s % 2], tail[("GU", s)][:, 0:F1], ACT.Silu).then_inc(e_silu.sem, 1)

            def turned_hidden(s, r):
                act.wait_ge(*tail.full(("HT", s), r))
                act.activation(ehT[s % 2], tail[("HT", s)][0:F1, 0:P], ACT.Copy)\
                    .then_inc(tail.drains(("HT", s)), 1)

            with act.Fori(0, EROUNDS) as r:
                def both(stage, pair):
                    stage(2 * pair, r)
                    stage(2 * pair + 1, r)

                both(turned_tokens, 0)
                both(gate, 0)
                for pair in range(EPAIRS):
                    if pair + 1 < EPAIRS:
                        both(turned_tokens, pair + 1)
                    both(turned_hidden, pair)
                    if pair + 1 < EPAIRS:
                        both(gate, pair + 1)

        def tail_pool(pool):
            def gather(s, r):
                pool.wait_ge(gi_ready.sem, gi_ready.at(r, s + 1))
                settle(pool)
                for k in range(TOPK):
                    pool.indirect_dma_start(
                        out=yk[s][:, k, :], out_offset=None, in_=y_dram,
                        in_offset=bass.IndirectOffsetOnAxis(ap=gi[:, s, k:k + 1], axis=0))\
                        .then_inc(gathered[s], 16)

            def combination(r, last):
                for s in range(TILES):
                    pool.wait_ge(var2.sem, var2.at(r, s + 1))
                    pool.tensor_tensor(rs[:, s:s + 1], ve[:, s:s + 1], half[:, 0:1], ALU.pow)\
                        .then_inc(rstd2.sem, 1)
                    if not last:
                        gather(s, r + 1)

            for s in range(4):
                pool.wait_ge(y_out[s], 16 * EGROUPS // 4 + CREDIT)
            for s in range(TILES):
                gather(s, 0)
            with pool.Fori(0, ROUNDS - 1) as r:
                combination(r, False)
            combination(ROUNDS - 1, True)

        def tail_vector(dve):
            def gate(s, r):
                dve.wait_ge(e_silu.sem, e_silu.at(r, s + 1))
                dve.tensor_tensor(eh[s % 2], esg[s % 2], tail[("GU", s)][:, F1:P], ALU.mult)\
                    .then_inc(tail.drains(("GU", s)), 1)

            def results(s, r):
                dve.wait_ge(*tail.full(("YO", s), r))
                dve.wait_ge(y_out[s % 4], r * 32 + CREDIT + 16 * (s // 4))
                dve.tensor_copy(yt[s % 4], tail[("YO", s)][:, 0:D]).then_inc(tail.drains(("YO", s)), 1)

            with dve.Fori(0, EROUNDS) as r:
                def both(stage, pair):
                    stage(2 * pair, r)
                    stage(2 * pair + 1, r)

                both(gate, 0)
                for pair in range(EPAIRS):
                    if pair + 1 < EPAIRS:
                        both(gate, pair + 1)
                    both(results, pair)

            def weights(s, r):
                one = bass.ds(r, 1)
                k = slice(s * TOPK, (s + 1) * TOPK)
                dve.tensor_copy(wt[:, s, :], wts[:, one, k].rearrange("p o k -> p (o k)"))
                dve.tensor_copy(gi[:, s, :], gidx[:, one, k].rearrange("p o k -> p (o k)"))\
                    .then_inc(gi_ready.sem, 1)
                dve.wait_ge(gi_ready.sem, gi_ready.at(r, s + 1))

            def combination(r, last):
                count = [0]

                def link(ins):
                    count[0] += 1
                    ins.then_inc(chain2.sem, 1)
                    dve.wait_ge(chain2.sem, chain2.at(r, count[0]))

                def finish(s):
                    dve.wait_ge(rstd2.sem, rstd2.at(r, s + 1))
                    dve.wait_ge(stored[s % 2], r * 32 + CREDIT + 16 * (s // 2))
                    a = acc[s % 2]
                    link(dve.tensor_scalar(a, a, mv[:, s, 0:1], rs[:, s:s + 1], ALU.subtract, ALU.mult))
                    dve.tensor_tensor(ot[s % 2], shx[s][:, 1, :], a, ALU.add).then_inc(out_ready.sem, 1)

                for s in range(TILES):
                    dve.wait_ge(shx_in[s], r * 32 + 32)
                    dve.wait_ge(gathered[s], r * 64 + 64)
                    a = acc[s % 2]
                    if s >= 2:
                        dve.wait_ge(out_ready.sem, out_ready.at(r, s - 1))
                    for k in range(TOPK):
                        link(dve.scalar_tensor_tensor(a, yk[s][:, k, :], wt[:, s, k:k + 1],
                                                      shx[s][:, 0, :] if k == 0 else a, ALU.mult, ALU.add))
                    if not last:
                        weights(s, r + 1)
                    link(dve.bn_stats(stats[:, s, :], a))
                    settle(dve)
                    link(dve.bn_aggr(mv[:, s, :], stats[:, s, :]))
                    dve.tensor_scalar(ve[:, s:s + 1], mv[:, s, 1:2], EPS, None, ALU.add).then_inc(var2.sem, 1)
                    if s >= 1:
                        finish(s - 1)
                finish(TILES - 1)
                dve.wait_ge(out_ready.sem, out_ready.at(r, TILES))
                if count[0] != chain2.per:
                    raise ValueError(f"dve_chain2 is raised {count[0]} times in a round")

            for s in range(TILES):
                weights(s, 0)
            with dve.Fori(0, ROUNDS - 1) as r:
                combination(r, False)
            combination(ROUNDS - 1, True)

        block = ctx.enter_context(nc.Block())

        def tok(r, n=GROUP, o=0):
            return bass.ds(r * GROUP + o, n)

        @block.sync
        def _(sp):
            for b in drained:
                sp.sem_inc(b, 1)
            for free in (stored_round, *stored, *y_out):
                sp.sem_inc(free, CREDIT)
            sp.dma_start(xin[:, :, :], A["x"][0:GROUP, :].rearrange("(t p) d -> p t d", p=P)).then_inc(x_in, 16)
            for dst, name in ((ident[:, :], "ident"), (iota[:, :], "iota"), (parity[:, :], "parity"),
                              (cstage[:, 0, 0:2 * P], "keyq_mask"), (cstage[:, 1, 0:2 * P], "qkey_mask"),
                              (cstage[:, 0, TRI:512], "earlier"),
                              (neg_in[:, :], "neg_sel"),
                              (chan[:, :, :], "chan"), (conv_w[:, :, :], "conv_w"), (conv_b[:, :], "conv_b")):
                sp.dma_start(dst, A[name]).then_inc(consts_in, 16)
            edges = [0] + [2 * D + HEADS + 2 * P * n for n in (*PROJ_PAIRS, PAIRS)]
            for lo, hi, landed in zip(edges, edges[1:], w_proj):
                sp.dma_start(w_in[:, :, lo:hi], A["w_in"][:, :, lo:hi]).then_inc(landed, 16)
                if landed is w_proj[1]:
                    sp.wait_ge(w_proj[0], 16)
            sp.dma_start(w_out[:, :, :], A["w_out"]).then_inc(w_sem["out"], 16)
            sp.dma_start(w_gu[:, :, :], A["w_gu"]).then_inc(w_sem["ffn"], 16)
            sp.dma_start(w_dn[:, :, :], A["w_dn"]).then_inc(w_sem["ffn"], 16)
            sp.dma_start(w_lora[:, :, :], A["w_lora"]).then_inc(w_sem["lora"], 16)
            sp.dma_start(w_lb[:, :], A["w_lb"]).then_inc(w_sem["lora"], 16)
            sp.dma_start(w_att[:, :, :, :], A["w_att"]).then_inc(w_sem["att"], 16)
            sp.dma_start(att_rows[:, :, :], A["att_rows"].broadcast_to([P, 2, D])).then_inc(w_sem["att"], 16)
            sp.dma_start(w_rt[:, :, :], A["w_rt"]).then_inc(w_sem["moe"], 16)
            sp.dma_start(rt_bias[:, :], A["rt_bias"].broadcast_to([P, E1])).then_inc(w_sem["moe"], 16)
            sp.dma_start(w_sgu[:, :, :], A["w_sgu"]).then_inc(w_sem["moe"], 16)
            sp.dma_start(w_sdn[:, :, :], A["w_sdn"]).then_inc(w_sem["moe"], 16)
            sp.wait_ge(pads_zero, 5)
            sp.dma_start(y_dram[SLOTS:SLOTS + P, :], tmp[:, 0, :]).then_inc(zero_filled, 16)
            for g in range(SLOTS // GROUP - 1):
                sp.dma_start(xg_dram[g * GROUP:(g + 1) * GROUP, :].rearrange("(t p) d -> p t d", p=P),
                             tmp[:, :, :]).then_inc(zero_filled, 16)

            def store(r):
                sp.wait_ge(x3_ready.sem, x3_ready.at(r, 2))
                settle(sp)
                sp.dma_start(x3_dram[tok(r), :].rearrange("(t p) d -> p t d", p=P),
                             x1[:, :, :]).then_inc(stored_round, 16)
                for j in range(2):
                    sp.wait_ge(*plan.drained(("SD", j), r))
                settle(sp)
                sp.dma_start(sh_dram[tok(r), :].rearrange("(t p) d -> p t d", p=P),
                             tmp[:, :, :]).then_inc(stored_round, 16)

            with sp.Fori(0, ROUNDS - 1) as r:
                sp.wait_ge(x_free.sem, x_free.at(r, 2))
                settle(sp)
                sp.dma_start(xin[:, :, :], A["x"][bass.ds(r * GROUP + GROUP, GROUP), :]
                             .rearrange("(t p) d -> p t d", p=P)).then_inc(x_in, 16)
                store(r)
            sp.wait_ge(x_free.sem, x_free.at(ROUNDS - 1, 2))
            sp.dma_start(xin[:, :, :], A["x"][0:GROUP, :].rearrange("(t p) d -> p t d", p=P)).then_inc(x_in, 16)
            for s in range(ESLOTS):
                load_experts(sp, s, s)
            store(ROUNDS - 1)
            sp.wait_ge(x_in, 16 * (ROUNDS + 1))
            tail_sync(sp)

        def transposes(pe, stage, n, src, j, r):
            key = ("T", stage, j)
            if n == 0:
                pe.wait_ge(mix_ready.sem, mix_ready.at(r + 1, 1 + j))
            else:
                pe.wait_ge(u_ready.sem, u_ready.at(r, 2 * n - 1 + j))
            pe.wait_ge(*plan.before(key, r))
            for c in range(DC):
                for i in range(2):
                    mm = pe.transpose(plan[key][:, c * HALF + i * P:c * HALF + (i + 1) * P],
                                      src[:, 2 * j + i, c * P:(c + 1) * P], ident[:, :])
            mm.then_inc(plan.fills(key), 1)

        def linear(pe, key, w, cols, r):
            pe.wait_ge(*plan.before(key, r))
            n = cols.stop - cols.start
            for k in range(DC):
                mm = pe.matmul(plan[key][0:n, :], w[:, k, cols], uT[:, k, :], start=k == 0, stop=k == DC - 1)
            mm.then_inc(plan.fills(key), 1)

        def first_linears(pe, stage, parts, r, turned_round):
            for j in range(2):
                pe.wait_ge(*plan.drained(("T", stage, j), turned_round))
                tokens = slice(j * HALF, (j + 1) * HALF)
                for key, w, cols in parts:
                    if j == 0:
                        pe.wait_ge(*plan.before(key, r))
                    n = cols.stop - cols.start
                    for k in range(DC):
                        mm = pe.matmul(plan[key][0:n, tokens], w[:, k, cols], uT[:, k, tokens],
                                       start=k == 0, stop=k == DC - 1)
                    if j == 1:
                        mm.then_inc(plan.fills(key), 1)

        def on_diagonal(bank):
            return bank[:, :].rearrange("p (b n) -> p b n", n=P)[:, 0:3:2, :]

        def head_of(p, e):
            return 4 * (2 * (p // 4) + e) + p % 4

        def x_block(t, q, hq):
            return x_pad[:, t, q * P + 32 * hq:q * P + 32 * (hq + 1)]

        def head_rows(h):
            return slice(32 * (h // 2 % 4), 32 * (h // 2 % 4) + 32)

        @block.tensor
        def _(pe):
            pe.wait_ge(consts_in, 160)
            for j in range(2):
                transposes(pe, "mix", 0, u, j, -1)
            pe.wait_ge(consts_cast, 1)
            pe.wait_ge(w_proj[0], 16)
            with pe.Fori(0, ROUNDS) as r:
                x_cols = [slice(D + c * P, D + (c + 1) * P) for c in range(DC)]
                first_linears(pe, "mix", [("dt", w_in, slice(2 * D, 2 * D + HEADS)), (("X", 0), w_in, x_cols[0])],
                              r, r - 1)
                linear(pe, ("X", 1), w_in, x_cols[1], r)

                def project_bc(p, w):
                    o = 2 * D + HEADS + (2 * p + w) * P
                    linear(pe, ("BC", p, w), w_in, slice(o, o + P), r)

                pe.wait_ge(w_proj[1], 16)
                for w in range(2):
                    project_bc(0, w)
                pe.wait_ge(cum_ready.sem, cum_ready.at(r, 1))
                pe.wait_ge(*plan.before("cumT", r))
                settle(pe)
                for t in range(TILES):
                    mm = pe.transpose(plan["cumT"][:, t * HEADS:(t + 1) * HEADS],
                                      cumP[:, t * P:(t + 1) * P], ident[0:HEADS, 0:HEADS])
                mm.then_inc(plan.fills("cumT"), 1)
                for c in range(DC):
                    linear(pe, ("Z", c), w_in, slice(c * P, (c + 1) * P), r)
                for w in range(2):
                    project_bc(1, w)
                for c in range(DC):
                    pe.wait_ge(*plan.drained(("X", c), r))
                    pe.wait_ge(*plan.before(("XT", c), r))
                    for t in range(TILES):
                        mm = pe.transpose(plan[("XT", c)][:, t * P:(t + 1) * P],
                                          xc[:, c, t * P:(t + 1) * P], ident[:, :])
                    mm.then_inc(plan.fills(("XT", c)), 1)
                pe.wait_ge(cum3_ready.sem, cum3_ready.at(r, 1))

                def decays(n):
                    p, b, e = uses[n]
                    key = ("A", p, b, e)
                    pe.wait_ge(*plan.before(key, r))
                    h = head_of(p, e)
                    pe.matmul(plan[key][:, 0:TRI], neg_sel[:, h:h + 1].broadcast_to([96, P]),
                              cum3[:, b, :], start=True, stop=False)
                    pe.matmul(on_diagonal(plan[key]), ident_bf[:, :], keyq_mask[:, :], start=False,
                              stop=True).then_inc(plan.fills(key), 1)

                def products(n):
                    p, b, e = uses[n]
                    key = ("CB", p, b, e)
                    rows = slice(e * STATE, (e + 1) * STATE)
                    B, C = bc[rows, p % 3, 0, :], bc[rows, p % 3, 1, :]
                    o = b * SEQ
                    pe.matmul(plan[key][:, 0:SEQ], B[:, o:o + P], C[:, o:o + SEQ], start=True, stop=True)
                    return key, lambda: pe.matmul(plan[key][:, SEQ:TRI], B[:, o + P:o + SEQ],
                                                  C[:, o + P:o + SEQ], start=True, stop=True)

                def add_y(ns):
                    for n in ns:
                        pe.wait_ge(*plan.drained(("CB", *uses[n]), r))
                    for i in range(2):
                        for n in ns:
                            p, b, e = uses[n]
                            q, hq = divmod(head_of(p, e), 4)
                            y = plan[("Y", q // 4)][32 * (q % 4):32 * (q % 4) + 32, :]
                            s = sc[:, n % 4, :]
                            o = b * SEQ
                            if i == 0:
                                pe.matmul(y[:, o:o + SEQ], x_block(2 * b, q, hq), s[:, 0:SEQ],
                                          start=False, stop=False, skip_group_check=True)
                            else:
                                pe.matmul(y[:, o + P:o + SEQ], x_block(2 * b + 1, q, hq),
                                          s[:, SEQ:TRI], start=False, stop=True,
                                          skip_group_check=True).then_inc(y_added.sem, 1)

                for g in range(2 * PAIRS):
                    p, b = divmod(g, SEQS)
                    ns = (2 * g, 2 * g + 1)
                    for n in ns:
                        decays(n)
                    if b == 0:
                        for w in range(2):
                            pe.wait_ge(*plan.drained(("BC", p, w), r))
                    for n in ns:
                        pe.wait_ge(*plan.before(("CB", *uses[n]), r))
                    for key, second in [products(n) for n in ns]:
                        second().then_inc(plan.fills(key), 1)
                    if p + 2 < PAIRS:
                        if p + 2 == PROJ_PAIRS[1] and b == 0:
                            pe.wait_ge(w_proj[2], 16)
                        project_bc(p + 2, b)
                    if g == 1:
                        for c in range(DC):
                            pe.wait_ge(*plan.before(("Y", c), r))
                            pe.matmul(plan[("Y", c)][:, :], zeros_bf[:, 0:P], zeros_bf[:, :], start=True,
                                      stop=False, skip_group_check=True).then_inc(plan.fills(("Y", c)), 1)
                    if g >= 1:
                        add_y((2 * g - 2, 2 * g - 1))
                add_y((62, 63))

                pe.wait_ge(w_sem["out"], 16)
                for j in range(2):
                    pe.wait_ge(*plan.before(("O", j), r))
                for c in range(DC):
                    pe.wait_ge(yg_ready.sem, yg_ready.at(r, c + 1))
                    for j in range(2):
                        for i in range(2):
                            t = 2 * j + i
                            mm = pe.matmul(plan[("O", j)][:, i * D:(i + 1) * D], yg[:, c, t * P:(t + 1) * P],
                                           w_out[:, c, :], start=c == 0 and i == 0, stop=c == DC - 1,
                                           skip_group_check=True)
                        if c == DC - 1:
                            mm.then_inc(plan.fills(("O", j)), 1)

                for j in range(2):
                    transposes(pe, "ffn", 1, u, j, r)
                pe.wait_ge(w_sem["ffn"], 32)
                first_linears(pe, "ffn", [(("G", 0), w_gu, slice(0, P)), (("U", 0), w_gu, slice(FF, FF + P))],
                              r, r)
                for f in range(1, FF // P):
                    linear(pe, ("G", f), w_gu, slice(f * P, (f + 1) * P), r)
                    linear(pe, ("U", f), w_gu, slice(FF + f * P, FF + (f + 1) * P), r)
                for f in range(FF // P - 2, FF // P):
                    pe.wait_ge(*plan.drained(("U", f), r))
                for j in range(2):
                    pe.wait_ge(*plan.before(("F", j), r))
                    for i in range(2):
                        t = 2 * j + i
                        for f in range(FF // P):
                            mm = pe.matmul(plan[("F", j)][:, i * D:(i + 1) * D], hf[:, f, t * P:(t + 1) * P],
                                           w_dn[:, f, :], start=f == 0, stop=f == FF // P - 1)
                    mm.then_inc(plan.fills(("F", j)), 1)

                pe.wait_ge(w_sem["lora"], 32)
                for j in range(2):
                    transposes(pe, "lora", 2, u, j, r)
                    pe.wait_ge(*plan.drained(("T", "lora", j), r))
                    for t in (2 * j, 2 * j + 1):
                        pe.wait_ge(*plan.before(("L", t), r))
                        for k in range(DC):
                            mm = pe.matmul(plan[("L", t)][:, 0:LW], uT[:, k, t * P:(t + 1) * P],
                                           w_lora[:, k, :], start=k == 0, stop=k == DC - 1)
                        mm.then_inc(plan.fills(("L", t)), 1)
                for j in range(2):
                    pe.wait_ge(hw_ready.sem, hw_ready.at(r, j + 1))
                    pe.wait_ge(*plan.before(("LT", j), r))
                    for i in range(2):
                        mm = pe.transpose(plan[("LT", j)][:, i * P:(i + 1) * P], hw[:, 2 * j + i, :], ident[:, :])
                    mm.then_inc(plan.fills(("LT", j)), 1)
                    pe.wait_ge(*plan.drained(("LT", j), r))
                    for t in (2 * j, 2 * j + 1):
                        pe.matmul(plan[("L", t)][:, 0:D], hwT[:, t * P:(t + 1) * P], w_lb[:, :],
                                  start=False, stop=True, skip_group_check=True).then_inc(lora_added.sem, 1)

                pe.wait_ge(w_sem["att"], 32)
                for j in range(2):
                    transposes(pe, "att", 3, u, j, r)
                    pe.wait_ge(*plan.drained(("T", "att", j), r))
                    cols = slice(j * HALF, (j + 1) * HALF)
                    for c in range(DC):
                        for n, key in enumerate((("Q", c), ("K", c))):
                            if j == 0:
                                pe.wait_ge(*plan.before(key, r))
                            for k in range(DC):
                                mm = pe.matmul(plan[key][:, cols], w_att[:, k, n, c * P:(c + 1) * P],
                                               uT[:, k, cols], start=k == 0, stop=k == DC - 1)
                            if j == 1:
                                mm.then_inc(plan.fills(key), 1)
                    pe.wait_ge(*plan.before(("V", j), r))
                    for i in range(2):
                        t = 2 * j + i
                        for k in range(DC):
                            mm = pe.matmul(plan[("V", j)][:, i * D:(i + 1) * D], uT[:, k, t * P:(t + 1) * P],
                                           w_att[:, k, 2, :], start=k == 0, stop=k == DC - 1)
                    mm.then_inc(plan.fills(("V", j)), 1)
                for b in range(SEQS):
                    pe.wait_ge(*plan.before(("OT", b), r))
                    pe.matmul(plan[("OT", b)][:, :], zeros_bf[:, 0:P], zeros_bf[:, :], start=True,
                              stop=False, skip_group_check=True).then_inc(plan.fills(("OT", b)), 1)

                def scores(ns):
                    for n in ns:
                        pe.wait_ge(*plan.before(("S", n), r))
                    for i in range(2):
                        for n in ns:
                            h, b = auses[n]
                            rows, o = head_rows(h), b * SEQ
                            q = qT[rows, h // 8, o:o + SEQ]
                            k = kT[h % 2][rows, h // 8, o:o + SEQ]
                            if i == 0:
                                pe.matmul(plan[("S", n)][:, 0:P], q[:, 0:P], k[:, 0:P], start=True,
                                          stop=False, skip_group_check=True)
                            else:
                                pe.matmul(plan[("S", n)][:, P:TRI], q[:, P:SEQ], k[:, 0:SEQ],
                                          start=False, stop=False, skip_group_check=True)
                    for n in ns:
                        pe.matmul(on_diagonal(plan[("S", n)]), ident_bf[:, :], qkey_mask[:, :], start=False,
                                  stop=True, skip_group_check=True).then_inc(plan.fills(("S", n)), 1)

                def turn_probs(n):
                    key = ("PT", n)
                    pe.wait_ge(*plan.before(key, r))
                    pe.wait_ge(probs.sem, probs.at(r, n + 1))
                    for i in range(3):
                        mm = pe.transpose(plan[key][:, i * P:(i + 1) * P], pr[:, n % 6, i * P:(i + 1) * P],
                                          ident[:, :])
                    mm.then_inc(plan.fills(key), 1)

                def add_o(ns):
                    for n in ns:
                        pe.wait_ge(*plan.drained(("PT", n), r))
                    for i in range(2):
                        for n in ns:
                            h, b = auses[n]
                            o = plan[("OT", b)][head_rows(h), h // 8 * SEQ:(h // 8 + 1) * SEQ]
                            s = prT[:, n % 4, :]
                            if i == 0:
                                pe.matmul(o, v_pad[:, 2 * b, h // 2, h % 2, :],
                                          s[:, 0:SEQ], start=False, stop=False, skip_group_check=True)
                            else:
                                pe.matmul(o[:, P:SEQ],
                                          v_pad[:, 2 * b + 1, h // 2, h % 2, :], s[:, SEQ:TRI],
                                          start=False, stop=True, skip_group_check=True)\
                                              .then_inc(o_added.sem, 1)

                def project_o(j):
                    pe.wait_ge(*plan.drained(("OT", j), r))
                    pe.wait_ge(*plan.before(("W", j), r))
                    for i in range(2):
                        t = 2 * j + i
                        for c in range(DC):
                            mm = pe.matmul(plan[("W", j)][:, i * D:(i + 1) * D], oT[:, c, t * P:(t + 1) * P],
                                           w_att[:, c, 3, :], start=c == 0, stop=c == DC - 1)
                    mm.then_inc(plan.fills(("W", j)), 1)

                def route(j):
                    pe.wait_ge(*plan.drained(("T", "moe", j), r))
                    pe.wait_ge(*plan.before(("R", j), r))
                    for i in range(2):
                        t = 2 * j + i
                        for k in range(DC):
                            mm = pe.matmul(plan[("R", j)][:, i * E1:(i + 1) * E1], uT[:, k, t * P:(t + 1) * P],
                                           w_rt[:, k, :], start=k == 0, stop=k == DC - 1)
                    mm.then_inc(plan.fills(("R", j)), 1)

                pe.wait_ge(w_sem["moe"], 64)
                for g in range(16 + 3):
                    if g in (0, 4):
                        pe.wait_ge(*plan.drained(("Q", g // 4), r))
                        pe.wait_ge(*plan.drained(("K", g // 4), r))
                    if g == 3:
                        for j in range(2):
                            pe.wait_ge(*plan.drained(("V", j), r))
                    if g < 16:
                        scores((2 * g, 2 * g + 1))
                    if 2 <= g < 18:
                        turn_probs(2 * g - 4)
                        turn_probs(2 * g - 3)
                    if 3 <= g:
                        add_o((2 * g - 6, 2 * g - 5))
                    if g == 11:
                        project_o(0)
                    if g == 16:
                        transposes(pe, "moe", 4, xf, 0, r)
                    if g == 17:
                        route(0)
                project_o(1)

                def shared_hidden(j):
                    for g in range(SHF // P // 2):
                        for name, o in (("SG", 2 * g * P), ("SU", SHF + 2 * g * P)):
                            key = (name, g, j)
                            pe.wait_ge(*plan.before(key, r))
                            for i in range(2):
                                for k in range(DC):
                                    mm = pe.matmul(plan[key][:, i * HALF:(i + 1) * HALF],
                                                   w_sgu[:, k, o + i * P:o + (i + 1) * P],
                                                   uT[:, k, j * HALF:(j + 1) * HALF],
                                                   start=k == 0, stop=k == DC - 1)
                            mm.then_inc(plan.fills(key), 1)

                def shared_down(j):
                    for g in range(SHF // P // 2):
                        pe.wait_ge(*plan.drained(("SU", g, j), r))
                    pe.wait_ge(*plan.before(("SD", j), r))
                    for i in range(2):
                        t = 2 * j + i
                        for f in range(SHF // P):
                            mm = pe.matmul(plan[("SD", j)][:, i * D:(i + 1) * D], hf[:, f, t * P:(t + 1) * P],
                                           w_sdn[:, f, :], start=f == 0, stop=f == SHF // P - 1)
                    mm.then_inc(plan.fills(("SD", j)), 1)

                shared_hidden(0)
                transposes(pe, "moe", 4, xf, 1, r)
                route(1)
                shared_hidden(1)
                shared_down(0)
                pe.wait_ge(chosen_ready.sem, chosen_ready.at(r, 1))
                pe.wait_ge(*plan.before("pos", r))
                for t in range(TILES):
                    pe.matmul(plan["pos"][:, t * E1:(t + 1) * E1], earlier[:, :], chosen[:, t, :],
                              start=True, stop=False)
                    mm = pe.matmul(plan["pos"][:, t * E1:(t + 1) * E1], ones_bf[:, :], before[:, t, :],
                                   start=False, stop=True)
                mm.then_inc(plan.fills("pos"), 1)
                shared_down(1)
                for j in range(2):
                    transposes(pe, "mix", 0, u, j, r)
            tail_tensor(pe)

        @block.scalar
        def _(act):
            act.wait_ge(consts_in, 160)

            def turned(stage, j, r, scale=None):
                key = ("T", stage, j)
                act.wait_ge(*plan.full(key, r))
                cols = slice(j * HALF, (j + 1) * HALF)
                if scale is None:
                    ins = act.activation(uT[:, :, cols], plan[key][:, :]
                                         .rearrange("p (c n) -> p c n", c=DC), ACT.Copy)
                else:
                    for c in range(DC):
                        ins = act.activation(uT[:, c, cols], plan[key][:, c * HALF:(c + 1) * HALF],
                                             ACT.Copy, scale=chan[:, c, scale:scale + 1])
                ins.then_inc(plan.drains(key), 1)

            for j in range(2):
                turned("mix", j, -1, 2)
            act.wait_ge(consts_cast, 1)
            with act.Fori(0, ROUNDS) as r:
                def first_tap(key, dst, j):
                    act.wait_ge(*plan.full(key, r))
                    act.activation(dst, plan[key][:, :], ACT.Identity, bias=conv_b[:, j:j + 1],
                                   scale=conv_w[:, j, TAPS - 1:TAPS]).then_inc(tap0.sem, 1)

                act.wait_ge(*plan.full("dt", r))
                act.activation(sp_a[:, :], plan["dt"][0:HEADS, :], ACT.Abs).then_inc(dt_abs.sem, 1)
                act.wait_ge(dt_abs.sem, dt_abs.at(r, 1))
                act.activation(sp_b[:, :], sp_a[:, :], ACT.Exp, scale=-1.0).then_inc(exp_dt.sem, 1)
                act.wait_ge(exp_dt.sem, exp_dt.at(r, 1))
                act.activation(sp_a[:, :], sp_b[:, :], ACT.Ln, bias=1.0).then_inc(dt_log.sem, 1)
                for c in range(DC):
                    first_tap(("X", c), xc[:, c, :], c)
                for w in range(2):
                    first_tap(("BC", 0, w), bc[:, 0, w, :], 2 + 16 * w)
                act.wait_ge(*plan.full("cumT", r))
                act.activation(cum_tok[:, :, :], plan["cumT"][:, 0:TILES * HEADS]
                               .rearrange("p (t h) -> p t h", t=TILES), ACT.Copy)\
                                   .then_inc(plan.drains("cumT"), 1)
                for c in range(DC):
                    key = ("Z", c)
                    act.wait_ge(*plan.full(key, r))
                    act.activation(sz[:, c, :], plan[key][:, :], ACT.Silu, bias=chan[:, c, 0:1])\
                        .then_inc(plan.drains(key), 1)
                act.wait_ge(pads_zero, 5)
                for w in range(2):
                    first_tap(("BC", 1, w), bc[:, 1, w, :], 3 + 16 * w)
                for c in range(DC):
                    act.wait_ge(*plan.full(("XT", c), r))
                    src = plan[("XT", c)][:, :].rearrange("p (t q h d) -> p t q h d", t=TILES, q=4, h=4)
                    for q in range(4):
                        o = (4 * c + q) * P
                        dst = x_pad[:, :, o:o + 160].rearrange("p t (h s) -> p t h s", h=4)[:, :, :, 0:8]
                        ins = act.activation(dst, src[:, :, q, :, :], ACT.Copy)
                    ins.then_inc(plan.drains(("XT", c)), 1)
                act.wait_ge(*plan.drained("cumT", r))
                for p in range(PAIRS):
                    for i in range(4):
                        n = 4 * p + i
                        _, b, e = uses[n]
                        h = head_of(p, e)
                        key = ("A", p, b, e)
                        act.wait_ge(*plan.full(key, r))
                        if n >= 4:
                            act.wait_ge(*plan.drained(("CB", *uses[n - 4]), r))
                        act.activation(dec[:, n % 4, 0:SEQ], plan[key][:, 0:SEQ], ACT.Exp,
                                       bias=cum_tok[:, 2 * b, h:h + 1])
                        act.activation(dec[:, n % 4, SEQ:TRI], plan[key][:, SEQ:TRI], ACT.Exp,
                                       bias=cum_tok[:, 2 * b + 1, h:h + 1]).then_inc(plan.drains(key), 1)
                        if e == 1 and p + 2 < PAIRS:
                            first_tap(("BC", p + 2, b), bc[:, (p + 2) % 3, b, :], 2 + 16 * b + p + 2)
                act.wait_ge(stored_round, r * 32 + CREDIT)
                for zeroed, n in ((zero_filled, 16 * (SLOTS // GROUP)), (scattered, CREDIT)):
                    act.wait_ge(zeroed, n)
                for t in range(TILES):
                    if t % 2 == 0:
                        act.wait_ge(*plan.drained(("O", t // 2), r))
                    act.activation(tmp[:, t, :], h1[:, t, :], ACT.Square, scale=1.0 / 16,
                                   accum_out=sm[:, t:t + 1]).then_inc(sumsq.sem, 1)
                for j in range(2):
                    turned("ffn", j, r, 3)

                def silu_gate(gk, uk, f):
                    act.wait_ge(*plan.full((gk, f), r))
                    if f >= 2:
                        act.wait_ge(*plan.drained((uk, f - 2), r))
                    act.activation(sg[:, f % 2, :], plan[(gk, f)][:, :], ACT.Silu)\
                        .then_inc(plan.drains((gk, f)), 1)

                for f in range(FF // P):
                    silu_gate("G", "U", f)
                for j in range(2):
                    turned("lora", j, r)
                    if j == 1:
                        act.wait_ge(lora_top.sem, lora_top.at(r, 1))
                        act.activation(wk[:, H[0], 0:2], wk[:, H[0], 0:2], ACT.Exp).then_inc(lora_exp.sem, 1)
                    for t in (2 * j, 2 * j + 1):
                        act.wait_ge(*plan.full(("L", t), r))
                        act.activation(lg0[:, t, :], plan[("L", t)][:, D:D + EXPERTS0], ACT.Copy)\
                            .then_inc(lora_lg.sem, 1)
                for j in range(2):
                    if j == 1:
                        act.wait_ge(lora_top.sem, lora_top.at(r, 2))
                        act.activation(wk[:, H[1], 0:2], wk[:, H[1], 0:2], ACT.Exp).then_inc(lora_exp.sem, 1)
                    act.wait_ge(*plan.full(("LT", j), r))
                    act.activation(hwT[:, j * HALF:(j + 1) * HALF], plan[("LT", j)][:, 0:HALF],
                                   ACT.Copy).then_inc(plan.drains(("LT", j)), 1)
                for j in range(2):
                    turned("att", j, r)
                for c in range(DC):
                    act.wait_ge(*plan.full(("Q", c), r))
                    act.activation(qT[:, c, :], plan[("Q", c)][:, :], ACT.Identity,
                                   bias=qbias[:, c:c + 1], scale=0.25).then_inc(plan.drains(("Q", c)), 1)
                    act.wait_ge(*plan.full(("K", c), r))
                    act.activation(kT[0][:, c, :], plan[("K", c)][:, :], ACT.Identity,
                                   bias=kbias[:, c, 0:1], scale=parity[:, 0:1])
                    act.activation(kT[1][:, c, :], plan[("K", c)][:, :], ACT.Identity,
                                   bias=kbias[:, c, 1:2], scale=parity[:, 1:2])\
                                       .then_inc(plan.drains(("K", c)), 1)

                def outputs(b):
                    act.wait_ge(o_added.sem, o_added.at(r, 16 * (b + 1)))
                    act.activation(oT[:, :, b * SEQ:(b + 1) * SEQ], plan[("OT", b)][:, :]
                                   .rearrange("p (c n) -> p c n", c=DC), ACT.Copy)\
                                       .then_inc(plan.drains(("OT", b)), 1)

                for n in range(32 + 4):
                    if n < 32:
                        act.wait_ge(nmax_ready.sem, nmax_ready.at(r, n + 1))
                        if n >= 6:
                            act.wait_ge(*plan.full(("PT", n - 6), r))
                        for i, cols in enumerate((slice(0, P), slice(P, TRI))):
                            ins = act.activation(pr[:, n % 6, cols], plan[("S", n)][:, cols], ACT.Exp,
                                                 bias=nmax[:, n % 4, i:i + 1], accum_out=esum[:, n % 4, i:i + 1])
                        ins.then_inc(plan.drains(("S", n)), 1)
                    if n >= 4:
                        m = n - 4
                        act.wait_ge(*plan.full(("PT", m), r))
                        if m >= 4:
                            act.wait_ge(o_added.sem, o_added.at(r, m - 3))
                        act.activation(prT[:, m % 4, :], plan[("PT", m)][:, 0:TRI], ACT.Copy)\
                            .then_inc(plan.drains(("PT", m)), 1)
                    if n == 22:
                        outputs(0)
                    if n == 34:
                        turned("moe", 0, r)
                outputs(1)

                def shared_silu(j):
                    for g in range(SHF // P // 2):
                        act.wait_ge(*plan.full(("SG", g, j), r))
                        if j == 1:
                            act.wait_ge(*plan.drained(("SU", g, 0), r))
                        act.activation(sg[:, g, :], plan[("SG", g, j)][:, :], ACT.Silu)\
                            .then_inc(plan.drains(("SG", g, j)), 1)

                def shared_sum(j):
                    act.wait_ge(*plan.full(("SD", j), r))
                    act.activation(tmp[:, H[j], :], plan[("SD", j)][:, :]
                                   .rearrange("p (t d) -> p t d", t=2), ACT.Copy)\
                                       .then_inc(plan.drains(("SD", j)), 1)

                shared_silu(0)
                turned("moe", 1, r)
                shared_silu(1)
                shared_sum(0)
                for j in range(2):
                    turned("mix", j, r, 2)
                shared_sum(1)
                act.wait_ge(top_ready.sem, top_ready.at(r, 1))
                act.activation(wk[:, :, :], lk[:, :, :], ACT.Exp).then_inc(top_exp.sem, 1)
                act.wait_ge(sidx_ready.sem, sidx_ready.at(r, 1))
                settle(act)
            tail_scalar(act)

        @block.gpsimd
        def _(pool):
            def power(n, cols, r):
                pool.wait_ge(var_ready.sem, var_ready.at(r, n))
                pool.tensor_tensor(rs[:, cols], ve[:, cols], half[:, cols], ALU.pow).then_inc(rstd_ready.sem, 1)

            def ahead_powers(r):
                for n in (1, 2):
                    pool.wait_ge(ahead_var.sem, ahead_var.at(r, n))
                    pool.tensor_tensor(rs1[:, :], ve1[:, :], half[:, :], ALU.pow).then_inc(ahead_rstd.sem, 1)

            pool.memset(half[:, :], -0.5).then_inc(pads_zero, 1)
            pool.wait_ge(pads_zero, 1)
            ahead_powers(0)
            pool.memset(tmp[:, :, :], 0.0).then_inc(pads_zero, 1)
            pool.memset(x_pad[:, :, :], 0.0).then_inc(pads_zero, 1)
            pool.memset(v_pad[:, :, :, :, :], 0.0).then_inc(pads_zero, 1)
            pool.memset(before[:, :, :], 0.0).then_inc(pads_zero, 1)
            pool.wait_ge(pads_zero, 5)
            pool.dma_start(xg_dram[SLOTS - GROUP:SLOTS, :].rearrange("(t p) d -> p t d", p=P),
                           tmp[:, :, :]).then_inc(scattered, CREDIT)

            with pool.Fori(0, ROUNDS) as r:
                for n, cols in enumerate(POWERS):
                    if n == len(POWERS) - 4:
                        ahead_powers(r + 1)
                    power(n + 1, cols, r)
                pool.wait_ge(sidx_ready.sem, sidx_ready.at(r, 1))
                settle(pool)
                pool.wait_ge(zero_filled, 16 * (SLOTS // GROUP))
                pool.wait_ge(scattered, CREDIT)
                for i in range(TILES * TOPK):
                    pool.indirect_dma_start(
                        out=xg_dram, out_offset=bass.IndirectOffsetOnAxis(ap=sidx[:, i:i + 1], axis=0),
                        in_=xf[:, i // TOPK, :], in_offset=None, bounds_check=SLOTS - 1,
                        oob_is_err=False).then_inc(scattered, 16)
            tail_pool(pool)

        @block.vector
        def _(dve):
            def ahead_link(ins, n, r):
                ins.then_inc(ahead_chain.sem, 1)
                dve.wait_ge(ahead_chain.sem, ahead_chain.at(r, n))

            def ahead_stats(r):
                dve.wait_ge(x_in, r * 16 + 16)
                for t in range(TILES):
                    ins = dve.bn_stats(stats1[:, t, :], xin[:, t, :])
                ahead_link(ins, 1, r)

            def ahead_moments(r):
                settle(dve)
                for t in range(TILES):
                    ins = dve.bn_aggr(mv1[:, t, :], stats1[:, t, :])
                ahead_link(ins, 2, r)
                dve.tensor_scalar(ve1[:, :], mv1[:, :, 1], EPS, None, ALU.add).then_inc(ahead_var.sem, 1)

            def ahead_second_variance(r):
                dve.wait_ge(ahead_rstd.sem, ahead_rstd.at(r, 1))
                ahead_link(dve.tensor_copy(r1[:, :], rs1[:, :]), 3, r)
                ahead_link(dve.tensor_tensor(sm1[:, :], mv1[:, :, 1], r1[:, :], ALU.mult), 4, r)
                ahead_link(dve.tensor_tensor(sm1[:, :], sm1[:, :], r1[:, :], ALU.mult), 5, r)
                dve.tensor_scalar(ve1[:, :], sm1[:, :], EPS, None, ALU.add).then_inc(ahead_var.sem, 1)

            def ahead_layernorm(r, j):
                for t in (2 * j, 2 * j + 1):
                    ins = dve.tensor_scalar(hn[:, t, :], xin[:, t, :], mv1[:, t, 0:1], r1[:, t:t + 1],
                                            ALU.subtract, ALU.mult)
                ins.then_inc(ahead_chain.sem, 1)

            def ahead_rmsnorm(r, j):
                dve.wait_ge(ahead_rstd.sem, ahead_rstd.at(r, 2))
                dve.wait_ge(ahead_chain.sem, ahead_chain.at(r, 6 + j))
                for t in (2 * j, 2 * j + 1):
                    ins = dve.tensor_scalar(u[:, t, :], hn[:, t, :], rs1[:, t:t + 1], None, ALU.mult)
                ins.then_inc(mix_ready.sem, 1)

            ahead_stats(0)
            ahead_moments(0)
            ahead_second_variance(0)
            for j in range(2):
                ahead_layernorm(0, j)
            for j in range(2):
                ahead_rmsnorm(0, j)
            dve.wait_ge(consts_in, 160)
            dve.tensor_copy(ident_bf[:, :], ident[:, :])
            dve.tensor_copy(keyq_mask[:, :], cstage[:, 0, 0:2 * P])
            dve.tensor_copy(qkey_mask[:, :], cstage[:, 1, 0:2 * P])
            dve.tensor_copy(earlier[:, :], cstage[:, 0, TRI:512])
            dve.memset(ones_bf[:, :], 1.0)
            dve.memset(zeros_bf[:, :], 0.0)
            dve.memset(ones[:, :], 1.0)
            dve.tensor_copy(neg_sel[:, :], neg_in[:, :])
            for c in range(DC):
                for e in range(2):
                    dve.tensor_tensor(kbias[:, c, e:e + 1], chan[:, c, 5:6], parity[:, e:e + 1], ALU.mult)
                dve.tensor_scalar(qbias[:, c:c + 1], chan[:, c, 4:5], 0.25, None, ALU.mult)
            dve.memset(stats[:, 0, 0:1], 0.0).then_inc(consts_cast, 1)
            dve.wait_ge(consts_cast, 1)
            dve.wait_ge(pads_zero, 5)
            with dve.Fori(0, ROUNDS) as r:
                count = [0]

                def link(ins):
                    count[0] += 1
                    ins.then_inc(chain.sem, 1)
                    dve.wait_ge(chain.sem, chain.at(r, count[0]))

                norms = [0]

                def ask(variance, cols):
                    norms[0] += 1
                    dve.tensor_scalar(ve[:, cols], variance, EPS, None, ALU.add).then_inc(var_ready.sem, 1)

                def answered():
                    dve.wait_ge(rstd_ready.sem, rstd_ready.at(r, norms[0]))

                def inv_std(variance, cols):
                    ask(variance, cols)
                    answered()

                def moments(srcs, cols):
                    for t, s in zip(range(cols.start, cols.stop), srcs):
                        ins = dve.bn_stats(stats[:, t, :], s)
                    link(ins)
                    settle(dve)
                    for t in range(cols.start, cols.stop):
                        ins = dve.bn_aggr(mv[:, t, :], stats[:, t, :])
                    link(ins)

                def norm(srcs, dst, cols):
                    moments(srcs, cols)
                    inv_std(mv[:, cols, 1], cols)
                    return normed(srcs, dst, cols)

                def normed(srcs, dst, cols):
                    for t, s in zip(range(cols.start, cols.stop), srcs):
                        ins = dve.tensor_scalar(dst[:, t, :], s, mv[:, t, 0:1], rs[:, t:t + 1],
                                                ALU.subtract, ALU.mult)
                    return ins

                def add_scaled(j, srcs, base):
                    for t, s in zip((2 * j, 2 * j + 1), srcs):
                        ins = dve.scalar_tensor_tensor(x1[:, t, :], s, rs[:, t:t + 1], base[:, t, :],
                                                       ALU.mult, ALU.add)
                    return ins

                def keep_shift(j):
                    link(dve.tensor_tensor(shift[:, H[j]], mv[:, H[j], 0], rs[:, H[j]], ALU.mult))

                def take_shift(j, stage):
                    dve.wait_ge(u_ready.sem, u_ready.at(r, 2 * stage + j + 1))
                    for t in (2 * j, 2 * j + 1):
                        ins = dve.tensor_scalar(x1[:, t, :], x1[:, t, :], shift[:, t:t + 1], None, ALU.subtract)
                    return ins

                def tiles(x, cols):
                    return [x[:, t, :] for t in range(cols.start, cols.stop)]

                taps_done = [0]

                def tap(s, chunks):
                    for n, (key, dst, j) in enumerate(chunks):
                        if s == 1:
                            taps_done[0] += 1
                            dve.wait_ge(tap0.sem, tap0.at(r, taps_done[0]))
                        else:
                            dve.wait_ge(chain.sem, chain.at(r, last_tap[0]))
                    for n, (key, dst, j) in enumerate(chunks):
                        d = dst.rearrange("p (b l) -> p b l", b=SEQS)[:, :, s:SEQ]
                        x = plan[key][:, :].rearrange("p (b l) -> p b l", b=SEQS)[:, :, 0:SEQ - s]
                        ins = dve.scalar_tensor_tensor(d, x, conv_w[:, j, TAPS - 1 - s:TAPS - s], d,
                                                       ALU.mult, ALU.add)
                        if s < TAPS - 1:
                            ins.then_inc(chain.sem, 1)
                            count[0] += 1
                            last_tap[0] = count[0]
                        else:
                            ins.then_inc(plan.drains(key), 1)

                last_tap = [0]

                def bc_chunk(p, w):
                    return (("BC", p, w), bc[:, p % 3, w, :], 2 + 16 * w + p)

                dve.wait_ge(*plan.full("dt", r))
                dt = plan["dt"][0:HEADS, :]
                dve.wait_ge(dt_log.sem, dt_log.at(r, 1))
                dve.scalar_tensor_tensor(sp_b[:, :], dt, 0.0, sp_a[:, :], ALU.max, ALU.add)\
                    .then_inc(plan.drains("dt"), 1)
                dve.wait_ge(*plan.drained("dt", r))
                for b in range(SEQS):
                    ins = dve.tensor_tensor_scan(cumP[:, b * SEQ:(b + 1) * SEQ], ones[0:HEADS, :],
                                                 sp_b[:, b * SEQ:(b + 1) * SEQ], 0.0, ALU.mult, ALU.add)
                ins.then_inc(cum_ready.sem, 1)
                dve.wait_ge(cum_ready.sem, cum_ready.at(r, 1))
                by_seq = cumP[:, :].rearrange("p (b l) -> p b l", b=SEQS)
                rest = sp_a[:, :].rearrange("p (b l) -> p b l", b=SEQS)
                mid = mid0[:, :].rearrange("p (b l) -> p b l", b=SEQS)
                link(dve.tensor_copy(cum3[0:HEADS, :, 0:SEQ], by_seq))
                link(dve.tensor_tensor(rest, by_seq, cum3[0:HEADS, :, 0:SEQ], ALU.subtract))
                link(dve.tensor_copy(mid, rest))
                dve.tensor_copy(cum3[HEADS:2 * HEADS, :, 0:SEQ], mid)
                link(dve.tensor_tensor(rest, rest, mid, ALU.subtract))
                link(dve.tensor_copy(cum3[2 * HEADS:96, :, 0:SEQ], rest))
                dve.tensor_copy(cum3[:, :, SEQ:TRI], cum3[:, :, P:SEQ]).then_inc(cum3_ready.sem, 1)
                for s in range(1, TAPS):
                    tap(s, [(("X", c), xc[:, c, :], c) for c in range(DC)])
                for s in range(1, TAPS):
                    tap(s, [bc_chunk(0, w) for w in range(2)])
                for s in range(1, TAPS - 1):
                    tap(s, [bc_chunk(1, w) for w in range(2)])

                def output(c):
                    dve.wait_ge(y_added.sem, y_added.at(r, 32 * (c + 1)))
                    dve.scalar_tensor_tensor(yg[:, c, :], xc[:, c, :], chan[:, c, 1:2], plan[("Y", c)][:, :],
                                             ALU.mult, ALU.add).then_inc(plan.drains(("Y", c)), 1)
                    dve.wait_ge(*plan.drained(("Y", c), r))
                    dve.tensor_tensor(yg[:, c, :], yg[:, c, :], sz[:, c, :], ALU.mult).then_inc(yg_ready.sem, 1)

                for n in range(4 * PAIRS):
                    if n == 2 * PAIRS + 6:
                        output(0)
                    p, b, e = uses[n]
                    key = ("CB", p, b, e)
                    dve.wait_ge(*plan.drained(("A", p, b, e), r))
                    dve.wait_ge(*plan.full(key, r))
                    if n >= 4:
                        dve.wait_ge(y_added.sem, y_added.at(r, n - 3))
                    dve.tensor_tensor(sc[:, n % 4, :], dec[:, n % 4, :], plan[key][:, 0:TRI],
                                      ALU.mult).then_inc(plan.drains(key), 1)
                    if n == 1:
                        tap(TAPS - 1, [bc_chunk(1, w) for w in range(2)])
                    if e == 1 and n >= 2 and uses[n - 2][0] + 2 < PAIRS:
                        tap(2, [bc_chunk(uses[n - 2][0] + 2, uses[n - 2][1])])
                        tap(3, [bc_chunk(uses[n - 2][0] + 2, uses[n - 2][1])])
                    if e == 1 and p + 2 < PAIRS:
                        tap(1, [bc_chunk(p + 2, b)])
                output(1)

                def half_of(x, j):
                    return x[:, 2 * j:2 * j + 2, :].rearrange("p t d -> p (t d)")

                for j in range(2):
                    dve.wait_ge(*plan.full(("O", j), r))
                    dve.tensor_tensor(half_of(h1, j), plan[("O", j)][:, :], half_of(hn, j), ALU.add)\
                        .then_inc(plan.drains(("O", j)), 1)
                for j in range(2):
                    dve.wait_ge(sumsq.sem, sumsq.at(r, 2 * j + 2))
                    inv_std(sm[:, H[j]], H[j])
                    for t in (2 * j, 2 * j + 1):
                        ins = dve.tensor_scalar(u[:, t, :], h1[:, t, :], rs[:, t:t + 1], None, ALU.mult)
                    ins.then_inc(u_ready.sem, 1)

                def gate(gk, uk, f):
                    dve.wait_ge(*plan.drained((gk, f), r))
                    dve.wait_ge(*plan.full((uk, f), r))
                    dve.tensor_tensor(hf[:, f, :], sg[:, f % 2, :], plan[(uk, f)][:, :], ALU.mult)\
                        .then_inc(plan.drains((uk, f)), 1)

                for f in range(FF // P):
                    gate("G", "U", f)
                for j in range(2):
                    dve.wait_ge(*plan.full(("F", j), r))
                    dve.tensor_tensor(half_of(h1, j), plan[("F", j)][:, :], half_of(h1, j), ALU.add)\
                        .then_inc(plan.drains(("F", j)), 1)
                    dve.wait_ge(*plan.drained(("F", j), r))
                    moments(tiles(h1, H[j]), H[j])
                    inv_std(mv[:, H[j], 1], H[j])
                    add_scaled(j, tiles(h1, H[j]), xin).then_inc(x_free.sem, 1)
                    dve.wait_ge(x_free.sem, x_free.at(r, j + 1))
                    keep_shift(j)
                    norm(tiles(x1, H[j]), u, H[j]).then_inc(u_ready.sem, 1)
                for j in range(2):
                    dve.wait_ge(lora_lg.sem, lora_lg.at(r, 2 * j + 2))
                    settle(dve)
                    for t in (2 * j, 2 * j + 1):
                        ins = dve.max(mx[:, t, :], lg0[:, t, :])
                    link(ins)
                    settle(dve)
                    dve.tensor_tensor(wk[:, H[j], 0:2], mx[:, H[j], 0:2],
                                      mx[:, H[j], 0:1].broadcast_to([P, 2, 2]), ALU.subtract)\
                                          .then_inc(lora_top.sem, 1)
                    for t in (2 * j, 2 * j + 1):
                        ins = dve.max_index(ix[:, t, :], mx[:, t, :], lg0[:, t, :])
                    link(ins)
                    link(dve.tensor_copy(ixf[:, H[j], 0:2], ix[:, H[j], 0:2]))
                    dve.tensor_tensor(oh0[:, H[j], :, :],
                                      ixf[:, H[j], 0:2].unsqueeze(3).broadcast_to([P, 2, 2, EXPERTS0]),
                                      iota[:, 0:EXPERTS0].unsqueeze(1).unsqueeze(1)
                                      .broadcast_to([P, 2, 2, EXPERTS0]), ALU.is_equal)
                    dve.wait_ge(lora_exp.sem, lora_exp.at(r, j + 1))
                    link(dve.tensor_tensor(wsum[:, H[j]], wk[:, H[j], 0], wk[:, H[j], 1], ALU.add))
                    link(dve.reciprocal(wsum[:, H[j]], wsum[:, H[j]]))
                    link(dve.scalar_tensor_tensor(wk[:, H[j], 0:2], wk[:, H[j], 0:2], LORA_ALPHA,
                                                  wsum[:, H[j]].unsqueeze(2).broadcast_to([P, 2, 2]),
                                                  ALU.mult, ALU.mult))
                    link(dve.tensor_tensor(oh0[:, H[j], :, :], oh0[:, H[j], :, :],
                                           wk[:, H[j], 0:2].unsqueeze(3).broadcast_to([P, 2, 2, EXPERTS0]),
                                           ALU.mult))
                    link(dve.tensor_tensor(wm[:, H[j], :], oh0[:, H[j], 0, :], oh0[:, H[j], 1, :], ALU.add))
                    for t in (2 * j, 2 * j + 1):
                        ins = dve.tensor_tensor(
                            hw[:, t, :].rearrange("p (e r) -> p e r", e=EXPERTS0),
                            plan[("L", t)][:, D + EXPERTS0:LW].rearrange("p (e r) -> p e r", e=EXPERTS0),
                            wm[:, t, :].unsqueeze(2).broadcast_to([P, EXPERTS0, RANK]), ALU.mult)
                    ins.then_inc(hw_ready.sem, 1)
                    if j == 0:
                        for i in range(2):
                            link(take_shift(i, 1))
                for j in range(2):
                    dve.wait_ge(lora_added.sem, lora_added.at(r, 2 * j + 2))
                    moments([plan[("L", t)][:, 0:D] for t in (2 * j, 2 * j + 1)], H[j])
                    inv_std(mv[:, H[j], 1], H[j])
                    for t in (2 * j, 2 * j + 1):
                        dve.scalar_tensor_tensor(x1[:, t, :], plan[("L", t)][:, 0:D], rs[:, t:t + 1], x1[:, t, :],
                                                 ALU.mult, ALU.add).then_inc(plan.drains(("L", t)), 1)
                    for t in (2 * j, 2 * j + 1):
                        dve.wait_ge(*plan.drained(("L", t), r))
                    keep_shift(j)
                    norm(tiles(x1, H[j]), u, H[j]).then_inc(u_ready.sem, 1)
                for j in range(2):
                    link(take_shift(j, 2))
                by_head = att_rows[:, 0, :].rearrange("p (g e d) -> p g e d", e=2, d=DK)
                for j in range(2):
                    dve.wait_ge(*plan.full(("V", j), r))
                    for i in range(2):
                        src = plan[("V", j)][:, i * D:(i + 1) * D].rearrange("p (g e d) -> p g e d", e=2, d=DK)
                        for e in range(2):
                            ins = dve.tensor_tensor(v_pad[:, 2 * j + i, :, e, DK * e:DK * e + DK],
                                                    src[:, :, e, :], by_head[:, :, e, :], ALU.add)
                    ins.then_inc(plan.drains(("V", j)), 1)

                def attended(j):
                    dve.wait_ge(*plan.full(("W", j), r))
                    dve.tensor_tensor(h1[:, H[j], :],
                                      plan[("W", j)][:, :].rearrange("p (t d) -> p t d", t=2),
                                      att_rows[:, 1, :].unsqueeze(1).broadcast_to([P, 2, D]),
                                      ALU.add).then_inc(plan.drains(("W", j)), 1)

                def attended_moments(j):
                    dve.wait_ge(*plan.drained(("W", j), r))
                    moments(tiles(h1, H[j]), H[j])
                    ask(mv[:, H[j], 1], H[j])

                def attended_norm(j):
                    answered()
                    link(add_scaled(j, tiles(h1, H[j]), x1))

                def routed_moments(j):
                    keep_shift(j)
                    moments(tiles(x1, H[j]), H[j])
                    ask(mv[:, H[j], 1], H[j])

                def routed_norm(j):
                    answered()
                    if j == 0:
                        dve.wait_ge(scattered, r * (TILES * TOPK * 16) + CREDIT)
                    normed(tiles(x1, H[j]), xf, H[j]).then_inc(u_ready.sem, 1)

                for n in range(32 + 1):
                    if n == 2:
                        ahead_stats(r + 1)
                    if n == 4:
                        ahead_moments(r + 1)
                    if n == 6:
                        ahead_second_variance(r + 1)
                    if n in (8, 10):
                        ahead_layernorm(r + 1, (n - 8) // 2)
                    if n in (12, 14):
                        ahead_rmsnorm(r + 1, (n - 12) // 2)
                    if n == 26:
                        attended(0)
                    if n == 27:
                        attended_moments(0)
                    if n == 28:
                        attended_norm(0)
                    if n == 29:
                        routed_moments(0)
                    if n == 30:
                        routed_norm(0)
                    if n == 32:
                        take_shift(0, 3).then_inc(x3_ready.sem, 1)
                    if n < 32:
                        dve.wait_ge(*plan.full(("S", n), r))
                        for i, cols in enumerate((slice(0, P), slice(P, TRI))):
                            ins = dve.tensor_reduce(nmax[:, n % 4, i:i + 1], plan[("S", n)][:, cols], AX.X,
                                                    ALU.max, negate=True)
                        ins.then_inc(nmax_ready.sem, 1)
                    if n >= 1:
                        m = n - 1
                        dve.wait_ge(*plan.drained(("S", m), r))
                        link(dve.reciprocal(esum[:, m % 4, :], esum[:, m % 4, :]))
                        for i, cols in enumerate((slice(0, P), slice(P, TRI))):
                            ins = dve.tensor_scalar(pr[:, m % 6, cols], pr[:, m % 6, cols],
                                                    esum[:, m % 4, i:i + 1], None, ALU.mult)
                        ins.then_inc(probs.sem, 1)
                attended(1)
                attended_moments(1)
                attended_norm(1)
                routed_moments(1)
                routed_norm(1)

                def shared_gate(j, g):
                    dve.wait_ge(*plan.drained(("SG", g, j), r))
                    dve.wait_ge(*plan.full(("SU", g, j), r))
                    key = ("SU", g, j)
                    dve.tensor_tensor(hf[:, 2 * g:2 * g + 2, j * HALF:(j + 1) * HALF],
                                      sg[:, g, :].rearrange("p (f n) -> p f n", f=2),
                                      plan[key][:, :].rearrange("p (f n) -> p f n", f=2),
                                      ALU.mult).then_inc(plan.drains(key), 1)

                shared_gate(0, 0)
                shared_gate(0, 1)
                for j in range(2):
                    dve.wait_ge(*plan.full(("R", j), r))
                    dve.tensor_copy(lgt[:, H[j], :].rearrange("p t e -> p (t e)"),
                                    plan[("R", j)][:, 0:2 * E1]).then_inc(plan.drains(("R", j)), 1)
                for j in range(2):
                    dve.wait_ge(*plan.drained(("R", j), r))
                link(dve.tensor_tensor(biased[:, :, :], lgt[:, :, :],
                                       rt_bias[:, :].unsqueeze(1).broadcast_to([P, TILES, E1]), ALU.add))
                settle(dve)
                for t in range(TILES):
                    ins = dve.max(mx[:, t, :], biased[:, t, :])
                link(ins)
                settle(dve)
                for t in range(TILES):
                    ins = dve.max_index(ix[:, t, :], mx[:, t, :], biased[:, t, :])
                link(ins)
                link(dve.tensor_copy(ixf[:, :, :], ix[:, :, 0:TOPK]))
                link(dve.tensor_tensor(oh, ixf[:, :, :].unsqueeze(3).broadcast_to([P, TILES, TOPK, E1]),
                                       iota[:, :].unsqueeze(1).unsqueeze(1).broadcast_to([P, TILES, TOPK, E1]),
                                       ALU.is_equal))
                with nc.allow_low_precision(reason="sums of zeros and ones up to one are exact"):
                    link(dve.tensor_reduce(chosen[:, :, :], oh.rearrange("p t k e -> p t e k"), AX.X, ALU.add))
                for t in range(TILES):
                    ins = dve.tensor_tensor(before[:, t + 1, :], before[:, t, :], chosen[:, t, :], ALU.add)
                    if t < TILES - 1:
                        link(ins)
                ins.then_inc(chosen_ready.sem, 1)
                link(dve.tensor_tensor(prod, oh, lgt[:, :, :].unsqueeze(2).broadcast_to([P, TILES, TOPK, E1]),
                                       ALU.mult))
                link(dve.tensor_reduce(lk[:, :, :], prod, AX.X, ALU.add))
                shared_gate(1, 0)
                shared_gate(1, 1)
                take_shift(1, 3).then_inc(x3_ready.sem, 1)
                dve.wait_ge(*plan.full("pos", r))
                dve.tensor_tensor(prod, oh, plan["pos"][:, 0:TILES * E1]
                                  .rearrange("p (t e) -> p t e", t=TILES).unsqueeze(2)
                                  .broadcast_to([P, TILES, TOPK, E1]), ALU.mult).then_inc(plan.drains("pos"), 1)
                dve.wait_ge(*plan.drained("pos", r))
                link(dve.tensor_copy(before[:, 0, :], before[:, TILES, :]))
                link(dve.tensor_reduce(slot[:, :, :], prod, AX.X, ALU.add))
                link(dve.tensor_scalar(over[:, :, :], slot[:, :, :], float(CAP), float(4 * SLOTS),
                                       ALU.is_ge, ALU.mult))
                link(dve.scalar_tensor_tensor(slot[:, :, :], ixf[:, :, :], float(CAP), slot[:, :, :],
                                              ALU.mult, ALU.add))
                link(dve.tensor_tensor(slot[:, :, :], slot[:, :, :], over[:, :, :], ALU.add))
                dve.tensor_copy(sidx[:, :].rearrange("p (t k) -> p t k", t=TILES),
                                slot[:, :, :]).then_inc(sidx_ready.sem, 1)
                dve.tensor_scalar(gidx[:, bass.ds(r, 1), :].rearrange("p o (t k) -> p (o t) k", t=TILES),
                                  slot[:, :, :], float(SLOTS), None, ALU.min)
                link(dve.tensor_reduce(wsum[:, :], lk[:, :, :], AX.X, ALU.max))
                dve.tensor_tensor(lk[:, :, :], lk[:, :, :],
                                  wsum[:, :].unsqueeze(2).broadcast_to([P, TILES, TOPK]),
                                  ALU.subtract).then_inc(top_ready.sem, 1)
                dve.wait_ge(top_exp.sem, top_exp.at(r, 1))
                link(dve.tensor_reduce(wsum[:, :], wk[:, :, :], AX.X, ALU.add))
                link(dve.reciprocal(wsum[:, :], wsum[:, :]))
                dve.tensor_tensor(wts[:, bass.ds(r, 1), :].rearrange("p o (t k) -> p (o t) k", t=TILES),
                                  wk[:, :, :], wsum[:, :].unsqueeze(2).broadcast_to([P, TILES, TOPK]), ALU.mult)
            if count[0] != chain.per:
                raise ValueError(f"dve_chain is raised {count[0]} times in a round")
            tail_vector(dve)


_SHAPE = (8, 256, 256)


def _layouts(np, i):
    f = np.float32

    def chunks(w):
        return np.ascontiguousarray(w.reshape(-1, 128, w.shape[1]).transpose(1, 0, 2))

    def channels(*vs):
        out = np.zeros((128, 2, 8), f)
        for n, v in enumerate(vs):
            out[:, :, n] = v.reshape(2, 128).T
        return out

    k, q = np.arange(128)[:, None], np.arange(128)[None, :]
    low = np.where(q >= k, 0.0, -1e30).astype(f)
    att = [i["L1_attn_" + n] for n in ("Wq", "Wk", "Wv", "Wo")]
    heads = [4 * (2 * (p // 4) + e) + p % 4 for p in range(16) for e in range(2)]
    state = (np.array(heads)[:, None] * 64 + np.arange(64)).ravel()
    conv_rows = np.concatenate([np.arange(256), 256 + state, 2304 + state])
    pairs = 512 + state.reshape(16, 1, 128) + 2048 * np.arange(2)[None, :, None]
    proj_rows = np.concatenate([np.arange(512), np.arange(4608, 4640), pairs.ravel()])
    gu = np.concatenate([i["L1_ffn_gate_w"], i["L1_ffn_up_w"]], 1)
    a = {
        "x": np.ascontiguousarray(i["L0_attn_hidden_states"].reshape(-1, 256)),
        "ident": np.eye(128, dtype=f),
        "iota": np.tile(np.arange(64, dtype=f), (128, 1)),
        "parity": np.stack([(np.arange(128) % 32 < 16), (np.arange(128) % 32 >= 16)], 1).astype(f),
        "keyq_mask": np.concatenate([low, low], 1),
        "qkey_mask": np.concatenate([low.T, low.T], 1),
        "earlier": (k < q).astype(f),
        "neg_sel": -np.tile(np.eye(32, dtype=f), (3, 1)),
        "chan": channels(i["L0_attn_z_bias"], np.repeat(i["L0_attn_D"], 8), i["L0_attn_norm1_w"],
                         i["L0_attn_norm2_w"], i["L1_attn_bq"], i["L1_attn_bk"]),
        "conv_w": np.ascontiguousarray(i["L0_attn_conv_w"][conv_rows].reshape(34, 128, 4).transpose(1, 0, 2)),
        "conv_b": np.ascontiguousarray(i["L0_attn_conv_b"][conv_rows].reshape(34, 128).T),
        "w_in": chunks(i["L0_attn_in_proj_w"][proj_rows].T),
        "w_out": chunks(i["L0_attn_out_proj_w"].T),
        "w_gu": chunks(np.concatenate([i["L0_attn_gate_w"], i["L0_attn_up_w"]], 0).T),
        "w_dn": chunks(i["L0_attn_down_w"].T),
        "w_lora": chunks(np.concatenate([i["L0_ffn_W"], i["L0_ffn_gate_w"],
                                         i["L0_ffn_A"].reshape(128, 256)], 0).T),
        "w_lb": np.ascontiguousarray(i["L0_ffn_B"].transpose(0, 2, 1).reshape(128, 256)),
        "w_att": np.ascontiguousarray(np.stack(att, 1).reshape(2, 128, 4, 256).transpose(1, 0, 2, 3)),
        "att_rows": np.stack([i["L1_attn_bv"], i["L1_attn_bo"]])[None],
        "w_rt": chunks(i["L1_ffn_router_w"].T),
        "rt_bias": i["L1_ffn_router_bias"][None, :],
        "w_sgu": chunks(np.concatenate([i["L1_ffn_sh_gate_w"].reshape(512, 256),
                                        i["L1_ffn_sh_up_w"].reshape(512, 256)], 0).T),
        "w_sdn": chunks(i["L1_ffn_sh_down_w"].transpose(0, 2, 1).reshape(512, 256)),
        "w_egu": np.ascontiguousarray(gu.transpose(2, 0, 1).reshape(2, 128, 64, 128).transpose(1, 0, 2, 3)),
        "w_edn": np.ascontiguousarray(i["L1_ffn_down_w"].transpose(2, 0, 1)),
    }
    return {n: np.ascontiguousarray(v) for n, v in a.items()}


def kernel(**inputs):
    import numpy as _np
    import concourse.bacc as _bacc
    from concourse import mybir as _mybir
    from concourse.bass_utils import run_bass_kernel_spmd as _run

    nc = _bacc.Bacc("TRN2", target_bir_lowering=False, num_devices=1)
    arrays = _layouts(_np, {n: _np.asarray(v) for n, v in inputs.items()})
    aps = {n: nc.dram_tensor("in_" + n, v.shape, _mybir.dt.from_np(v.dtype), kind="ExternalInput").ap()
           for n, v in arrays.items()}
    out = nc.dram_tensor("out_dram", (TOKENS, D), F32, kind="ExternalOutput").ap()
    sandwich(nc, aps, out)
    r = _run(nc, [{"in_" + n: v for n, v in arrays.items()}], core_ids=[0])
    return r.results[0]["out_dram"].reshape(_SHAPE)
```
